# Optimizing a Trainium2 kernel written in Bass

```python
import numpy as np
import jax
import jax.numpy as jnp

def _softmax(x, axis=-1):
    return jax.nn.softmax(x, axis=axis)

def _gelu(x):
    return jax.nn.gelu(x, approximate=True)

def _silu(x):
    return jax.nn.silu(x)

def _sigmoid(x):
    return jax.nn.sigmoid(x)

def _layernorm(x, axis=-1, eps=1e-05):
    m = jnp.mean(x, axis=axis, keepdims=True)
    v = jnp.var(x, axis=axis, keepdims=True)
    return (x - m) / jnp.sqrt(v + eps)

def _scatter_add(tgt, idx, src, axis=0):
    return tgt.at[idx].add(src)

def _segment_sum(src, seg, n):
    return jax.ops.segment_sum(src, seg, n)
kernel_name = 'mk_xattn_ffn_d2_seqx_r8_689319'

def setup_inputs(seed: int=0):
    np.random.seed(seed)
    _w = jnp.asarray

    def _rec_inputs():
        import jax
        import jax.numpy as jnp
        _rk = jax.random.key(seed)
        x = -0.000125 + 0.9999 * jax.random.normal(jax.random.fold_in(_rk, 1), (8, 128, 256), jnp.float32)
        _lenS = 128 - jax.random.randint(jax.random.fold_in(_rk, 7), (8,), 0, max(1, 128 // 4) + 1, jnp.int32)
        _lenS2 = 128 - jax.random.randint(jax.random.fold_in(_rk, 8), (8,), 0, max(1, 128 // 4) + 1, jnp.int32)
        _ctx_2048P = jax.random.normal(jax.random.fold_in(_rk, 11), (8, 16, 256), jnp.float32)
        _ctx_2048c = jax.random.dirichlet(jax.random.fold_in(_rk, 511), 0.3 * jnp.ones((16,), jnp.float32), (8, 128))
        _ctx_2048t = jnp.einsum('bsk,bkd->bsd', _ctx_2048c, _ctx_2048P)
        _ctx_2048t = _ctx_2048t * jax.lax.rsqrt(jnp.mean(jnp.square(_ctx_2048t)) + 1e-12) * 0.953939
        ctx_2048 = -1.52775e-05 + 0.999936 * (_ctx_2048t + 0.3 * jax.random.normal(jax.random.fold_in(_rk, 611), (8, 128, 256), jnp.float32))
        return (x, ctx_2048)
    x, ctx_2048 = _rec_inputs()

    def _L0_xattn_setup():
        import jax, jax.numpy as jnp
        import numpy as np
        B, DIM1, DIM2, LATENT, T = (16, 128, 128, 64, 256)
        LN_EPS = 1e-05
        key = jax.random.key(seed)
        ks = jax.random.split(key, 8)

        def xavier(k, shape):
            fan_out, fan_in = shape
            std = float(np.sqrt(2.0 / (fan_in + fan_out)))
            return jax.random.normal(k, shape, dtype=jnp.float32) * std
        return {'input1': jax.random.normal(ks[0], (B, DIM1, T), dtype=jnp.float32), 'input2': jax.random.normal(ks[1], (B, DIM2, T), dtype=jnp.float32), 'theta_w': xavier(ks[2], (LATENT, DIM2)), 'theta_b': jnp.zeros((LATENT,), jnp.float32), 'phi_w': xavier(ks[3], (LATENT, DIM1)), 'phi_b': jnp.zeros((LATENT,), jnp.float32), 'g_w': xavier(ks[4], (LATENT, DIM1)), 'g_b': jnp.zeros((LATENT,), jnp.float32), 'ln_gamma': jnp.ones((LATENT, T), jnp.float32), 'ln_beta': jnp.zeros((LATENT, T), jnp.float32), 'out_w': xavier(ks[5], (DIM2, LATENT)), 'out_b': jnp.zeros((DIM2,), jnp.float32)}
    _L0_xattn_all = _L0_xattn_setup()
    _L0_xattn_in = {k: v for k, v in _L0_xattn_all.items() if k in ('theta_w', 'theta_b', 'phi_w', 'phi_b', 'g_w', 'g_b', 'ln_gamma', 'ln_beta', 'out_w', 'out_b')}
    del _L0_xattn_all

    def _L0_ffn_setup():
        import jax, jax.numpy as jnp
        import numpy as np
        L, B, D = (256, 1, 256)
        H = 16
        DK, DV = (D // 2, D)
        HDK, HDV = (DK // H, DV // H)
        RATIO = 2
        BASE = 10000.0
        EPS = 1e-05

        def _apply_rotary(x, cos, sin):
            d2 = x.shape[-1] // 2
            x1, x2 = (x[..., :d2], x[..., d2:])
            return jnp.concatenate([x1 * cos - x2 * sin, x2 * cos + x1 * sin], axis=-1)
        key = jax.random.key(seed)
        ks = jax.random.split(key, 8)
        s = 0.02
        return {'x': jax.random.normal(ks[0], (L, B, D), jnp.float32), 'conv_w': jax.random.normal(ks[1], (D, 2), jnp.float32) * 0.5, 'Wq': jax.random.normal(ks[2], (D, DK), jnp.float32) * s, 'Wk': jax.random.normal(ks[3], (D, DK), jnp.float32) * s, 'Wv': jax.random.normal(ks[4], (D, DV), jnp.float32) * s, 'Wg': jax.random.normal(ks[5], (D, DV), jnp.float32) * s, 'router_w': jax.random.normal(ks[6], (H, HDV, RATIO), jnp.float32) * s, 'Wout': jax.random.normal(ks[7], (DV, D), jnp.float32) * s}
    _L0_ffn_all = _L0_ffn_setup()
    _L0_ffn_in = {k: v for k, v in _L0_ffn_all.items() if k in ('conv_w', 'Wq', 'Wk', 'Wv', 'Wg', 'router_w', 'Wout')}
    del _L0_ffn_all

    def _L1_xattn_setup():
        import jax, jax.numpy as jnp
        import numpy as np
        N_HEAD = 8
        key = jax.random.key(seed)
        k1, k2, k3 = jax.random.split(key, 3)
        B, D, L = (4, 128, 256)
        q = jax.random.normal(k1, (B, D, L), dtype=jnp.float32)
        k = jax.random.normal(k2, (B, D, L), dtype=jnp.float32)
        v = jax.random.normal(k3, (B, D, L), dtype=jnp.float32)
        gamma = jnp.ones((), dtype=jnp.float32)
        return {'q': q, 'k': k, 'v': v, 'gamma': gamma}
    _L1_xattn_all = _L1_xattn_setup()
    _L1_xattn_in = {k: v for k, v in _L1_xattn_all.items() if k in ('gamma',)}
    del _L1_xattn_all

    def _L1_ffn_setup():
        import jax, jax.numpy as jnp
        import numpy as np
        B, T, D = (2, 128, 256)
        E, F, K = (64, 64, 4)
        S, HS = (2, 64 * 4)
        key = jax.random.key(seed)
        ks = jax.random.split(key, 9)
        s = 0.02
        f32 = jnp.float32
        return {'x': jax.random.normal(ks[0], (B, T, D), f32), 'router_w': jax.random.normal(ks[1], (D, E), f32) * s, 'router_bias': jnp.zeros((E,), f32), 'wg': jax.random.normal(ks[2], (E, D, F), f32) * s, 'wu': jax.random.normal(ks[3], (E, D, F), f32) * s, 'wd': jax.random.normal(ks[4], (E, F, D), f32) * s, 'swg': jax.random.normal(ks[5], (S, D, HS), f32) * s, 'swu': jax.random.normal(ks[6], (S, D, HS), f32) * s, 'swd': jax.random.normal(ks[7], (S, HS, D), f32) * s}
    _L1_ffn_all = _L1_ffn_setup()
    _L1_ffn_in = {k: v for k, v in _L1_ffn_all.items() if k in ('router_w', 'router_bias', 'wg', 'wu', 'wd', 'swg', 'swu', 'swd')}
    del _L1_ffn_all
    return {'x': x, 'ctx_2048': ctx_2048, 'L0_xattn_theta_w': _L0_xattn_in['theta_w'], 'L0_xattn_theta_b': _L0_xattn_in['theta_b'], 'L0_xattn_phi_w': _L0_xattn_in['phi_w'], 'L0_xattn_phi_b': _L0_xattn_in['phi_b'], 'L0_xattn_g_w': _L0_xattn_in['g_w'], 'L0_xattn_g_b': _L0_xattn_in['g_b'], 'L0_xattn_ln_gamma': _L0_xattn_in['ln_gamma'], 'L0_xattn_ln_beta': _L0_xattn_in['ln_beta'], 'L0_xattn_out_w': _L0_xattn_in['out_w'], 'L0_xattn_out_b': _L0_xattn_in['out_b'], 'L0_ffn_conv_w': _L0_ffn_in['conv_w'], 'L0_ffn_Wq': _L0_ffn_in['Wq'], 'L0_ffn_Wk': _L0_ffn_in['Wk'], 'L0_ffn_Wv': _L0_ffn_in['Wv'], 'L0_ffn_Wg': _L0_ffn_in['Wg'], 'L0_ffn_router_w': _L0_ffn_in['router_w'], 'L0_ffn_Wout': _L0_ffn_in['Wout'], 'L1_xattn_gamma': _L1_xattn_in['gamma'], 'L1_ffn_router_w': _L1_ffn_in['router_w'], 'L1_ffn_router_bias': _L1_ffn_in['router_bias'], 'L1_ffn_wg': _L1_ffn_in['wg'], 'L1_ffn_wu': _L1_ffn_in['wu'], 'L1_ffn_wd': _L1_ffn_in['wd'], 'L1_ffn_swg': _L1_ffn_in['swg'], 'L1_ffn_swu': _L1_ffn_in['swu'], 'L1_ffn_swd': _L1_ffn_in['swd']}

def reference(x, ctx_2048, L0_xattn_theta_w, L0_xattn_theta_b, L0_xattn_phi_w, L0_xattn_phi_b, L0_xattn_g_w, L0_xattn_g_b, L0_xattn_ln_gamma, L0_xattn_ln_beta, L0_xattn_out_w, L0_xattn_out_b, L0_ffn_conv_w, L0_ffn_Wq, L0_ffn_Wk, L0_ffn_Wv, L0_ffn_Wg, L0_ffn_router_w, L0_ffn_Wout, L1_xattn_gamma, L1_ffn_router_w, L1_ffn_router_bias, L1_ffn_wg, L1_ffn_wu, L1_ffn_wd, L1_ffn_swg, L1_ffn_swu, L1_ffn_swd):
    import jax
    import jax.numpy as jnp

    def _L0_xattn_ref(input1, input2, theta_w, theta_b, phi_w, phi_b, g_w, g_b, ln_gamma, ln_beta, out_w, out_b):
        import jax, jax.numpy as jnp
        import numpy as np
        B, DIM1, DIM2, LATENT, T = (16, 128, 128, 64, 256)
        LN_EPS = 1e-05
        theta_x = jnp.einsum('ld,bdt->btl', theta_w, input2) + theta_b
        phi_x = jnp.einsum('ld,bdt->blt', phi_w, input1) + phi_b[:, None]
        scores = jnp.einsum('btl,bls->bts', theta_x, phi_x)
        p = jax.nn.softmax(scores, axis=-1)
        g_x = jnp.einsum('ld,bdt->btl', g_w, input1) + g_b
        t_x = jnp.einsum('bts,bsl->blt', p, g_x)
        mu = jnp.mean(t_x, axis=(1, 2), keepdims=True)
        var = jnp.var(t_x, axis=(1, 2), keepdims=True)
        h = (t_x - mu) * jax.lax.rsqrt(var + LN_EPS) * ln_gamma + ln_beta
        h = jax.nn.relu(h)
        w_t = jnp.einsum('ol,blt->bot', out_w, h) + out_b[None, :, None]
        return w_t + input2

    def _L0_ffn_ref(x, conv_w, Wq, Wk, Wv, Wg, router_w, Wout):
        import jax, jax.numpy as jnp
        import numpy as np
        L, B, D = (256, 1, 256)
        H = 16
        DK, DV = (D // 2, D)
        HDK, HDV = (DK // H, DV // H)
        RATIO = 2
        BASE = 10000.0
        EPS = 1e-05

        def _apply_rotary(x, cos, sin):
            d2 = x.shape[-1] // 2
            x1, x2 = (x[..., :d2], x[..., d2:])
            return jnp.concatenate([x1 * cos - x2 * sin, x2 * cos + x1 * sin], axis=-1)
        x = jnp.transpose(x, (1, 0, 2))
        b, l, d = x.shape
        x_prev = jnp.pad(x, ((0, 0), (1, 0), (0, 0)))[:, :l]
        x = jax.nn.silu(x_prev * conv_w[:, 0] + x * conv_w[:, 1])
        q = jax.nn.silu(x @ Wq)
        k = x @ Wk
        v = x @ Wv
        g = x @ Wg
        q = q.reshape(b, l, H, HDK).transpose(0, 2, 1, 3)
        k = k.reshape(b, l, H, HDK).transpose(0, 2, 1, 3)
        v = v.reshape(b, l, H, HDV).transpose(0, 2, 1, 3)
        inv_freq = 1.0 / BASE ** (jnp.arange(0, HDK, 2, dtype=jnp.float32) / HDK)
        freqs = jnp.arange(l, dtype=jnp.float32)[:, None] * inv_freq[None, :]
        cos, sin = (jnp.cos(freqs), jnp.sin(freqs))
        q = _apply_rotary(q, cos, sin)
        k = _apply_rotary(k, cos, sin)
        logits = jnp.einsum('bhld,hdr->bhlr', v, router_w)
        scores = jax.nn.softmax(logits, axis=-1)
        onehot = jax.nn.one_hot(jnp.argmax(scores, axis=-1), RATIO, dtype=scores.dtype)
        masked_scores = scores * onehot
        masked_ind = onehot
        sum_ind = jnp.cumsum(masked_ind, axis=2)
        norm = jnp.where(sum_ind > 0, 1.0 / jnp.maximum(sum_ind, 1.0), 0.0)[..., None]
        q_exp = q[:, :, :, None, :] * masked_scores[..., None] * norm
        k_exp = k[:, :, :, None, :] * masked_ind[..., None]
        q_exp = q_exp.reshape(b, H, l, RATIO * HDK)
        k_exp = k_exp.reshape(b, H, l, RATIO * HDK)
        qk = jnp.einsum('bhld,bhmd->bhlm', q_exp, k_exp) * HDK ** (-0.5)
        mask = jnp.tril(jnp.ones((l, l), dtype=qk.dtype))
        qk = qk * mask
        o = jnp.einsum('bhlm,bhmd->bhld', qk, v)
        o = o.transpose(0, 2, 1, 3)
        mu = jnp.mean(o, axis=-1, keepdims=True)
        var = jnp.var(o, axis=-1, keepdims=True)
        o = (o - mu) / jnp.sqrt(var + EPS)
        out = jax.nn.silu(g) * o.reshape(b, l, d)
        out = out @ Wout
        return jnp.transpose(out, (1, 0, 2))

    def _L1_xattn_ref(q, k, v, gamma):
        import jax, jax.numpy as jnp
        import numpy as np
        N_HEAD = 8
        B, Dq, Lq = q.shape
        Dv, Lk = (v.shape[-2], v.shape[-1])
        h = N_HEAD
        dq = Dq // h
        dv = Dv // h
        qh = q.reshape(B, h, dq, Lq)
        kh = k.reshape(B, h, dq, Lk)
        vh = v.reshape(B, h, dv, Lk)
        scale = 1.0 / jnp.sqrt(jnp.asarray(dq, dtype=q.dtype))
        qk = jnp.einsum('bhdq,bhdl->bhql', qh, kh) * scale
        sm = jax.nn.softmax(qk, axis=-1)
        ret = jnp.einsum('bhql,bhdl->bhdq', sm, vh)
        ret = ret.reshape(B, Dv, Lq)
        return gamma * ret

    def _L1_ffn_ref(x, router_w, router_bias, wg, wu, wd, swg, swu, swd):
        import jax, jax.numpy as jnp
        import numpy as np
        B, T, D = (2, 128, 256)
        E, F, K = (64, 64, 4)
        S, HS = (2, 64 * 4)
        b, t, d = x.shape
        flat = x.reshape(b * t, d)
        n = flat.shape[0]
        logits = flat @ router_w
        scores = jax.nn.softmax(logits, axis=-1)
        _, topk_idx = jax.lax.top_k(logits + router_bias, K)
        topk_scores = jnp.take_along_axis(scores, topk_idx, axis=-1)
        topk_scores = topk_scores / topk_scores.sum(axis=-1, keepdims=True)
        comb = jnp.zeros((n, E), dtype=flat.dtype).at[jnp.arange(n)[:, None], topk_idx].set(topk_scores)
        g = jax.nn.silu(jnp.einsum('nd,edf->nef', flat, wg))
        u = jnp.einsum('nd,edf->nef', flat, wu)
        routed = jnp.einsum('ne,nef,efd->nd', comb, g * u, wd)
        sg = jax.nn.silu(jnp.einsum('nd,sdh->nsh', flat, swg))
        su = jnp.einsum('nd,sdh->nsh', flat, swu)
        shared = jnp.einsum('nsh,shd->nd', sg * su, swd)
        return (routed + shared).reshape(b, t, d)
    x = x + _L0_xattn_ref(_layernorm(x, axis=-1), ctx_2048, L0_xattn_theta_w, L0_xattn_theta_b, L0_xattn_phi_w, L0_xattn_phi_b, L0_xattn_g_w, L0_xattn_g_b, L0_xattn_ln_gamma, L0_xattn_ln_beta, L0_xattn_out_w, L0_xattn_out_b)
    x = x + _L0_ffn_ref(_layernorm(x, axis=-1), L0_ffn_conv_w, L0_ffn_Wq, L0_ffn_Wk, L0_ffn_Wv, L0_ffn_Wg, L0_ffn_router_w, L0_ffn_Wout)
    x = x + _L1_xattn_ref(_layernorm(x, axis=-1), ctx_2048, ctx_2048, L1_xattn_gamma)
    x = x + _L1_ffn_ref(_layernorm(x, axis=-1), L1_ffn_router_w, L1_ffn_router_bias, L1_ffn_wg, L1_ffn_wu, L1_ffn_wd, L1_ffn_swg, L1_ffn_swu, L1_ffn_swd)
    return x

_drawn_inputs = setup_inputs


def setup_inputs(seed=0):
    import zlib

    import numpy as np

    out = dict(_drawn_inputs(seed))
    spreads = {'L0_xattn_theta_b': (0.0, 0.1),
     'L0_xattn_phi_b': (0.0, 2.0),
     'L0_xattn_g_b': (0.0, 0.1),
     'L0_xattn_ln_gamma': (1.0, 0.2),
     'L0_xattn_ln_beta': (0.0, 0.1),
     'L0_xattn_out_b': (0.0, 0.8),
     'L1_ffn_router_bias': (0.0, 0.8)}
    factors = {'L0_ffn_conv_w': 8.0,
     'L0_ffn_Wq': 8.0,
     'L0_ffn_Wk': 8.0,
     'L0_ffn_Wv': 8.0,
     'L0_ffn_Wg': 8.0,
     'L0_ffn_router_w': 8.0,
     'L0_ffn_Wout': 8.0,
     'L1_ffn_router_w': 8.0,
     'L1_ffn_wg': 8.0,
     'L1_ffn_wu': 8.0,
     'L1_ffn_wd': 8.0,
     'L1_ffn_swg': 4.834,
     'L1_ffn_swu': 4.728,
     'L1_ffn_swd': 4.767}
    for name, (base, spread) in spreads.items():
        noise = np.random.default_rng([zlib.crc32(name.encode()), seed]).standard_normal(out[name].shape)
        drawn = base * np.exp(spread * noise) if base else spread * noise
        out[name] = jnp.asarray(drawn.astype(out[name].dtype))
    for name, factor in factors.items():
        out[name] = (out[name] * factor).astype(out[name].dtype)
    return out
```

```python
import numpy as np
import concourse.bass as bass
from concourse import mybir
from contextlib import ExitStack

F32 = mybir.dt.float32
BF16 = mybir.dt.bfloat16
ALU = mybir.AluOpType
ACT = mybir.ActivationFunctionType
X_AXIS = mybir.AxisListType.X

P = 128
NB = 8
T = 256
EPS = 1e-5


class Shared:
    pass


def stage_a(nc, shared, x, ctx_in, theta_wT, phi_wT, g_wT, out_wT2, col_consts, gamma2, beta2):
    stack = ExitStack()
    with stack:
        def sb(name, shape, dt=F32):
            return stack.enter_context(nc.sbuf_tensor(name, shape, dt))

        sem = shared.sem

        NP = NB // 2
        X, C, ident, half = shared.X, shared.C, shared.ident, shared.half
        thw = sb("thw", [P, 64])
        phw = sb("phw", [P, 64])
        gw = sb("gw", [P, 64])
        outw = sb("outw", [P, 2, P])
        cols = sb("cols", [P, 4])
        gamma = sb("gamma", [P, T])
        beta = sb("beta", [P, T])
        blk64 = sb("blk64", [P, P])

        stats = sb("stats", [P, NB, 6])
        mv = sb("mv", [P, NB, 2])
        vare = sb("vare", [P, NB])
        rstd = sb("rstd", [P, NB])
        xn = sb("xn", [P, 2, 2, T])
        thph = sb("thph", [P, 2, 2 * T])
        gx = sb("gx", [P, 2, 2 * 2 * 64])
        nmax = sb("nmax", [P, 2, 4])
        psums = sb("psums", [P, 2, 4])
        prec = sb("prec", [P, 2, 4])
        pr = sb("pr", [P, 2, 4, T])
        pn = sb("pn", [P, 4, T])
        pT = sb("pT", [P, 4, T])
        tx = sb("tx", [P, T])
        tstat = sb("tstat", [P, 6])
        tmv = sb("tmv", [P, 2])
        te = sb("te", [P, 2])
        tm = sb("tm", [P, 4])
        trs = sb("trs", [P, 1])
        h1 = sb("h1", [P, T])
        h2 = sb("h2", [P, T])
        h3 = sb("h3", [P, T])
        hr = sb("hr", [P, T])
        xa = sb("xa", [P, 2, T])

        PS = [stack.enter_context(nc.psum_tensor(f"ps{i}", [P, 512], F32)) for i in range(8)]

        sx, sc_, sw = sem("x_in"), sem("ctx_in"), sem("w_in")
        s_id = sem("ident_ready")
        s_mv = sem("mv_ready")
        s_rstd = sem("rstd_ready")
        s_xn = sem("xn_ready")
        s_tp = sem("thetaphi_done")
        s_g = sem("g_done")
        s_tps = sem("thetaphi_sb")
        s_gs = sem("g_sb")
        s_sc = sem("scores_done")
        s_nm = sem("nmax_ready")
        s_ex = sem("exp_done")
        s_pn = sem("pn_ready")
        s_pt = sem("pT_done")
        s_pta = sem("pT_sb_act")
        s_ptd = sem("pT_sb_dve")
        s_tx = sem("tx_done")
        s_txs = sem("tx_sb")
        s_te = sem("te_ready")
        s_st = sem("stat_done")
        s_tv = sem("tvar_ready")
        s_tr = sem("trstd_ready")
        s_h1 = sem("h1_ready")
        s_h2 = sem("h2_ready")
        s_h3 = sem("h3_ready")
        s_h = sem("h_ready")
        s_o = sem("o_done")
        s_xa = sem("xa_ready")
        s_x1 = sem("x1_ready")
        s_dv = sem("dve_chain")

        thb, phb, gb, outb = (cols[:, j:j + 1] for j in range(4))

        block = stack.enter_context(nc.Block())

        @block.sync
        def _(sp):
            sp.dma_start(X[:, 0:2, :], x[0:2].rearrange("b p t -> p b t")).then_inc(sx, 16)
            sp.dma_start(X[:, 2:NB, :], x[2:NB].rearrange("b p t -> p b t")).then_inc(sx, 16)

        @block.gpsimd
        def _(pool):
            pool.memset(ident[:, :], 0.0).then_inc(s_id, 1)
            pool.memset(blk64[:, :], 0.0).then_inc(s_id, 1)
            pool.memset(half[:, :], -0.5).then_inc(s_id, 1)
            pool.wait_ge(s_id, 3)
            pool.affine_select(out=ident[:, :], in_=ident[:, :], compare_op=ALU.not_equal, fill=1.0, base=0,
                               pattern=[[-1, P]], channel_multiplier=1).then_inc(s_id, 1)
            pool.wait_ge(s_id, 4)
            pool.memset(blk64[0:64, 0:64], 1.0 / 64).then_inc(s_id, 1)
            pool.wait_ge(s_id, 5)
            pool.memset(blk64[64:128, 64:128], 1.0 / 64).then_inc(s_id, 1)
            pool.wait_ge(s_id, 6)
            pool.wait_ge(s_mv, 1)
            pool.tensor_tensor(rstd[:, :], vare[:, :], half[:, 0:NB], ALU.pow).then_inc(s_rstd, 1)
            for i in range(NP):
                pool.wait_ge(s_tv, i + 1)
                pool.tensor_tensor(trs[:, :], tm[:, 3:4], half[:, 0:1], ALU.pow).then_inc(s_tr, 1)
                pool.wait_ge(s_h1, i + 1)
                pool.tensor_tensor(h2[:, :], h1[:, :], gamma[:, :], ALU.mult).then_inc(s_h2, 1)
                pool.wait_ge(s_h2, i + 1)
                pool.tensor_tensor(h3[:, :], h2[:, :], beta[:, :], ALU.add).then_inc(s_h3, 1)
                pool.wait_ge(s_xa, i + 1)
                pool.wait_ge(sc_, 16)
                pool.tensor_tensor(X[:, 2 * i:2 * i + 2, :], xa[:, :, :], C[:, 2 * i:2 * i + 2, :], ALU.add).then_inc(s_x1, 1)

        @block.scalar
        def _(act):
            act.dma_start(cols[:, :], col_consts).then_inc(sw, 16)
            act.dma_start(thw[:, :], theta_wT).then_inc(sw, 16)
            act.dma_start(phw[:, :], phi_wT).then_inc(sw, 16)
            act.dma_start(gw[:, :], g_wT).then_inc(sw, 16)
            act.dma_start(C[:, :, :], ctx_in.rearrange("b p t -> p b t")).then_inc(sc_, 16)
            act.dma_start(outw[:, :, :], out_wT2).then_inc(sw, 16)
            act.dma_start(gamma[:, :], gamma2).then_inc(sw, 16)
            act.dma_start(beta[:, :], beta2).then_inc(sw, 16)
            act.wait_ge(sw, 7 * 16)

            def front(i):
                s = i % 2
                act.wait_ge(s_tp, i + 1)
                nc.scalar.activation(thph[:, s, 0:T], PS[0][:, 0:T], ACT.Identity, bias=thb)
                nc.scalar.activation(thph[:, s, T:2 * T], PS[0][:, T:2 * T], ACT.Identity, bias=phb).then_inc(s_tps, 1)
                act.wait_ge(s_nm, i + 1)
                for k in range(4):
                    last = nc.scalar.activation(pr[:, s, k, :], PS[2 + k // 2][:, (k % 2) * T:(k % 2 + 1) * T], ACT.Exp,
                                                bias=nmax[:, s, k:k + 1], accum_out=psums[:, s, k:k + 1])
                last.then_inc(s_ex, 1)

            def back(i):
                act.wait_ge(s_pt, i + 1)
                nc.scalar.copy(pT[:, 0:2, :], PS[4][:, :]).then_inc(s_pta, 1)
                act.wait_ge(s_tx, i + 1)
                if i:
                    act.wait_ge(s_h1, i)
                nc.scalar.activation(tx[:, :], PS[6][:, 0:T], ACT.Identity, bias=gb).then_inc(s_txs, 1)
                act.wait_ge(s_h3, i + 1)
                nc.scalar.activation(hr[:, :], h3[:, :], ACT.Relu).then_inc(s_h, 1)

            for i in range(NP + 1):
                if i < NP:
                    front(i)
                if i > 0:
                    back(i - 1)

        @block.vector
        def _(dve):
            n = [0]

            def link(ins):
                n[0] += 1
                ins.then_inc(s_dv, 1)
                dve.wait_ge(s_dv, n[0])

            dve.wait_ge(sx, 32)
            for b in range(NB):
                last = nc.vector.bn_stats(stats[:, b, :], X[:, b, :])
            link(last)
            for b in range(NB):
                last = nc.vector.bn_aggr(mv[:, b, :], stats[:, b, :])
            link(last)
            nc.vector.tensor_scalar(vare[:, :], mv[:, :, 1], EPS, None, ALU.add).then_inc(s_mv, 1)
            dve.wait_ge(s_rstd, 1)

            def xnorm(i):
                s = i % 2
                if i >= 2:
                    dve.wait_ge(s_g, i - 1)
                for j in range(2):
                    b = 2 * i + j
                    last = nc.vector.tensor_scalar(xn[:, s, j, :], X[:, b, :], mv[:, b, 0:1], rstd[:, b:b + 1], ALU.subtract, ALU.mult)
                last.then_inc(s_xn, 1)

            def front(i):
                s = i % 2
                if i + 1 < NP:
                    xnorm(i + 1)
                dve.wait_ge(s_g, i + 1)
                nc.vector.tensor_copy(gx[:, s, :], PS[1][:, 0:256]).then_inc(s_gs, 1)
                dve.wait_ge(s_sc, i + 1)
                for k in range(2):
                    last = nc.vector.tensor_reduce(nmax[:, s, 2 * k:2 * k + 2], PS[2 + k][:, :].rearrange("p (c s) -> p c s", c=2),
                                                   X_AXIS, ALU.max, negate=True)
                last.then_inc(s_nm, 1)

            def norm(i):
                s = i % 2
                dve.wait_ge(s_ex, i + 1)
                link(nc.vector.reciprocal(prec[:, s, :], psums[:, s, :]))
                if i:
                    dve.wait_ge(s_pt, i)
                for k in range(4):
                    last = nc.vector.tensor_scalar(pn[:, k, :], pr[:, s, k, :], prec[:, s, k:k + 1], None, ALU.mult)
                last.then_inc(s_pn, 1)

            def back(i):
                dve.wait_ge(s_pt, i + 1)
                nc.vector.tensor_copy(pT[:, 2:4, :], PS[5][:, :].rearrange("p (c s) -> p c s", c=2)).then_inc(s_ptd, 1)
                dve.wait_ge(s_txs, i + 1)
                link(nc.vector.bn_stats(tstat[:, :], tx[:, :]))
                link(nc.vector.bn_aggr(tmv[:, :], tstat[:, :]))
                nc.vector.tensor_copy(te[:, 0:1], tmv[:, 0:1])
                link(nc.vector.tensor_tensor(tm[:, 0:1], tmv[:, 0:1], tmv[:, 0:1], ALU.mult))
                nc.vector.tensor_tensor(te[:, 1:2], tm[:, 0:1], tmv[:, 1:2], ALU.add).then_inc(s_te, 1)
                dve.wait_ge(s_st, i + 1)
                link(nc.vector.tensor_copy(tm[:, 1:3], PS[6][:, T:T + 2]))
                link(nc.vector.tensor_tensor(tm[:, 0:1], tm[:, 1:2], tm[:, 1:2], ALU.mult))
                link(nc.vector.tensor_tensor(tm[:, 0:1], tm[:, 2:3], tm[:, 0:1], ALU.subtract))
                nc.vector.tensor_scalar(tm[:, 3:4], tm[:, 0:1], EPS, None, ALU.add).then_inc(s_tv, 1)
                dve.wait_ge(s_tr, i + 1)
                if i:
                    dve.wait_ge(s_h2, i)
                nc.vector.tensor_scalar(h1[:, :], tx[:, :], tm[:, 1:2], trs[:, :], ALU.subtract, ALU.mult).then_inc(s_h1, 1)
                dve.wait_ge(s_o, i + 1)
                if i:
                    dve.wait_ge(s_x1, i)
                nc.vector.scalar_tensor_tensor(xa[:, :, :], PS[7][:, :].rearrange("p (b t) -> p b t", b=2), outb,
                                               X[:, 2 * i:2 * i + 2, :], ALU.add, ALU.add).then_inc(s_xa, 1)

            xnorm(0)
            for i in range(NP + 1):
                if i < NP:
                    front(i)
                if i > 0:
                    back(i - 1)
                if i < NP:
                    norm(i)

        @block.tensor
        def _(pe):
            pe.wait_ge(sw, 7 * 16)
            pe.wait_ge(sc_, 16)
            pe.wait_ge(s_id, 6)

            def front(i):
                s = i % 2
                if i:
                    pe.wait_ge(s_tps, i)
                for j in range(2):
                    nc.tensor.matmul(PS[0][64 * j:64 * j + 64, 0:T], thw[:, :], C[:, 2 * i + j, :], start=True, stop=True)
                pe.wait_ge(s_xn, i + 1)
                for j in range(2):
                    last = nc.tensor.matmul(PS[0][64 * j:64 * j + 64, T:2 * T], phw[:, :], xn[:, s, j, :], start=True, stop=True)
                last.then_inc(s_tp, 1)
                if i:
                    pe.wait_ge(s_gs, i)
                for j in range(2):
                    for c in range(2):
                        k = 2 * j + c
                        last = nc.tensor.matmul(PS[1][:, 64 * k:64 * k + 64], xn[:, s, j, c * P:(c + 1) * P], gw[:, :], start=True, stop=True)
                last.then_inc(s_g, 1)
                pe.wait_ge(s_tps, i + 1)
                if i:
                    pe.wait_ge(s_ex, i)
                for j in range(2):
                    for c in range(2):
                        last = nc.tensor.matmul(PS[2 + j][:, c * T:(c + 1) * T], thph[64 * j:64 * j + 64, s, c * P:(c + 1) * P],
                                                thph[64 * j:64 * j + 64, s, T:2 * T], start=True, stop=True)
                last.then_inc(s_sc, 1)

            def back(i):
                s = i % 2
                pe.wait_ge(s_pn, i + 1)
                if i:
                    pe.wait_ge(s_pta, i)
                    pe.wait_ge(s_ptd, i)
                for j in range(2):
                    for c in range(2):
                        for ct in range(2):
                            last = nc.tensor.transpose(PS[4 + j][:, c * T + ct * P:c * T + (ct + 1) * P], pn[:, 2 * j + ct, c * P:(c + 1) * P], ident[:, :])
                last.then_inc(s_pt, 1)
                pe.wait_ge(s_gs, i + 1)
                pe.wait_ge(s_pta, i + 1)
                pe.wait_ge(s_ptd, i + 1)
                if i:
                    pe.wait_ge(s_tv, i)
                for c in range(2):
                    for j in range(2):
                        last = nc.tensor.matmul(PS[6][64 * j:64 * j + 64, 0:T], gx[:, s, 64 * (2 * j + c):64 * (2 * j + c) + 64],
                                                pT[:, 2 * j + c, :], start=(c == 0), stop=(c == 1))
                last.then_inc(s_tx, 1)
                pe.wait_ge(s_te, i + 1)
                nc.tensor.matmul(PS[6][:, T:T + 2], blk64[:, :], te[:, :], start=True, stop=True).then_inc(s_st, 1)
                pe.wait_ge(s_h, i + 1)
                if i:
                    pe.wait_ge(s_xa, i)
                for j in range(2):
                    last = nc.tensor.matmul(PS[7][:, j * T:(j + 1) * T], outw[:, j, :], hr[:, :], start=True, stop=True)
                last.then_inc(s_o, 1)

            for i in range(NP + 1):
                if i < NP:
                    front(i)
                if i > 0:
                    back(i - 1)



def stage_b(nc, shared, conv_cols, w_qg, w_kv, rw, rot, w_out):
    stack = ExitStack()
    with stack:
        def sb(name, shape, dt=F32):
            return stack.enter_context(nc.sbuf_tensor(name, shape, dt))

        sem = shared.sem
        X, ident, half = shared.X, shared.ident, shared.half
        L, H, DK, DV = NB, 16, 8, 16
        NG = L // 2

        cw = sb("b_cw", [P, 2, 2])
        wa = sb("b_wa", [P, 2, 400])
        wb = sb("b_wb", [P, 2, 384])
        wo = sb("b_wo", [P, 2, T])
        rws = sb("b_rw", [P, H, DV, 2])
        rwd = sb("b_rwd", [P, H, DV])
        wtmp = sb("b_wtmp", [P, 2, T])
        wmean = sb("b_wmean", [P, 2, H])
        trig = sb("b_trig", [P, 3, L, 4])
        lp1 = sb("b_lp1", [P, L, H])

        stats = sb("b_stats", [P, L, 6])
        mv = sb("b_mv", [P, L, 2])
        vare = sb("b_vare", [P, L])
        rstd = sb("b_rstd", [P, L])
        xn = sb("b_xn", [P, 2, 2, T])
        XT = sb("b_XT", [P, 2, L + 1, P])
        tmp = sb("b_tmp", [P, 2, 2, P])
        y = sb("b_y", [P, 2, 2, P])
        xc = sb("b_xc", [P, 2, 2, 2, P])
        Q = sb("b_Q", [P, L, P])
        G = sb("b_G", [P, L, T])
        D = sb("b_D", [P, L, H])
        KV = sb("b_KV", [P, L, 384])
        r1 = sb("b_r1", [P, 4, P])
        r2 = sb("b_r2", [P, 4, P])
        r1k = sb("b_r1k", [P, 4, P])
        r2k = sb("b_r2k", [P, 4, P])
        QR = sb("b_QR", [P, L, P])
        KR = sb("b_KR", [P, L, P])
        ind = sb("b_ind", [P, L, H])
        cum = sb("b_cum", [P, L, H])
        ca = sb("b_ca", [P, L, H])
        cb = sb("b_cb", [P, L, H])
        cc = sb("b_cc", [P, L, H])
        cd = sb("b_cd", [P, L, H])
        absd = sb("b_absd", [P, L, H])
        sg = sb("b_sg", [P, L, H])
        cf = sb("b_cf", [P, L, H])
        same = sb("b_same", [P, L, L, H])
        AC = sb("b_AC", [P, L, L, H])
        prod = sb("b_prod", [P, 2, L * P])
        S = sb("b_S", [P, 2, L * H])
        S2 = sb("b_S2", [P, 2, L * H])
        W = sb("b_W", [P, 2, L * T])
        O = sb("b_O", [P, L, T])
        sq = sb("b_sq", [P, 4, T])
        vs = sb("b_vs", [P, 4 * H])
        ve = sb("b_ve", [P, 4 * H])
        vr = sb("b_vr", [P, 4 * H])
        og = sb("b_og", [P, 4, T])
        on = sb("b_on", [P, 2, 4, T])
        oT = sb("b_oT", [P, 2, 2 * T])

        PS = [stack.enter_context(nc.psum_tensor(f"b_ps{i}", [P, 512], F32)) for i in range(8)]
        s_w, s_cw, s_rw, s_wo, s_tg = sem("b_w_in"), sem("b_cw_in"), sem("b_rw_in"), sem("b_wo_in"), sem("b_trig_in")
        s_lp = sem("b_consts")
        s_wd = sem("b_weights_ready")
        s_mv, s_rstd = sem("b_mv"), sem("b_rstd")
        s_xn, s_t, s_xt, s_y, s_xc, s_p = sem("b_xn"), sem("b_transposed"), sem("b_xT_sb"), sem("b_conv"), sem("b_xc"), sem("b_proj")
        s_qgd, s_kv = sem("b_qgd_sb"), sem("b_kv_sb")
        s_qr, s_kr = sem("b_q_rot"), sem("b_k_rot")
        s_abs, s_sg = sem("b_abs"), sem("b_sig")
        s_pr, s_s2, s_W, s_O = sem("b_prod"), sem("b_scores"), sem("b_W"), sem("b_O")
        s_red = sem("b_prod_used")
        s_sq, s_ve, s_vr, s_og, s_on, s_ot, s_ots, s_y2, s_x2 = (sem("b_" + n) for n in
            ("sq", "ve", "vr", "og", "on", "oT", "oT_sb", "wout", "x2"))
        s_dv, s_pl = sem("b_dve_chain"), sem("b_pool_chain")

        block = stack.enter_context(nc.Block())

        @block.sync
        def _(sp):
            sp.dma_start(cw[:, :, :], conv_cols).then_inc(s_cw, 16)
            sp.dma_start(wa[:, :, 0:384], w_qg.rearrange("(c p) n -> p c n", p=P)).then_inc(s_w, 16)
            sp.dma_start(wb[:, :, :], w_kv.rearrange("(c p) n -> p c n", p=P)).then_inc(s_w, 16)
            sp.dma_start(rws[:, :, :, :], rw.partition_broadcast(P)).then_inc(s_rw, 16)
            sp.dma_start(trig[:, :, :, :], rot.partition_broadcast(P)).then_inc(s_tg, 16)
            sp.dma_start(wo[:, :, :], w_out.rearrange("(c p) n -> p c n", p=P)).then_inc(s_wo, 16)

        @block.gpsimd
        def _(pool):
            n = [0]

            def link(ins):
                n[0] += 1
                ins.then_inc(s_pl, 1)
                pool.wait_ge(s_pl, n[0])

            for l in range(L):
                link(pool.memset(lp1[:, l, :], float(l + 1)))
            link(pool.memset(XT[:, :, 0, :], 0.0))
            pool.memset(half[:, :], -0.5).then_inc(s_lp, 1)
            pool.wait_ge(s_lp, 1)
            pool.wait_ge(s_mv, 1)
            pool.tensor_tensor(rstd[:, :], vare[:, :], half[:, 0:L], ALU.pow).then_inc(s_rstd, 1)

            pool.wait_ge(s_tg, 16)

            def rot_k(g):
                pool.wait_ge(s_kv, 4 * (g + 1))
                ls = slice(4 * g, 4 * g + 4)
                k = KV[:, ls, 0:P]
                cos = trig[:, 0, ls, :].unsqueeze(2).broadcast_to([P, 4, 2 * H, 4])
                sin = trig[:, 1, ls, :].unsqueeze(2).broadcast_to([P, 4, H, 4])
                nsin = trig[:, 2, ls, :].unsqueeze(2).broadcast_to([P, 4, H, 4])
                k5 = k.rearrange("p l (h e f) -> p l h e f", e=2, f=4)
                t5 = r2k[:, :, :].rearrange("p l (h e f) -> p l h e f", e=2, f=4)
                pool.tensor_tensor(r1k[:, :, :].rearrange("p l (h f) -> p l h f", f=4), k.rearrange("p l (h f) -> p l h f", f=4), cos, ALU.mult)
                pool.tensor_tensor(t5[:, :, :, 0, :], k5[:, :, :, 1, :], nsin, ALU.mult)
                link(pool.tensor_tensor(t5[:, :, :, 1, :], k5[:, :, :, 0, :], sin, ALU.mult))
                pool.tensor_tensor(KR[:, ls, :], r1k[:, :, :], r2k[:, :, :], ALU.add).then_inc(s_kr, 1)
                pool.wait_ge(s_kr, g + 1)

            def prod_qk(l):
                pool.wait_ge(s_qr, l // 4 + 1)
                if l >= 2:
                    pool.wait_ge(s_red, l - 1)
                pool.tensor_tensor(prod[:, l % 2, 0:(l + 1) * P].rearrange("p (m x) -> p m x", m=l + 1),
                                   QR[:, l, :].unsqueeze(1).broadcast_to([P, l + 1, P]), KR[:, 0:l + 1, :], ALU.mult).then_inc(s_pr, 1)

            def gate(g):
                pool.wait_ge(s_ve, g + 1)
                pool.tensor_tensor(vr[:, :], ve[:, :], half[:, 0:4 * H], ALU.pow).then_inc(s_vr, 1)
                if g:
                    pool.wait_ge(s_on, g)
                pool.tensor_tensor(og[:, :, :], O[:, 4 * g:4 * g + 4, :], G[:, 4 * g:4 * g + 4, :], ALU.mult).then_inc(s_og, 1)

            rot_k(0)
            for l in range(4):
                prod_qk(l)
            rot_k(1)
            for l in range(4, 8):
                prod_qk(l)
                if l == 6:
                    gate(0)
            gate(1)

        @block.scalar
        def _(act):
            for g in range(NG + 1):
                if g < NG:
                    act.wait_ge(s_t, g + 1)
                    for c in range(2):
                        last = nc.scalar.copy(XT[:, c, 1 + 2 * g:3 + 2 * g, :], PS[c][:, 0:256].rearrange("p (l b) -> p l b", l=2))
                    last.then_inc(s_xt, 1)
                    act.wait_ge(s_y, g + 1)
                    if g >= 2:
                        act.wait_ge(s_p, 2 * (g - 1))
                    nc.scalar.activation(xc[:, g % 2, :, :, :], y[:, :, :, :], ACT.Silu).then_inc(s_xc, 1)
                if g > 0:
                    for l in (2 * g - 2, 2 * g - 1):
                        act.wait_ge(s_p, l + 1)
                        bank = PS[2 + 2 * (l % 2)]
                        nc.scalar.activation(Q[:, l, :], bank[:, 0:P], ACT.Silu)
                        nc.scalar.activation(G[:, l, :], bank[:, P:P + T], ACT.Silu)
                        nc.scalar.copy(D[:, l, :], bank[:, 384:400]).then_inc(s_qgd, 1)
            act.wait_ge(s_abs, 1)
            nc.scalar.activation(sg[:, :, :], absd[:, :, :], ACT.Sigmoid).then_inc(s_sg, 1)
            for g in range(2):
                act.wait_ge(s_O, 4 * (g + 1))
                if g:
                    act.wait_ge(s_ve, g)
                nc.scalar.activation(sq[:, :, :], O[:, 4 * g:4 * g + 4, :], ACT.Square).then_inc(s_sq, 1)
                for j in range(4):
                    l = 4 * g + j
                    act.wait_ge(s_ot, l + 1)
                    if l >= 2:
                        act.wait_ge(s_y2, l - 1)
                    nc.scalar.copy(oT[:, l % 2, 0:T], PS[l % 2][:, 0:T]).then_inc(s_ots, 1)

        @block.vector
        def _(dve):
            n = [0]

            def link(ins):
                n[0] += 1
                ins.then_inc(s_dv, 1)
                dve.wait_ge(s_dv, n[0])

            for b in range(L):
                last = nc.vector.bn_stats(stats[:, b, :], X[:, b, :])
            link(last)
            for b in range(L):
                last = nc.vector.bn_aggr(mv[:, b, :], stats[:, b, :])
            link(last)
            nc.vector.tensor_scalar(vare[:, :], mv[:, :, 1], EPS, None, ALU.add).then_inc(s_mv, 1)
            dve.wait_ge(s_rw, 16)
            link(nc.vector.tensor_tensor(rwd[:, :, :], rws[:, :, :, 1], rws[:, :, :, 0], ALU.subtract))
            dve.wait_ge(s_w, 32)
            wv = wb[:, :, P:384]
            link(nc.vector.tensor_tensor(wtmp[:, :, :], wv, rwd[:, :, :].rearrange("p h d -> p (h d)").unsqueeze(1).broadcast_to([P, 2, T]), ALU.mult))
            for c in range(2):
                nc.vector.reduce_sum(wa[:, c, 384:400], wtmp[:, c, :].rearrange("p (h d) -> p h d", h=H), X_AXIS)
                last = nc.vector.reduce_sum(wmean[:, c, :], wb[:, c, P:384].rearrange("p (h d) -> p h d", h=H), X_AXIS)
            link(last)
            for c in range(2):
                v = wb[:, c, P:384].rearrange("p (h d) -> p h d", h=H)
                last = nc.vector.scalar_tensor_tensor(v, wmean[:, c, :].unsqueeze(2).broadcast_to([P, H, DV]), -1.0 / DV, v, ALU.mult, ALU.add)
            last.then_inc(s_wd, 1)
            dve.wait_ge(s_rstd, 1)
            dve.wait_ge(s_cw, 16)

            def norm(g):
                if g >= 2:
                    dve.wait_ge(s_t, g - 1)
                for j in range(2):
                    l = 2 * g + j
                    last = nc.vector.tensor_scalar(xn[:, g % 2, j, :], X[:, l, :], mv[:, l, 0:1], rstd[:, l:l + 1], ALU.subtract, ALU.mult)
                last.then_inc(s_xn, 1)

            def conv(g):
                dve.wait_ge(s_xt, g + 1)
                if g:
                    dve.wait_ge(s_xc, g)
                for c in range(2):
                    last = nc.vector.tensor_scalar(tmp[:, c, :, :], XT[:, c, 1 + 2 * g:3 + 2 * g, :], cw[:, c, 1:2], None, ALU.mult)
                link(last)
                for c in range(2):
                    last = nc.vector.scalar_tensor_tensor(y[:, c, :, :], XT[:, c, 2 * g:2 * g + 2, :], cw[:, c, 0:1], tmp[:, c, :, :], ALU.mult, ALU.add)
                last.then_inc(s_y, 1)

            def take_kv(l):
                dve.wait_ge(s_p, l + 1)
                nc.vector.tensor_copy(KV[:, l, :], PS[3 + 2 * (l % 2)][:, 0:384]).then_inc(s_kv, 1)

            norm(0)
            norm(1)
            for g in range(NG + 1):
                if g < NG:
                    conv(g)
                    if g + 2 < NG:
                        norm(g + 2)
                if g > 0:
                    take_kv(2 * g - 2)
                    take_kv(2 * g - 1)

            dve.wait_ge(s_tg, 16)
            for g in range(2):
                ls = slice(4 * g, 4 * g + 4)
                dve.wait_ge(s_qgd, 4 * (g + 1))
                q = Q[:, ls, :]
                cos = trig[:, 0, ls, :].unsqueeze(2).broadcast_to([P, 4, 2 * H, 4])
                sin = trig[:, 1, ls, :].unsqueeze(2).broadcast_to([P, 4, H, 4])
                nsin = trig[:, 2, ls, :].unsqueeze(2).broadcast_to([P, 4, H, 4])
                q5 = q.rearrange("p l (h e f) -> p l h e f", e=2, f=4)
                t5 = r2[:, :, :].rearrange("p l (h e f) -> p l h e f", e=2, f=4)
                nc.vector.tensor_tensor(r1[:, :, :].rearrange("p l (h f) -> p l h f", f=4), q.rearrange("p l (h f) -> p l h f", f=4), cos, ALU.mult)
                nc.vector.tensor_tensor(t5[:, :, :, 0, :], q5[:, :, :, 1, :], nsin, ALU.mult)
                link(nc.vector.tensor_tensor(t5[:, :, :, 1, :], q5[:, :, :, 0, :], sin, ALU.mult))
                nc.vector.tensor_tensor(QR[:, ls, :], r1[:, :, :], r2[:, :, :], ALU.add).then_inc(s_qr, 1)
                dve.wait_ge(s_qr, g + 1)

            nc.vector.scalar_tensor_tensor(absd[:, :, :], D[:, :, :], -1.0, D[:, :, :], ALU.mult, ALU.max).then_inc(s_abs, 1)
            link(nc.vector.tensor_scalar(ind[:, :, :], D[:, :, :], 0.0, None, ALU.is_gt))
            link(nc.vector.tensor_copy(cum[:, 0, :], ind[:, 0, :]))
            for l in range(1, L):
                link(nc.vector.tensor_tensor(cum[:, l, :], cum[:, l - 1, :], ind[:, l, :], ALU.add))
            dve.wait_ge(s_lp, 1)
            link(nc.vector.tensor_tensor(ca[:, :, :], lp1[:, :, :], cum[:, :, :], ALU.subtract))
            link(nc.vector.tensor_tensor(cb[:, :, :], cum[:, :, :], ca[:, :, :], ALU.subtract))
            link(nc.vector.tensor_tensor(cc[:, :, :], cb[:, :, :], ind[:, :, :], ALU.mult))
            link(nc.vector.tensor_tensor(cd[:, :, :], cc[:, :, :], ca[:, :, :], ALU.add))
            link(nc.vector.reciprocal(cb[:, :, :], cd[:, :, :]))
            dve.wait_ge(s_sg, 1)
            nc.vector.scalar_tensor_tensor(cf[:, :, :], sg[:, :, :], float(DK) ** -0.5, cb[:, :, :], ALU.mult, ALU.mult)
            link(nc.vector.tensor_tensor(same[:, :, :, :], ind[:, :, :].unsqueeze(2).broadcast_to([P, L, L, H]),
                                         ind[:, :, :].unsqueeze(1).broadcast_to([P, L, L, H]), ALU.is_equal))
            link(nc.vector.tensor_tensor(AC[:, :, :, :], same[:, :, :, :], cf[:, :, :].unsqueeze(2).broadcast_to([P, L, L, H]), ALU.mult))

            def attend(l):
                s = l % 2
                m = l + 1
                dve.wait_ge(s_pr, l + 1)
                nc.vector.reduce_sum(S[:, s, 0:m * H], prod[:, s, 0:m * P].rearrange("p (x d) -> p x d", d=DK), X_AXIS).then_inc(s_red, 1)
                dve.wait_ge(s_red, l + 1)
                link(nc.vector.tensor_tensor(S2[:, s, 0:m * H], S[:, s, 0:m * H], AC[:, l, 0:m, :].rearrange("p m h -> p (m h)"), ALU.mult))
                link(nc.vector.tensor_tensor(W[:, s, 0:m * T].rearrange("p (m h d) -> p m h d", m=m, h=H),
                                             S2[:, s, 0:m * H].rearrange("p (m h) -> p m h", m=m).unsqueeze(3).broadcast_to([P, m, H, DV]),
                                             KV[:, 0:m, P:384].rearrange("p m (h d) -> p m h d", h=H), ALU.mult))
                nc.vector.reduce_sum(O[:, l, :], W[:, s, 0:m * T].rearrange("p (m x) -> p x m", m=m), X_AXIS).then_inc(s_O, 1)

            def head_norm(g):
                dve.wait_ge(s_sq, g + 1)
                if g:
                    dve.wait_ge(s_vr, g)
                link(nc.vector.reduce_sum(vs[:, :], sq[:, :, :].rearrange("p l (h d) -> p (l h) d", h=H), X_AXIS))
                nc.vector.tensor_scalar(ve[:, :], vs[:, :], 1.0 / DV, EPS, ALU.mult, ALU.add).then_inc(s_ve, 1)

            def scale(g):
                dve.wait_ge(s_vr, g + 1)
                dve.wait_ge(s_og, g + 1)
                nc.vector.tensor_tensor(on[:, g, :, :].rearrange("p l (h d) -> p (l h) d", h=H), og[:, :, :].rearrange("p l (h d) -> p (l h) d", h=H),
                                        vr[:, :].unsqueeze(2).broadcast_to([P, 4 * H, DV]), ALU.mult).then_inc(s_on, 1)

            def residual(l):
                dve.wait_ge(s_y2, l + 1)
                nc.vector.tensor_tensor(X[:, l, :], PS[2 + l % 2][:, 0:T], X[:, l, :], ALU.add).then_inc(s_x2, 1)

            for l in range(4):
                attend(l)
            attend(4)
            head_norm(0)
            attend(5)
            attend(6)
            scale(0)
            attend(7)
            for l in range(4):
                residual(l)
            head_norm(1)
            scale(1)
            for l in range(4, 8):
                residual(l)

        @block.tensor
        def _(pe):
            def transposes(g):
                pe.wait_ge(s_xn, g + 1)
                if g:
                    pe.wait_ge(s_xt, g)
                for c in range(2):
                    for j in range(2):
                        last = nc.tensor.transpose(PS[c][:, j * P:(j + 1) * P], xn[:, g % 2, j, c * P:(c + 1) * P], ident[:, :])
                last.then_inc(s_t, 1)

            transposes(0)
            for g in range(NG):
                if g + 1 < NG:
                    transposes(g + 1)
                pe.wait_ge(s_xc, g + 1)
                if g == 0:
                    pe.wait_ge(s_wd, 1)
                for j in range(2):
                    l = 2 * g + j
                    if l >= 2:
                        pe.wait_ge(s_qgd, l - 1)
                        pe.wait_ge(s_kv, l - 1)
                    for c in range(2):
                        nc.tensor.matmul(PS[2 + 2 * j][:, 0:400], xc[:, g % 2, c, j, :], wa[:, c, :], start=(c == 0), stop=(c == 1))
                    for c in range(2):
                        last = nc.tensor.matmul(PS[3 + 2 * j][:, 0:384], xc[:, g % 2, c, j, :], wb[:, c, :], start=(c == 0), stop=(c == 1))
                    last.then_inc(s_p, 1)
            pe.wait_ge(s_wo, 16)
            pe.wait_ge(s_qgd, L)
            pe.wait_ge(s_kv, L)
            for l in range(L):
                pe.wait_ge(s_on, l // 4 + 1)
                if l >= 2:
                    pe.wait_ge(s_ots, l - 1)
                for c in range(2):
                    last = nc.tensor.transpose(PS[l % 2][:, c * P:(c + 1) * P], on[:, l // 4, l % 4, c * P:(c + 1) * P], ident[:, :])
                last.then_inc(s_ot, 1)
                pe.wait_ge(s_ots, l + 1)
                if l >= 2:
                    pe.wait_ge(s_x2, l - 1)
                for c in range(2):
                    last = nc.tensor.matmul(PS[2 + l % 2][:, 0:T], oT[:, l % 2, c * P:(c + 1) * P], wo[:, c, :], start=(c == 0), stop=(c == 1))
                last.then_inc(s_y2, 1)


def stage_c(nc, shared, gamma):
    stack = ExitStack()
    with stack:
        def sb(name, shape, dt=F32):
            return stack.enter_context(nc.sbuf_tensor(name, shape, dt))

        sem = shared.sem
        X, C, ident, half = shared.X, shared.C, shared.ident, shared.half
        H, D = 8, 16
        NC = T // P
        QPART = (0, 1, 2, 0, 1, 0)
        KPART = (0, 0, 0, 1, 1, 2)
        ROWS = 6 * D

        gam = sb("c_gamma", [P, 1])
        stats = sb("c_stats", [P, NB, 6])
        mv = sb("c_mv", [P, NB, 2])
        vare = sb("c_vare", [P, NB])
        rstd = sb("c_rstd", [P, NB])
        ksp = sb("c_ksp", [P, 3, NB, T], BF16)
        kr = sb("c_kr", [P, NB, T])
        KS = sb("c_KS", [P, NB, H, T], BF16)
        VZ = sb("c_VZ", [P, NB, NC, 2, 4, 32])
        one3 = sb("c_one3", [3, H * T], BF16)
        OZ = sb("c_OZ", [P, 2, 32])
        xn = sb("c_xn", [P, 2, T])
        qsp = sb("c_qsp", [P, 2, 3, T], BF16)
        qr = sb("c_qr", [P, 2, T])
        QS = sb("c_QS", [P, 2, H, T], BF16)
        nm = sb("c_nm", [P, 2, H, NC])
        nmr = sb("c_nmr", [16, P])
        nmT = sb("c_nmT", [16, P])
        nms = sb("c_nms", [16, 2, 3, P], BF16)
        pT = sb("c_pT", [P, 2, NC, H, T])
        rinv = sb("c_rinv", [P, 2, T])
        ret = sb("c_ret", [P, 2, T])

        kd = nc.dram_tensor("k_parts", (3, P, NB, T), BF16, kind="Internal").ap()
        md = nc.dram_tensor("max_parts", (NB, 16, 3, P), BF16, kind="Internal").ap()
        qd = nc.dram_tensor("q_parts", (NB, 3, P, T), BF16, kind="Internal").ap()

        PM = [stack.enter_context(nc.psum_tensor(f"c_pm{i}", [P, 512], F32)) for i in range(2)]
        PE2 = [stack.enter_context(nc.psum_tensor(f"c_pe{i}", [P, 1024], F32)) for i in range(2)]
        PV = stack.enter_context(nc.psum_tensor("c_pv", [P, 512], F32))
        PZ = stack.enter_context(nc.psum_tensor("c_pz", [P, 512], F32))

        s_gam, s_ks, s_kd, s_kin, s_one, s_ones = sem("c_gamma_in"), sem("c_ksplit"), sem("c_k_stored"), sem("c_k_loaded"), sem("c_ones"), sem("c_one_rows")
        s_mv, s_rstd, s_xn = sem("c_mv"), sem("c_rstd"), sem("c_xn")
        s_qh, s_qr1, s_qm, s_q = sem("c_q_hi"), sem("c_q_rest"), sem("c_q_mid"), sem("c_q_lo")
        s_qd = [sem(f"c_q_stored{j}") for j in range(2)]
        s_qin = [sem(f"c_q_loaded{j}") for j in range(2)]
        s_vt, s_vz = sem("c_v_transposed"), sem("c_v_sb")
        s_m1, s_mx, s_mt, s_ms = sem("c_scores"), sem("c_max"), sem("c_maxT"), sem("c_max_split")
        s_md = sem("c_max_stored")
        s_mtc = sem("c_maxT_sb")
        s_min = [sem(f"c_max_loaded{j}") for j in range(2)]
        s_s2, s_ex, s_pv, s_ri, s_ret, s_x3 = sem("c_scoresT"), sem("c_exp"), sem("c_pv_done"), sem("c_rinv"), sem("c_ret"), sem("c_x3")
        s_dv, s_pl = sem("c_dve_chain"), sem("c_pool_chain")

        block = stack.enter_context(nc.Block())

        @block.sync
        def _(sp):
            sp.wait_ge(s_ks, 4)
            sp.dma_start(kd.rearrange("j p b t -> p j b t"), ksp[:, :, :, :]).then_inc(s_kd, 16)
            sp.wait_ge(s_kd, 16)
            for j, part in enumerate(KPART):
                for hb in range(0, NB, 4):
                    for b in range(hb, hb + 4):
                        sp.dma_start(KS[D * j:D * (j + 1), b, :, :], kd[part, :, b, :].rearrange("(h d) t -> d h t", d=D)).then_inc(s_kin, 16)

            def parts_of_q(b):
                sp.wait_ge(s_q, b + 1)
                sp.dma_start(qd[b].rearrange("j p t -> p j t"), qsp[:, b % 2, :, :]).then_inc(s_qd[b % 2], 16)
                sp.wait_ge(s_qd[b % 2], 16 * (b // 2 + 1))
                if b >= 2:
                    sp.wait_ge(s_s2, 4 * (b - 1))
                for j, part in enumerate(QPART):
                    sp.dma_start(QS[D * j:D * (j + 1), b % 2, :, :], qd[b, part].rearrange("(h d) t -> d h t", d=D)).then_inc(s_qin[b % 2], 16)

            def rows_of_max(b):
                sp.wait_ge(s_ms, b + 1)
                sp.dma_start(md[b], nms[:, b % 2, :, :]).then_inc(s_md, 16)
                sp.wait_ge(s_md, 16 * (b + 1))
                sp.dma_start(QS[ROWS:ROWS + 3, b % 2, :, :].rearrange("j h (c q) -> j (h c) q", c=NC), md[b].rearrange("r j q -> j r q")).then_inc(s_min[b % 2], 16)

            parts_of_q(0)
            rows_of_max(0)
            for b in range(1, NB):
                parts_of_q(b)
                rows_of_max(b)

        @block.gpsimd
        def _(pool):
            n = [0]

            def link(ins):
                n[0] += 1
                ins.then_inc(s_pl, 1)
                pool.wait_ge(s_pl, n[0])

            pool.dma_start(gam[:, :], gamma.partition_broadcast(P)).then_inc(s_gam, 16)
            link(pool.memset(one3[:, :], 1.0))
            pool.dma_start(KS[ROWS:ROWS + 3, :, :, :].rearrange("j b h t -> j b (h t)"), one3[:, :].unsqueeze(1).broadcast_to([3, NB, H * T])).then_inc(s_ones, 16)
            link(pool.memset(OZ[:, :, :], 0.0))
            link(pool.memset(OZ[:, 0, 0:D], 1.0))
            pool.memset(OZ[:, 1, D:2 * D], 1.0).then_inc(s_one, 1)
            pool.memset(VZ[:, :, :, :, :, :], 0.0).then_inc(s_one, 1)
            pool.wait_ge(s_mv, 1)
            pool.tensor_tensor(rstd[:, :], vare[:, :], half[:, 0:NB], ALU.pow).then_inc(s_rstd, 1)
            pool.tensor_copy(ksp[:, 0, :, :], C[:, :, :]).then_inc(s_ks, 1)
            pool.wait_ge(s_ks, 1)
            link(pool.tensor_tensor(kr[:, :, :], C[:, :, :], ksp[:, 0, :, :], ALU.subtract))
            pool.tensor_copy(ksp[:, 1, :, :], kr[:, :, :]).then_inc(s_ks, 1)
            pool.wait_ge(s_ks, 2)
            pool.tensor_tensor(ksp[:, 2, :, :], kr[:, :, :], ksp[:, 1, :, :], ALU.subtract).then_inc(s_ks, 2)

            def split_q(b):
                pool.wait_ge(s_qh, b + 1)
                pool.tensor_tensor(qr[:, b % 2, :], xn[:, b % 2, :], qsp[:, b % 2, 0, :], ALU.subtract).then_inc(s_qr1, 1)
                pool.wait_ge(s_qm, b + 1)
                pool.tensor_tensor(qsp[:, b % 2, 2, :], qr[:, b % 2, :], qsp[:, b % 2, 1, :], ALU.subtract).then_inc(s_q, 1)

            def add(b):
                pool.wait_ge(s_ret, b + 1)
                pool.tensor_tensor(X[:, b, :], ret[:, b % 2, :], X[:, b, :], ALU.add).then_inc(s_x3, 1)

            split_q(0)
            for b in range(NB):
                if b + 1 < NB:
                    split_q(b + 1)
                if b:
                    add(b - 1)
            add(NB - 1)

        @block.scalar
        def _(act):
            def hi_mid(b):
                act.wait_ge(s_xn, b + 1)
                if b >= 2:
                    act.wait_ge(s_qd[b % 2], 16 * (b // 2))
                nc.scalar.copy(qsp[:, b % 2, 0, :], xn[:, b % 2, :]).then_inc(s_qh, 1)
                act.wait_ge(s_qr1, b + 1)
                nc.scalar.copy(qsp[:, b % 2, 1, :], qr[:, b % 2, :]).then_inc(s_qm, 1)

            hi_mid(0)
            hi_mid(1)
            for b in range(NB):
                for u in range(4):
                    act.wait_ge(s_s2, 4 * b + u + 1)
                    if b >= 2 and u == 0:
                        act.wait_ge(s_pv, b - 1)
                    nc.scalar.activation(pT[:, b % 2, u // 2, 4 * (u % 2):4 * (u % 2) + 4, :], PE2[u % 2][:, :].rearrange("p (h q) -> p h q", h=4),
                                         ACT.Exp, scale=D ** -0.5).then_inc(s_ex, 1)
                if b + 2 < NB:
                    hi_mid(b + 2)

        @block.vector
        def _(dve):
            n = [0]

            def link(ins):
                n[0] += 1
                ins.then_inc(s_dv, 1)
                dve.wait_ge(s_dv, n[0])

            for b in range(NB):
                last = nc.vector.bn_stats(stats[:, b, :], X[:, b, :])
            link(last)
            for b in range(NB):
                last = nc.vector.bn_aggr(mv[:, b, :], stats[:, b, :])
            link(last)
            nc.vector.tensor_scalar(vare[:, :], mv[:, :, 1], EPS, None, ALU.add).then_inc(s_mv, 1)
            dve.wait_ge(s_rstd, 1)

            def norm(b):
                if b >= 2:
                    dve.wait_ge(s_q, b - 1)
                nc.vector.tensor_scalar(xn[:, b % 2, :], X[:, b, :], mv[:, b, 0:1], rstd[:, b:b + 1], ALU.subtract, ALU.mult).then_inc(s_xn, 1)

            def maxima(b):
                for h in range(H):
                    dve.wait_ge(s_m1, H * b + h + 1)
                    nc.vector.tensor_reduce(nm[:, b % 2, h, :], PM[h % 2][:, :].rearrange("p (c l) -> p c l", c=NC), X_AXIS, ALU.max, negate=True).then_inc(s_mx, 1)

            def split_max(b):
                dve.wait_ge(s_mt, b + 1)
                if b >= 2:
                    dve.wait_ge(s_min[b % 2], 16 * (b // 2))
                nc.vector.tensor_copy(nmT[:, :], PM[0][0:16, 0:P]).then_inc(s_mtc, 1)
                dve.wait_ge(s_mtc, b + 1)
                link(nc.vector.tensor_copy(nms[:, b % 2, 0, :], nmT[:, :]))
                link(nc.vector.tensor_tensor(nmr[:, :], nmT[:, :], nms[:, b % 2, 0, :], ALU.subtract))
                link(nc.vector.tensor_copy(nms[:, b % 2, 1, :], nmr[:, :]))
                nc.vector.tensor_tensor(nms[:, b % 2, 2, :], nmr[:, :], nms[:, b % 2, 1, :], ALU.subtract).then_inc(s_ms, 1)

            def finish(b):
                dve.wait_ge(s_pv, b + 1)
                nc.vector.reciprocal(rinv[:, b % 2, :], PZ[:, 0:T]).then_inc(s_ri, 1)
                dve.wait_ge(s_ri, b + 1)
                if b >= 2:
                    dve.wait_ge(s_x3, b - 1)
                nc.vector.scalar_tensor_tensor(ret[:, b % 2, :], PV[:, 0:T], gam[:, :], rinv[:, b % 2, :], ALU.mult, ALU.mult).then_inc(s_ret, 1)

            norm(0)
            norm(1)
            dve.wait_ge(s_one, 2)
            for b in range(NB):
                dve.wait_ge(s_vt, b + 1)
                for a in range(2):
                    last = nc.vector.tensor_copy(VZ[:, b, :, a, :, D * a:D * (a + 1)],
                                                 PM[b % 2][:, 0:T].rearrange("p (c i n) -> p c i n", c=NC, i=4)[:, :, :, D * a:D * (a + 1)])
                last.then_inc(s_vz, 1)
            maxima(0)
            split_max(0)
            dve.wait_ge(s_gam, 16)
            for b in range(NB):
                if b + 1 < NB:
                    maxima(b + 1)
                    split_max(b + 1)
                if b + 2 < NB:
                    norm(b + 2)
                if b:
                    finish(b - 1)
            finish(NB - 1)

        @block.tensor
        def _(pe):
            for b in range(NB):
                if b >= 2:
                    pe.wait_ge(s_vz, b - 1)
                for c in range(NC):
                    last = nc.tensor.transpose(PM[b % 2][:, c * P:(c + 1) * P], C[:, b, c * P:(c + 1) * P], ident[:, :])
                last.then_inc(s_vt, 1)
            pe.wait_ge(s_vz, NB)
            pe.wait_ge(s_kin, 16 * 6 * NB)
            pe.wait_ge(s_one, 2)
            pe.wait_ge(s_ones, 16)

            def scores(b, h):
                if h == 0:
                    pe.wait_ge(s_qin[b % 2], 96 * (b // 2 + 1))
                    if b:
                        pe.wait_ge(s_mtc, b)
                if H * b + h >= 2:
                    pe.wait_ge(s_mx, H * b + h - 1)
                for c in range(NC):
                    last = nc.tensor.matmul(PM[h % 2][:, c * T:(c + 1) * T], QS[0:ROWS, b % 2, h, c * P:(c + 1) * P], KS[0:ROWS, b, h, :], start=True, stop=True)
                last.then_inc(s_m1, 1)

            def max_rows(b):
                pe.wait_ge(s_mx, H * (b + 1))
                nc.tensor.transpose(PM[0][0:16, 0:P], nm[:, b % 2, :, :].rearrange("p h c -> p (h c)"), ident[:, :]).then_inc(s_mt, 1)

            def scores_t(b, u):
                c, h0 = u // 2, 4 * (u % 2)
                if u == 0:
                    pe.wait_ge(s_min[b % 2], 16 * (b // 2 + 1))
                if 4 * b + u >= 2:
                    pe.wait_ge(s_ex, 4 * b + u - 1)
                for k in range(4):
                    last = nc.tensor.matmul(PE2[u % 2][:, k * T:(k + 1) * T], KS[0:ROWS + 3, b, h0 + k, c * P:(c + 1) * P], QS[0:ROWS + 3, b % 2, h0 + k, :], start=True, stop=True)
                last.then_inc(s_s2, 1)

            def values(b, u):
                c, a = u // 2, u % 2
                if u == 0:
                    pe.wait_ge(s_ex, 4 * (b + 1))
                    if b:
                        pe.wait_ge(s_ret, b)
                for bank, w in ((PV, VZ[:, b, c, a, :, :]), (PZ, None)):
                    for i in range(4):
                        last = nc.tensor.matmul(bank[32 * i:32 * i + 32, 0:T], OZ[:, a, :] if w is None else w[:, i, :], pT[:, b % 2, c, 2 * i + a, :],
                                                start=(u == 0), stop=(u == 3))
                if u == 3:
                    last.then_inc(s_pv, 1)

            for h in range(H):
                scores(0, h)
            max_rows(0)
            for b in range(NB + 1):
                for u in range(4):
                    if b < NB:
                        scores_t(b, u)
                    if b + 1 < NB:
                        scores(b + 1, 2 * u)
                        scores(b + 1, 2 * u + 1)
                    if b:
                        values(b - 1, u)
                if b + 1 < NB:
                    max_rows(b + 1)


def stage_d(nc, shared, w_router, router_bias, w_gate, w_up, w_down, out):
    stack = ExitStack()
    with stack:
        def sb(name, shape, dt=F32):
            return stack.enter_context(nc.sbuf_tensor(name, shape, dt))

        sem = shared.sem
        X, ident, half = shared.X, shared.ident, shared.half
        E, F, K = 64, 64, 4
        FW = w_gate.shape[1]
        NK = FW // 512
        EC = FW // F

        WG = sb("d_WG", [P, 2, FW])
        WU = sb("d_WU", [P, 2, FW])
        WD = sb("d_WD", [P, FW // P, T])
        wr = sb("d_wr", [P, 2, E])
        bias = sb("d_bias", [P, E])
        iota = sb("d_iota", [P, E])
        iotai = sb("d_iotai", [P, E], mybir.dt.int32)
        stats = sb("d_stats", [P, NB, 6])
        mv = sb("d_mv", [P, NB, 2])
        vare = sb("d_vare", [P, NB])
        rstd = sb("d_rstd", [P, NB])
        xn = sb("d_xn", [P, T])
        xT = sb("d_xT", [P, 2, P])
        lg = sb("d_lg", [P, E])
        lb = sb("d_lb", [P, E])
        top = sb("d_top", [P, 8])
        topi = sb("d_topi", [P, 8], mybir.dt.uint32)
        topf = sb("d_topf", [P, 8])
        oh = sb("d_oh", [P, K, E])
        mask = sb("d_mask", [P, E])
        nmx = sb("d_nmx", [P, 1])
        ex = sb("d_ex", [P, E])
        em = sb("d_em", [P, E])
        den = sb("d_den", [P, 1])
        rden = sb("d_rden", [P, 1])
        comb = sb("d_comb", [P, EC])
        sg = sb("d_sg", [P, 2, 512])
        h = sb("d_h", [P, 2, 512])
        hc = sb("d_hc", [P, 2, 512])
        hT = sb("d_hT", [P, 2, 512])

        PS = [stack.enter_context(nc.psum_tensor(f"d_ps{i}", [P, 512], F32)) for i in range(8)]
        s_w, s_i, s_it, s_mv, s_rstd, s_xn, s_t, s_xt, s_r, s_lg, s_ex, s_comb, s_g, s_u, s_sg, s_h, s_hc, s_ht, s_hts, s_y, s_x4, s_dv, s_out, s_c1 = (sem("d_" + n) for n in
            ("w", "i", "iota", "mv", "rstd", "xn", "t", "xt", "router", "lg", "ex", "comb", "g", "u", "sg", "h", "hc", "ht", "hts", "y", "x4", "dve_chain", "stored", "ones"))

        block = stack.enter_context(nc.Block())

        @block.sync
        def _(sp):
            sp.dma_start(wr[:, :, :], w_router.rearrange("(c p) n -> p c n", p=P)).then_inc(s_w, 16)
            sp.dma_start(bias[:, :], router_bias.partition_broadcast(P)).then_inc(s_w, 16)
            sp.dma_start(WG[:, :, :], w_gate.rearrange("(c p) n -> p c n", p=P)).then_inc(s_w, 16)
            sp.dma_start(WU[:, :, :], w_up.rearrange("(c p) n -> p c n", p=P)).then_inc(s_w, 16)
            sp.dma_start(WD[:, :, :], w_down.rearrange("(c p) n -> p c n", p=P)).then_inc(s_w, 16)
            for b in range(NB):
                sp.wait_ge(s_x4, b + 1)
                sp.dma_start(out[b], X[:, b, :]).then_inc(s_out, 16)
            sp.wait_ge(s_out, 16 * NB)

        @block.gpsimd
        def _(pool):
            pool.iota(iotai[:, :], pattern=[[1, E]], base=0, channel_multiplier=0).then_inc(s_i, 1)
            pool.memset(comb[:, E:EC], 1.0).then_inc(s_c1, 1)
            pool.wait_ge(s_mv, 1)
            pool.tensor_tensor(rstd[:, :], vare[:, :], half[:, 0:NB], ALU.pow).then_inc(s_rstd, 1)
            for b in range(NB):
                pool.wait_ge(s_comb, b + 1)
                if b == 0:
                    pool.wait_ge(s_c1, 1)
                for k in range(NK):
                    n = NK * b + k
                    pool.wait_ge(s_h, n + 1)
                    if n >= 2:
                        pool.wait_ge(s_ht, n - 1)
                    pool.tensor_tensor(hc[:, n % 2, :].rearrange("p (e f) -> p e f", f=F), h[:, n % 2, :].rearrange("p (e f) -> p e f", f=F),
                                       comb[:, 8 * k:8 * k + 8].unsqueeze(2).broadcast_to([P, 8, F]), ALU.mult).then_inc(s_hc, 1)

        @block.scalar
        def _(act):
            for b in range(NB):
                act.wait_ge(s_t, b + 1)
                nc.scalar.copy(xT[:, :, :], PS[0][:, 0:T].rearrange("p (c t) -> p c t", c=2)).then_inc(s_xt, 1)
                act.wait_ge(s_lg, b + 1)
                nc.scalar.activation(ex[:, :], lg[:, :], ACT.Exp, bias=nmx[:, :]).then_inc(s_ex, 1)
                for k in range(NK + 1):
                    n = NK * b + k
                    if k < NK:
                        act.wait_ge(s_g, n + 1)
                        if n >= 2:
                            act.wait_ge(s_h, n - 1)
                        nc.scalar.activation(sg[:, n % 2, :], PS[2 + 2 * (n % 2)][:, :], ACT.Silu).then_inc(s_sg, 1)
                    if k:
                        m = n - 1
                        act.wait_ge(s_ht, m + 1)
                        if m >= 2:
                            act.wait_ge(s_y, m - 1)
                        nc.scalar.copy(hT[:, m % 2, :], PS[6][:, :]).then_inc(s_hts, 1)

        @block.vector
        def _(dve):
            n = [0]

            def link(ins):
                n[0] += 1
                ins.then_inc(s_dv, 1)
                dve.wait_ge(s_dv, n[0])

            for b in range(NB):
                last = nc.vector.bn_stats(stats[:, b, :], X[:, b, :])
            link(last)
            for b in range(NB):
                last = nc.vector.bn_aggr(mv[:, b, :], stats[:, b, :])
            link(last)
            nc.vector.tensor_scalar(vare[:, :], mv[:, :, 1], EPS, None, ALU.add).then_inc(s_mv, 1)
            dve.wait_ge(s_i, 1)
            link(nc.vector.tensor_copy(iota[:, :], iotai[:, :]))
            dve.wait_ge(s_rstd, 1)
            for b in range(NB):
                if b:
                    dve.wait_ge(s_t, b)
                nc.vector.tensor_scalar(xn[:, :], X[:, b, :], mv[:, b, 0:1], rstd[:, b:b + 1], ALU.subtract, ALU.mult).then_inc(s_xn, 1)
                dve.wait_ge(s_r, b + 1)
                if b == 0:
                    dve.wait_ge(s_w, 80)
                else:
                    dve.wait_ge(s_hc, NK * b)
                link(nc.vector.tensor_copy(lg[:, :], PS[1][:, 0:E]))
                nc.vector.tensor_reduce(nmx[:, :], lg[:, :], X_AXIS, ALU.max, negate=True).then_inc(s_lg, 1)
                link(nc.vector.tensor_tensor(lb[:, :], lg[:, :], bias[:, :], ALU.add))
                link(nc.vector.max(top[:, :], lb[:, :]))
                link(nc.vector.max_index(topi[:, :], top[:, :], lb[:, :]))
                link(nc.vector.tensor_copy(topf[:, :], topi[:, :]))
                link(nc.vector.tensor_tensor(oh[:, :, :], iota[:, :].unsqueeze(1).broadcast_to([P, K, E]), topf[:, 0:K].unsqueeze(2).broadcast_to([P, K, E]), ALU.is_equal))
                link(nc.vector.reduce_sum(mask[:, :], oh[:, :, :].rearrange("p k e -> p e k"), X_AXIS))
                dve.wait_ge(s_ex, b + 1)
                link(nc.vector.tensor_tensor(em[:, :], ex[:, :], mask[:, :], ALU.mult))
                link(nc.vector.reduce_sum(den[:, :], em[:, :], X_AXIS))
                link(nc.vector.reciprocal(rden[:, :], den[:, :]))
                nc.vector.tensor_scalar(comb[:, 0:E], em[:, :], rden[:, :], None, ALU.mult).then_inc(s_comb, 1)
                for k in range(NK):
                    m = NK * b + k
                    dve.wait_ge(s_sg, m + 1)
                    dve.wait_ge(s_u, m + 1)
                    if m >= 2:
                        dve.wait_ge(s_hc, m - 1)
                    nc.vector.tensor_tensor(h[:, m % 2, :], PS[3 + 2 * (m % 2)][:, :], sg[:, m % 2, :], ALU.mult).then_inc(s_h, 1)
                dve.wait_ge(s_y, NK * (b + 1))
                nc.vector.tensor_tensor(X[:, b, :], PS[7][:, 0:T], X[:, b, :], ALU.add).then_inc(s_x4, 1)

        @block.tensor
        def _(pe):
            pe.wait_ge(s_w, 80)

            def down(m):
                k = m % NK
                pe.wait_ge(s_hc, m + 1)
                if m:
                    pe.wait_ge(s_hts, m)
                for j in range(4):
                    last = nc.tensor.transpose(PS[6][:, j * P:(j + 1) * P], hc[:, m % 2, j * P:(j + 1) * P], ident[:, :])
                last.then_inc(s_ht, 1)
                pe.wait_ge(s_hts, m + 1)
                if k == 0 and m:
                    pe.wait_ge(s_x4, m // NK)
                for j in range(4):
                    last = nc.tensor.matmul(PS[7][:, 0:T], hT[:, m % 2, j * P:(j + 1) * P], WD[:, 4 * k + j, :], start=(k == 0 and j == 0), stop=(k == NK - 1 and j == 3))
                last.then_inc(s_y, 1)

            for b in range(NB):
                pe.wait_ge(s_xn, b + 1)
                for c in range(2):
                    last = nc.tensor.transpose(PS[0][:, c * P:(c + 1) * P], xn[:, c * P:(c + 1) * P], ident[:, :])
                last.then_inc(s_t, 1)
                pe.wait_ge(s_xt, b + 1)
                if b:
                    pe.wait_ge(s_lg, b)
                for c in range(2):
                    last = nc.tensor.matmul(PS[1][:, 0:E], xT[:, c, :], wr[:, c, :], start=(c == 0), stop=(c == 1))
                last.then_inc(s_r, 1)
                for k in range(NK):
                    m = NK * b + k
                    if m >= 2:
                        pe.wait_ge(s_h, m - 1)
                    for c in range(2):
                        last = nc.tensor.matmul(PS[2 + 2 * (m % 2)][:, :], xT[:, c, :], WG[:, c, 512 * k:512 * (k + 1)], start=(c == 0), stop=(c == 1))
                    last.then_inc(s_g, 1)
                    for c in range(2):
                        last = nc.tensor.matmul(PS[3 + 2 * (m % 2)][:, :], xT[:, c, :], WU[:, c, 512 * k:512 * (k + 1)], start=(c == 0), stop=(c == 1))
                    last.then_inc(s_u, 1)
                    if k:
                        down(m - 1)
                down(NK * b + NK - 1)


def build(nc, x, ctx_in, theta_wT, phi_wT, g_wT, out_wT2, col_consts, gamma2, beta2,
          conv_cols, w_qg, w_kv, rw, rot, w_out, gamma,
          w_router, router_bias, w_gate, w_up, w_down, out):
    stack = ExitStack()
    with stack:
        shared = Shared()
        shared.sem = lambda name: stack.enter_context(nc.semaphore(name))
        shared.X = stack.enter_context(nc.sbuf_tensor("X", [P, NB, T], F32))
        shared.C = stack.enter_context(nc.sbuf_tensor("C", [P, NB, T], F32))
        shared.ident = stack.enter_context(nc.sbuf_tensor("ident", [P, P], F32))
        shared.half = stack.enter_context(nc.sbuf_tensor("half", [P, 64], F32))
        stage_a(nc, shared, x, ctx_in, theta_wT, phi_wT, g_wT, out_wT2, col_consts, gamma2, beta2)
        stage_b(nc, shared, conv_cols, w_qg, w_kv, rw, rot, w_out)
        stage_c(nc, shared, gamma)
        stage_d(nc, shared, w_router, router_bias, w_gate, w_up, w_down, out)


def kernel(**inputs):
    import concourse.bacc as _bacc
    from concourse import mybir as _mybir
    from concourse.bass_utils import run_bass_kernel_spmd as _run

    a = {k: np.asarray(v) for k, v in inputs.items()}
    two = lambda m: np.ascontiguousarray(np.concatenate([m, m], axis=0))
    def own_half(w):
        z = np.zeros_like(w)
        return np.stack([np.concatenate([w, z]), np.concatenate([z, w])], axis=1)

    host = {
        "x": a["x"], "ctx_in": a["ctx_2048"],
        "theta_wT": a["L0_xattn_theta_w"].T, "phi_wT": a["L0_xattn_phi_w"].T, "g_wT": a["L0_xattn_g_w"].T,
        "out_wT2": own_half(a["L0_xattn_out_w"].T),
        "col_consts": np.stack([two(a["L0_xattn_theta_b"]), two(a["L0_xattn_phi_b"]), two(a["L0_xattn_g_b"]), a["L0_xattn_out_b"]], axis=1),
        "gamma2": two(a["L0_xattn_ln_gamma"]), "beta2": two(a["L0_xattn_ln_beta"]),
    }
    def side_by_side(routed, common):
        return np.concatenate([w.transpose(1, 0, 2).reshape(T, -1) for w in (routed, common)], axis=1)

    inv_freq = (1.0 / np.float32(10000.0) ** (np.arange(0, 8, 2, dtype=np.float32) / np.float32(8))).astype(np.float32)
    ang = np.arange(NB, dtype=np.float32)[:, None] * inv_freq[None, :]
    host |= {
        "conv_cols": a["L0_ffn_conv_w"].reshape(2, P, 2).transpose(1, 0, 2),
        "w_qg": np.concatenate([a["L0_ffn_Wq"], a["L0_ffn_Wg"]], axis=1),
        "w_kv": np.concatenate([a["L0_ffn_Wk"], a["L0_ffn_Wv"]], axis=1),
        "rw": a["L0_ffn_router_w"],
        "rot": np.stack([np.cos(ang), np.sin(ang), -np.sin(ang)]).astype(np.float32),
        "w_out": a["L0_ffn_Wout"],
        "c_gamma": a["L1_xattn_gamma"].reshape(1),
        "w_router": a["L1_ffn_router_w"], "router_bias": a["L1_ffn_router_bias"],
        "w_gate": side_by_side(a["L1_ffn_wg"], a["L1_ffn_swg"]), "w_up": side_by_side(a["L1_ffn_wu"], a["L1_ffn_swu"]),
        "w_down": np.concatenate([a["L1_ffn_wd"].reshape(-1, T), a["L1_ffn_swd"].reshape(-1, T)], axis=0),
    }
    nc = _bacc.Bacc("TRN2", target_bir_lowering=False, num_devices=1)
    arrays, args = {}, []
    for name, v in host.items():
        v = np.ascontiguousarray(v)
        arrays[name + "_dram"] = v
        args.append(nc.dram_tensor(name + "_dram", v.shape, _mybir.dt.from_np(v.dtype), kind="ExternalInput").ap())
    args.append(nc.dram_tensor("out_dram", (NB, P, T), F32, kind="ExternalOutput").ap())
    build(nc, *args)
    r = _run(nc, [arrays], core_ids=[0])
    return r.results[0]["out_dram"]
```

```python
import numpy as np
import concourse.bass as bass
from concourse import mybir
from contextlib import ExitStack

F32 = mybir.dt.float32
BF16 = mybir.dt.bfloat16
ALU = mybir.AluOpType
ACT = mybir.ActivationFunctionType
X_AXIS = mybir.AxisListType.X

P = 128
NB = 8
T = 256
EPS = 1e-5
QPART = (0, 1, 2, 0, 1, 0)
KPART = (0, 0, 0, 1, 1, 2)
N_EXPERT = 64
OVER_TILES = 32
N_TILES = N_EXPERT + OVER_TILES


class Shared:
    pass


def stage_a(nc, shared, x, ctx_in, theta_wT, phi_wT, g_wT, out_wT2, col_consts, gamma2, beta2):
    stack = ExitStack()
    with stack:
        def sb(name, shape, dt=F32):
            return stack.enter_context(nc.sbuf_tensor(name, shape, dt))

        sem = shared.sem

        NP = NB // 2
        X, C, ident, half = shared.X, shared.C, shared.ident, shared.half
        thw = sb("thw", [P, 64])
        phw = sb("phw", [P, 64])
        gw = sb("gw", [P, 64])
        outw = sb("outw", [P, 2, P])
        cols = sb("cols", [P, 4])
        gamma = sb("gamma", [P, T])
        beta = sb("beta", [P, T])
        blk64 = sb("blk64", [P, P])

        stats = sb("stats", [P, NB, 6])
        mv = sb("mv", [P, NB, 2])
        vare = sb("vare", [P, NB])
        rstd = sb("rstd", [P, NB])
        xn = sb("xn", [P, 2, 2, T])
        thph = sb("thph", [P, 2, 2 * T])
        gx = sb("gx", [P, 2, 2 * 2 * 64])
        nmax = sb("nmax", [P, 2, 4])
        psums = sb("psums", [P, 2, 4])
        prec = sb("prec", [P, 2, 4])
        pr = sb("pr", [P, 2, 4, T])
        pn = sb("pn", [P, 4, T])
        pT = sb("pT", [P, 4, T])
        tx = sb("tx", [P, T])
        tstat = sb("tstat", [P, 6])
        tmv = sb("tmv", [P, 2])
        te = sb("te", [P, 2])
        tm = sb("tm", [P, 4])
        trs = sb("trs", [P, 1])
        h1 = sb("h1", [P, T])
        h2 = sb("h2", [P, T])
        h3 = sb("h3", [P, T])
        hr = sb("hr", [P, T])
        xa = sb("xa", [P, 2, T])
        ksp, kr = shared.ksp, sb("kr", [P, 2, T])

        PS = [stack.enter_context(nc.psum_tensor(f"ps{i}", [P, 512], F32)) for i in range(8)]

        sx, sc_, sw = sem("x_in"), sem("ctx_in"), sem("w_in")
        s_id = sem("ident_ready")
        s_mv = sem("mv_ready")
        s_rstd = sem("rstd_ready")
        s_xn = sem("xn_ready")
        s_tp = sem("thetaphi_done")
        s_g = sem("g_done")
        s_tps = sem("thetaphi_sb")
        s_gs = sem("g_sb")
        s_sc = sem("scores_done")
        s_nm = sem("nmax_ready")
        s_ex = sem("exp_done")
        s_pn = sem("pn_ready")
        s_pt = sem("pT_done")
        s_pta = sem("pT_sb_act")
        s_ptd = sem("pT_sb_dve")
        s_tx = sem("tx_done")
        s_txs = sem("tx_sb")
        s_te = sem("te_ready")
        s_st = sem("stat_done")
        s_tv = sem("tvar_ready")
        s_tr = sem("trstd_ready")
        s_h1 = sem("h1_ready")
        s_h2 = sem("h2_ready")
        s_h3 = sem("h3_ready")
        s_h = sem("h_ready")
        s_o = sem("o_done")
        s_xa = sem("xa_ready")
        s_x1 = sem("x1_ready")
        s_dv = sem("dve_chain")
        s_ks, s_kr = sem("ctx_split"), sem("ctx_rest")

        thb, phb, gb, outb = (cols[:, j:j + 1] for j in range(4))

        block = stack.enter_context(nc.Block())

        @block.sync
        def _(sp):
            sp.dma_start(X[:, 0:2, :], x[0:2].rearrange("b p t -> p b t")).then_inc(sx, 16)
            sp.dma_start(X[:, 2:NB, :], x[2:NB].rearrange("b p t -> p b t")).then_inc(sx, 16)
            sp.wait_ge(s_ks, 3 * NP)
            for h in range(8):
                sp.dma_start(shared.kd[:, :, :, h, :].rearrange("d j b t -> d (j b) t"), ksp[16 * h:16 * h + 16, :, :, :].rearrange("p j b t -> p (j b) t")).then_inc(shared.s_kd, 16)

        @block.gpsimd
        def _(pool):
            pool.memset(ident[:, :], 0.0).then_inc(s_id, 1)
            pool.memset(blk64[:, :], 0.0).then_inc(s_id, 1)
            pool.memset(half[:, :], -0.5).then_inc(s_id, 1)
            pool.wait_ge(s_id, 3)
            pool.affine_select(out=ident[:, :], in_=ident[:, :], compare_op=ALU.not_equal, fill=1.0, base=0,
                               pattern=[[-1, P]], channel_multiplier=1).then_inc(s_id, 1)
            pool.wait_ge(s_id, 4)
            pool.memset(blk64[0:64, 0:64], 1.0 / 64).then_inc(s_id, 1)
            pool.wait_ge(s_id, 5)
            pool.memset(blk64[64:128, 64:128], 1.0 / 64).then_inc(s_id, 1)
            pool.wait_ge(s_id, 6)
            pool.wait_ge(s_mv, 1)
            pool.tensor_tensor(rstd[:, :], vare[:, :], half[:, 0:NB], ALU.pow).then_inc(s_rstd, 1)
            for i in range(NP):
                bs = slice(2 * i, 2 * i + 2)
                pool.wait_ge(sc_, 16)
                pool.tensor_copy(ksp[:, 0, bs, :], C[:, bs, :]).then_inc(s_ks, 1)
                pool.wait_ge(s_ks, 3 * i + 1)
                pool.tensor_tensor(kr[:, :, :], C[:, bs, :], ksp[:, 0, bs, :], ALU.subtract).then_inc(s_kr, 1)
                pool.wait_ge(s_kr, i + 1)
                pool.tensor_copy(ksp[:, 1, bs, :], kr[:, :, :]).then_inc(s_ks, 1)
                pool.wait_ge(s_ks, 3 * i + 2)
                pool.tensor_tensor(ksp[:, 2, bs, :], kr[:, :, :], ksp[:, 1, bs, :], ALU.subtract).then_inc(s_ks, 1)
                pool.wait_ge(s_ks, 3 * i + 3)
                pool.wait_ge(s_tv, i + 1)
                pool.tensor_tensor(trs[:, :], tm[:, 3:4], half[:, 0:1], ALU.pow).then_inc(s_tr, 1)
                pool.wait_ge(s_h1, i + 1)
                pool.tensor_tensor(h2[:, :], h1[:, :], gamma[:, :], ALU.mult).then_inc(s_h2, 1)
                pool.wait_ge(s_h2, i + 1)
                pool.tensor_tensor(h3[:, :], h2[:, :], beta[:, :], ALU.add).then_inc(s_h3, 1)
                pool.wait_ge(s_xa, i + 1)
                pool.wait_ge(sc_, 16)
                pool.tensor_tensor(X[:, 2 * i:2 * i + 2, :], xa[:, :, :], C[:, 2 * i:2 * i + 2, :], ALU.add).then_inc(s_x1, 1)

        @block.scalar
        def _(act):
            act.dma_start(cols[:, :], col_consts).then_inc(sw, 16)
            act.dma_start(thw[:, :], theta_wT).then_inc(sw, 16)
            act.dma_start(phw[:, :], phi_wT).then_inc(sw, 16)
            act.dma_start(gw[:, :], g_wT).then_inc(sw, 16)
            act.dma_start(C[:, :, :], ctx_in.rearrange("b p t -> p b t")).then_inc(sc_, 16)
            act.dma_start(outw[:, :, :], out_wT2).then_inc(sw, 16)
            act.dma_start(gamma[:, :], gamma2).then_inc(sw, 16)
            act.dma_start(beta[:, :], beta2).then_inc(sw, 16)
            act.wait_ge(sw, 7 * 16)

            def front(i):
                s = i % 2
                act.wait_ge(s_tp, i + 1)
                nc.scalar.activation(thph[:, s, 0:T], PS[0][:, 0:T], ACT.Identity, bias=thb)
                nc.scalar.activation(thph[:, s, T:2 * T], PS[0][:, T:2 * T], ACT.Identity, bias=phb).then_inc(s_tps, 1)
                act.wait_ge(s_nm, i + 1)
                for k in range(4):
                    last = nc.scalar.activation(pr[:, s, k, :], PS[2 + k // 2][:, (k % 2) * T:(k % 2 + 1) * T], ACT.Exp,
                                                bias=nmax[:, s, k:k + 1], accum_out=psums[:, s, k:k + 1])
                last.then_inc(s_ex, 1)

            def back(i):
                act.wait_ge(s_pt, i + 1)
                nc.scalar.copy(pT[:, 0:2, :], PS[4][:, :]).then_inc(s_pta, 1)
                act.wait_ge(s_tx, i + 1)
                if i:
                    act.wait_ge(s_h1, i)
                nc.scalar.activation(tx[:, :], PS[6][:, 0:T], ACT.Identity, bias=gb).then_inc(s_txs, 1)
                act.wait_ge(s_h3, i + 1)
                nc.scalar.activation(hr[:, :], h3[:, :], ACT.Relu).then_inc(s_h, 1)

            for i in range(NP + 1):
                if i < NP:
                    front(i)
                if i > 0:
                    back(i - 1)

        @block.vector
        def _(dve):
            n = [0]

            def link(ins):
                n[0] += 1
                ins.then_inc(s_dv, 1)
                dve.wait_ge(s_dv, n[0])

            dve.wait_ge(sx, 32)
            for b in range(NB):
                last = nc.vector.bn_stats(stats[:, b, :], X[:, b, :])
            link(last)
            for b in range(NB):
                last = nc.vector.bn_aggr(mv[:, b, :], stats[:, b, :])
            link(last)
            nc.vector.tensor_scalar(vare[:, :], mv[:, :, 1], EPS, None, ALU.add).then_inc(s_mv, 1)
            dve.wait_ge(s_rstd, 1)

            def xnorm(i):
                s = i % 2
                if i >= 2:
                    dve.wait_ge(s_g, i - 1)
                for j in range(2):
                    b = 2 * i + j
                    last = nc.vector.tensor_scalar(xn[:, s, j, :], X[:, b, :], mv[:, b, 0:1], rstd[:, b:b + 1], ALU.subtract, ALU.mult)
                last.then_inc(s_xn, 1)

            def front(i):
                s = i % 2
                if i + 1 < NP:
                    xnorm(i + 1)
                dve.wait_ge(s_g, i + 1)
                nc.vector.tensor_copy(gx[:, s, :], PS[1][:, 0:256]).then_inc(s_gs, 1)
                dve.wait_ge(s_sc, i + 1)
                for k in range(2):
                    last = nc.vector.tensor_reduce(nmax[:, s, 2 * k:2 * k + 2], PS[2 + k][:, :].rearrange("p (c s) -> p c s", c=2),
                                                   X_AXIS, ALU.max, negate=True)
                last.then_inc(s_nm, 1)

            def norm(i):
                s = i % 2
                dve.wait_ge(s_ex, i + 1)
                link(nc.vector.reciprocal(prec[:, s, :], psums[:, s, :]))
                if i:
                    dve.wait_ge(s_pt, i)
                for k in range(4):
                    last = nc.vector.tensor_scalar(pn[:, k, :], pr[:, s, k, :], prec[:, s, k:k + 1], None, ALU.mult)
                last.then_inc(s_pn, 1)

            def back(i):
                dve.wait_ge(s_pt, i + 1)
                nc.vector.tensor_copy(pT[:, 2:4, :], PS[5][:, :].rearrange("p (c s) -> p c s", c=2)).then_inc(s_ptd, 1)
                dve.wait_ge(s_txs, i + 1)
                link(nc.vector.bn_stats(tstat[:, :], tx[:, :]))
                link(nc.vector.bn_aggr(tmv[:, :], tstat[:, :]))
                nc.vector.tensor_copy(te[:, 0:1], tmv[:, 0:1])
                link(nc.vector.tensor_tensor(tm[:, 0:1], tmv[:, 0:1], tmv[:, 0:1], ALU.mult))
                nc.vector.tensor_tensor(te[:, 1:2], tm[:, 0:1], tmv[:, 1:2], ALU.add).then_inc(s_te, 1)
                dve.wait_ge(s_st, i + 1)
                link(nc.vector.tensor_copy(tm[:, 1:3], PS[6][:, T:T + 2]))
                link(nc.vector.tensor_tensor(tm[:, 0:1], tm[:, 1:2], tm[:, 1:2], ALU.mult))
                link(nc.vector.tensor_tensor(tm[:, 0:1], tm[:, 2:3], tm[:, 0:1], ALU.subtract))
                nc.vector.tensor_scalar(tm[:, 3:4], tm[:, 0:1], EPS, None, ALU.add).then_inc(s_tv, 1)
                dve.wait_ge(s_tr, i + 1)
                if i:
                    dve.wait_ge(s_h2, i)
                nc.vector.tensor_scalar(h1[:, :], tx[:, :], tm[:, 1:2], trs[:, :], ALU.subtract, ALU.mult).then_inc(s_h1, 1)
                dve.wait_ge(s_o, i + 1)
                if i:
                    dve.wait_ge(s_x1, i)
                nc.vector.scalar_tensor_tensor(xa[:, :, :], PS[7][:, :].rearrange("p (b t) -> p b t", b=2), outb,
                                               X[:, 2 * i:2 * i + 2, :], ALU.add, ALU.add).then_inc(s_xa, 1)

            xnorm(0)
            for i in range(NP + 1):
                if i < NP:
                    front(i)
                if i > 0:
                    back(i - 1)
                if i < NP:
                    norm(i)

        @block.tensor
        def _(pe):
            pe.wait_ge(sw, 7 * 16)
            pe.wait_ge(sc_, 16)
            pe.wait_ge(s_id, 6)

            def front(i):
                s = i % 2
                if i:
                    pe.wait_ge(s_tps, i)
                for j in range(2):
                    nc.tensor.matmul(PS[0][64 * j:64 * j + 64, 0:T], thw[:, :], C[:, 2 * i + j, :], start=True, stop=True)
                pe.wait_ge(s_xn, i + 1)
                for j in range(2):
                    last = nc.tensor.matmul(PS[0][64 * j:64 * j + 64, T:2 * T], phw[:, :], xn[:, s, j, :], start=True, stop=True)
                last.then_inc(s_tp, 1)
                if i:
                    pe.wait_ge(s_gs, i)
                for j in range(2):
                    for c in range(2):
                        k = 2 * j + c
                        last = nc.tensor.matmul(PS[1][:, 64 * k:64 * k + 64], xn[:, s, j, c * P:(c + 1) * P], gw[:, :], start=True, stop=True)
                last.then_inc(s_g, 1)
                pe.wait_ge(s_tps, i + 1)
                if i:
                    pe.wait_ge(s_ex, i)
                for j in range(2):
                    for c in range(2):
                        last = nc.tensor.matmul(PS[2 + j][:, c * T:(c + 1) * T], thph[64 * j:64 * j + 64, s, c * P:(c + 1) * P],
                                                thph[64 * j:64 * j + 64, s, T:2 * T], start=True, stop=True)
                last.then_inc(s_sc, 1)

            def back(i):
                s = i % 2
                pe.wait_ge(s_pn, i + 1)
                if i:
                    pe.wait_ge(s_pta, i)
                    pe.wait_ge(s_ptd, i)
                for j in range(2):
                    for c in range(2):
                        for ct in range(2):
                            last = nc.tensor.transpose(PS[4 + j][:, c * T + ct * P:c * T + (ct + 1) * P], pn[:, 2 * j + ct, c * P:(c + 1) * P], ident[:, :])
                last.then_inc(s_pt, 1)
                pe.wait_ge(s_gs, i + 1)
                pe.wait_ge(s_pta, i + 1)
                pe.wait_ge(s_ptd, i + 1)
                if i:
                    pe.wait_ge(s_tv, i)
                for c in range(2):
                    for j in range(2):
                        last = nc.tensor.matmul(PS[6][64 * j:64 * j + 64, 0:T], gx[:, s, 64 * (2 * j + c):64 * (2 * j + c) + 64],
                                                pT[:, 2 * j + c, :], start=(c == 0), stop=(c == 1))
                last.then_inc(s_tx, 1)
                pe.wait_ge(s_te, i + 1)
                nc.tensor.matmul(PS[6][:, T:T + 2], blk64[:, :], te[:, :], start=True, stop=True).then_inc(s_st, 1)
                pe.wait_ge(s_h, i + 1)
                if i:
                    pe.wait_ge(s_xa, i)
                for j in range(2):
                    last = nc.tensor.matmul(PS[7][:, j * T:(j + 1) * T], outw[:, j, :], hr[:, :], start=True, stop=True)
                last.then_inc(s_o, 1)

            for i in range(NP + 1):
                if i < NP:
                    front(i)
                if i > 0:
                    back(i - 1)



def stage_b(nc, shared, conv_cols, w_qg, w_kv, rw, rot, w_out):
    stack = ExitStack()
    with stack:
        def sb(name, shape, dt=F32):
            return stack.enter_context(nc.sbuf_tensor(name, shape, dt))

        sem = shared.sem
        X, ident, half = shared.X, shared.ident, shared.half
        L, H, DK, DV = NB, 16, 8, 16
        NG = L // 2

        zeros = sb("b_zeros", [P, T])
        one3 = sb("b_one3", [3, 8 * T], BF16)
        s_z, s_one3 = sem("b_zeros_ready"), sem("b_ones_ready")
        shared.n_zero_dmas = 8
        cw = sb("b_cw", [P, 2, 2])
        wa = sb("b_wa", [P, 2, 400])
        wb = sb("b_wb", [P, 2, 384])
        wo = sb("b_wo", [P, 2, T])
        rws = sb("b_rw", [P, H, DV, 2])
        rwd = sb("b_rwd", [P, H, DV])
        wtmp = sb("b_wtmp", [P, 2, T])
        wmean = sb("b_wmean", [P, 2, H])
        trig = sb("b_trig", [P, 3, L, 4])
        lp1 = sb("b_lp1", [P, L, H])

        stats = sb("b_stats", [P, L, 6])
        mv = sb("b_mv", [P, L, 2])
        vare = sb("b_vare", [P, L])
        rstd = sb("b_rstd", [P, L])
        xn = sb("b_xn", [P, 2, 2, T])
        XT = sb("b_XT", [P, 2, L + 1, P])
        tmp = sb("b_tmp", [P, 2, 2, P])
        y = sb("b_y", [P, 2, 2, P])
        xc = sb("b_xc", [P, 2, 2, 2, P])
        Q = sb("b_Q", [P, L, P])
        G = sb("b_G", [P, L, T])
        D = sb("b_D", [P, L, H])
        KV = sb("b_KV", [P, L, 384])
        r1 = sb("b_r1", [P, 4, P])
        r2 = sb("b_r2", [P, 4, P])
        r1k = sb("b_r1k", [P, 4, P])
        r2k = sb("b_r2k", [P, 4, P])
        QR = sb("b_QR", [P, L, P])
        KR = sb("b_KR", [P, L, P])
        ind = sb("b_ind", [P, L, H])
        cum = sb("b_cum", [P, L, H])
        ca = sb("b_ca", [P, L, H])
        cb = sb("b_cb", [P, L, H])
        cc = sb("b_cc", [P, L, H])
        cd = sb("b_cd", [P, L, H])
        absd = sb("b_absd", [P, L, H])
        sg = sb("b_sg", [P, L, H])
        cf = sb("b_cf", [P, L, H])
        same = sb("b_same", [P, L, L, H])
        AC = sb("b_AC", [P, L, L, H])
        prod = sb("b_prod", [P, 2, L * P])
        S = sb("b_S", [P, 2, L * H])
        S2 = sb("b_S2", [P, 2, L * H])
        W = sb("b_W", [P, 2, L * T])
        O = sb("b_O", [P, L, T])
        sq = sb("b_sq", [P, 4, T])
        vs = sb("b_vs", [P, 4 * H])
        ve = sb("b_ve", [P, 4 * H])
        vr = sb("b_vr", [P, 4 * H])
        og = sb("b_og", [P, 4, T])
        on = sb("b_on", [P, 2, 4, T])
        oT = xn[:, :, :, :].rearrange("p a j t -> p a (j t)")

        PS = [stack.enter_context(nc.psum_tensor(f"b_ps{i}", [P, 512], F32)) for i in range(8)]
        s_w, s_cw, s_rw, s_wo, s_tg = sem("b_w_in"), sem("b_cw_in"), sem("b_rw_in"), sem("b_wo_in"), sem("b_trig_in")
        s_lp = sem("b_consts")
        s_wd = sem("b_weights_ready")
        s_mv, s_rstd = sem("b_mv"), sem("b_rstd")
        s_xn, s_t, s_xt, s_y, s_xc, s_p = sem("b_xn"), sem("b_transposed"), sem("b_xT_sb"), sem("b_conv"), sem("b_xc"), sem("b_proj")
        s_qgd, s_kv = sem("b_qgd_sb"), sem("b_kv_sb")
        s_qr, s_kr = sem("b_q_rot"), sem("b_k_rot")
        s_abs, s_sg = sem("b_abs"), sem("b_sig")
        s_pr, s_s2, s_W, s_O = sem("b_prod"), sem("b_scores"), sem("b_W"), sem("b_O")
        s_red = sem("b_prod_used")
        s_sq, s_ve, s_vr, s_og, s_on, s_ot, s_ots, s_y2, s_x2 = (sem("b_" + n) for n in
            ("sq", "ve", "vr", "og", "on", "oT", "oT_sb", "wout", "x2"))
        s_dv, s_pl = sem("b_dve_chain"), sem("b_pool_chain")

        block = stack.enter_context(nc.Block())

        @block.sync
        def _(sp):
            sp.dma_start(cw[:, :, :], conv_cols).then_inc(s_cw, 16)
            sp.dma_start(wa[:, :, 0:384], w_qg.rearrange("(c p) n -> p c n", p=P)).then_inc(s_w, 16)
            sp.dma_start(wb[:, :, :], w_kv.rearrange("(c p) n -> p c n", p=P)).then_inc(s_w, 16)
            sp.dma_start(rws[:, :, :, :], rw.partition_broadcast(P)).then_inc(s_rw, 16)
            sp.dma_start(trig[:, :, :, :], rot.partition_broadcast(P)).then_inc(s_tg, 16)
            sp.dma_start(wo[:, :, :], w_out.rearrange("(c p) n -> p c n", p=P)).then_inc(s_wo, 16)
            sp.wait_ge(shared.s_kd, 16 * 8)
            for j, part in enumerate(KPART):
                sp.dma_start(shared.KS[16 * j:16 * (j + 1), :, :, :], shared.kd[:, part, :, :, :]).then_inc(shared.s_kin, 16)
            sp.wait_ge(s_one3, 1)
            sp.dma_start(shared.KS[96:99, :, :, :].rearrange("j b h t -> j b (h t)"), one3[:, :].unsqueeze(1).broadcast_to([3, NB, 8 * T])).then_inc(shared.s_kin, 16)
            sp.wait_ge(s_z, 1)
            per = N_TILES // 6
            for j, rows in [(j, shared.XG) for j in range(6)] + [(4, shared.YD), (5, shared.YD)]:
                sp.dma_start(rows[P * per * j:P * per * (j + 1), :].rearrange("(p t) d -> p t d", p=P), zeros[:, :].unsqueeze(1).broadcast_to([P, per, T])).then_inc(shared.s_zeroed, 16)

        @block.gpsimd
        def _(pool):
            n = [0]

            def link(ins):
                n[0] += 1
                ins.then_inc(s_pl, 1)
                pool.wait_ge(s_pl, n[0])

            pool.memset(one3[:, :], 1.0).then_inc(s_one3, 1)
            pool.wait_ge(s_one3, 1)
            pool.memset(zeros[:, :], 0.0).then_inc(s_z, 1)
            pool.wait_ge(s_z, 1)
            for l in range(L):
                link(pool.memset(lp1[:, l, :], float(l + 1)))
            link(pool.memset(XT[:, :, 0, :], 0.0))
            pool.memset(half[:, :], -0.5).then_inc(s_lp, 1)
            pool.wait_ge(s_lp, 1)
            pool.wait_ge(s_mv, 1)
            pool.tensor_tensor(rstd[:, :], vare[:, :], half[:, 0:L], ALU.pow).then_inc(s_rstd, 1)

            pool.wait_ge(s_tg, 16)

            def rot_k(g):
                pool.wait_ge(s_kv, 4 * (g + 1))
                ls = slice(4 * g, 4 * g + 4)
                k = KV[:, ls, 0:P]
                cos = trig[:, 0, ls, :].unsqueeze(2).broadcast_to([P, 4, 2 * H, 4])
                sin = trig[:, 1, ls, :].unsqueeze(2).broadcast_to([P, 4, H, 4])
                nsin = trig[:, 2, ls, :].unsqueeze(2).broadcast_to([P, 4, H, 4])
                k5 = k.rearrange("p l (h e f) -> p l h e f", e=2, f=4)
                t5 = r2k[:, :, :].rearrange("p l (h e f) -> p l h e f", e=2, f=4)
                pool.tensor_tensor(r1k[:, :, :].rearrange("p l (h f) -> p l h f", f=4), k.rearrange("p l (h f) -> p l h f", f=4), cos, ALU.mult)
                pool.tensor_tensor(t5[:, :, :, 0, :], k5[:, :, :, 1, :], nsin, ALU.mult)
                link(pool.tensor_tensor(t5[:, :, :, 1, :], k5[:, :, :, 0, :], sin, ALU.mult))
                pool.tensor_tensor(KR[:, ls, :], r1k[:, :, :], r2k[:, :, :], ALU.add).then_inc(s_kr, 1)
                pool.wait_ge(s_kr, g + 1)

            def prod_qk(l):
                pool.wait_ge(s_qr, l // 4 + 1)
                if l >= 2:
                    pool.wait_ge(s_red, l - 1)
                pool.tensor_tensor(prod[:, l % 2, 0:(l + 1) * P].rearrange("p (m x) -> p m x", m=l + 1),
                                   QR[:, l, :].unsqueeze(1).broadcast_to([P, l + 1, P]), KR[:, 0:l + 1, :], ALU.mult).then_inc(s_pr, 1)

            def gate(g):
                pool.wait_ge(s_ve, g + 1)
                pool.tensor_tensor(vr[:, :], ve[:, :], half[:, 0:4 * H], ALU.pow).then_inc(s_vr, 1)
                if g:
                    pool.wait_ge(s_on, g)
                pool.tensor_tensor(og[:, :, :], O[:, 4 * g:4 * g + 4, :], G[:, 4 * g:4 * g + 4, :], ALU.mult).then_inc(s_og, 1)

            rot_k(0)
            for l in range(4):
                prod_qk(l)
            rot_k(1)
            for l in range(4, 8):
                prod_qk(l)
                if l == 6:
                    gate(0)
            gate(1)

        @block.scalar
        def _(act):
            for g in range(NG + 1):
                if g < NG:
                    act.wait_ge(s_t, g + 1)
                    for c in range(2):
                        last = nc.scalar.copy(XT[:, c, 1 + 2 * g:3 + 2 * g, :], PS[c][:, 0:256].rearrange("p (l b) -> p l b", l=2))
                    last.then_inc(s_xt, 1)
                    act.wait_ge(s_y, g + 1)
                    if g >= 2:
                        act.wait_ge(s_p, 2 * (g - 1))
                    nc.scalar.activation(xc[:, g % 2, :, :, :], y[:, :, :, :], ACT.Silu).then_inc(s_xc, 1)
                if g > 0:
                    for l in (2 * g - 2, 2 * g - 1):
                        act.wait_ge(s_p, l + 1)
                        bank = PS[2 + 2 * (l % 2)]
                        nc.scalar.activation(Q[:, l, :], bank[:, 0:P], ACT.Silu)
                        nc.scalar.activation(G[:, l, :], bank[:, P:P + T], ACT.Silu)
                        nc.scalar.copy(D[:, l, :], bank[:, 384:400]).then_inc(s_qgd, 1)
            act.wait_ge(s_abs, 1)
            nc.scalar.activation(sg[:, :, :], absd[:, :, :], ACT.Sigmoid).then_inc(s_sg, 1)
            for g in range(2):
                act.wait_ge(s_O, 4 * (g + 1))
                if g:
                    act.wait_ge(s_ve, g)
                nc.scalar.activation(sq[:, :, :], O[:, 4 * g:4 * g + 4, :], ACT.Square).then_inc(s_sq, 1)
                for j in range(4):
                    l = 4 * g + j
                    act.wait_ge(s_ot, l + 1)
                    if l >= 2:
                        act.wait_ge(s_y2, l - 1)
                    nc.scalar.copy(oT[:, l % 2, 0:T], PS[l % 2][:, 0:T]).then_inc(s_ots, 1)

        @block.vector
        def _(dve):
            n = [0]

            def link(ins):
                n[0] += 1
                ins.then_inc(s_dv, 1)
                dve.wait_ge(s_dv, n[0])

            for b in range(L):
                last = nc.vector.bn_stats(stats[:, b, :], X[:, b, :])
            link(last)
            for b in range(L):
                last = nc.vector.bn_aggr(mv[:, b, :], stats[:, b, :])
            link(last)
            nc.vector.tensor_scalar(vare[:, :], mv[:, :, 1], EPS, None, ALU.add).then_inc(s_mv, 1)
            dve.wait_ge(s_rw, 16)
            link(nc.vector.tensor_tensor(rwd[:, :, :], rws[:, :, :, 1], rws[:, :, :, 0], ALU.subtract))
            dve.wait_ge(s_w, 32)
            wv = wb[:, :, P:384]
            link(nc.vector.tensor_tensor(wtmp[:, :, :], wv, rwd[:, :, :].rearrange("p h d -> p (h d)").unsqueeze(1).broadcast_to([P, 2, T]), ALU.mult))
            for c in range(2):
                nc.vector.reduce_sum(wa[:, c, 384:400], wtmp[:, c, :].rearrange("p (h d) -> p h d", h=H), X_AXIS)
                last = nc.vector.reduce_sum(wmean[:, c, :], wb[:, c, P:384].rearrange("p (h d) -> p h d", h=H), X_AXIS)
            link(last)
            for c in range(2):
                v = wb[:, c, P:384].rearrange("p (h d) -> p h d", h=H)
                last = nc.vector.scalar_tensor_tensor(v, wmean[:, c, :].unsqueeze(2).broadcast_to([P, H, DV]), -1.0 / DV, v, ALU.mult, ALU.add)
            last.then_inc(s_wd, 1)
            dve.wait_ge(s_rstd, 1)
            dve.wait_ge(s_cw, 16)

            def norm(g):
                if g >= 2:
                    dve.wait_ge(s_t, g - 1)
                for j in range(2):
                    l = 2 * g + j
                    last = nc.vector.tensor_scalar(xn[:, g % 2, j, :], X[:, l, :], mv[:, l, 0:1], rstd[:, l:l + 1], ALU.subtract, ALU.mult)
                last.then_inc(s_xn, 1)

            def conv(g):
                dve.wait_ge(s_xt, g + 1)
                if g:
                    dve.wait_ge(s_xc, g)
                for c in range(2):
                    last = nc.vector.tensor_scalar(tmp[:, c, :, :], XT[:, c, 1 + 2 * g:3 + 2 * g, :], cw[:, c, 1:2], None, ALU.mult)
                link(last)
                for c in range(2):
                    last = nc.vector.scalar_tensor_tensor(y[:, c, :, :], XT[:, c, 2 * g:2 * g + 2, :], cw[:, c, 0:1], tmp[:, c, :, :], ALU.mult, ALU.add)
                last.then_inc(s_y, 1)

            def take_kv(l):
                dve.wait_ge(s_p, l + 1)
                nc.vector.tensor_copy(KV[:, l, :], PS[3 + 2 * (l % 2)][:, 0:384]).then_inc(s_kv, 1)

            norm(0)
            norm(1)
            for g in range(NG + 1):
                if g < NG:
                    conv(g)
                    if g + 2 < NG:
                        norm(g + 2)
                if g > 0:
                    take_kv(2 * g - 2)
                    take_kv(2 * g - 1)

            dve.wait_ge(s_tg, 16)
            for g in range(2):
                ls = slice(4 * g, 4 * g + 4)
                dve.wait_ge(s_qgd, 4 * (g + 1))
                q = Q[:, ls, :]
                cos = trig[:, 0, ls, :].unsqueeze(2).broadcast_to([P, 4, 2 * H, 4])
                sin = trig[:, 1, ls, :].unsqueeze(2).broadcast_to([P, 4, H, 4])
                nsin = trig[:, 2, ls, :].unsqueeze(2).broadcast_to([P, 4, H, 4])
                q5 = q.rearrange("p l (h e f) -> p l h e f", e=2, f=4)
                t5 = r2[:, :, :].rearrange("p l (h e f) -> p l h e f", e=2, f=4)
                nc.vector.tensor_tensor(r1[:, :, :].rearrange("p l (h f) -> p l h f", f=4), q.rearrange("p l (h f) -> p l h f", f=4), cos, ALU.mult)
                nc.vector.tensor_tensor(t5[:, :, :, 0, :], q5[:, :, :, 1, :], nsin, ALU.mult)
                link(nc.vector.tensor_tensor(t5[:, :, :, 1, :], q5[:, :, :, 0, :], sin, ALU.mult))
                nc.vector.tensor_tensor(QR[:, ls, :], r1[:, :, :], r2[:, :, :], ALU.add).then_inc(s_qr, 1)
                dve.wait_ge(s_qr, g + 1)

            nc.vector.scalar_tensor_tensor(absd[:, :, :], D[:, :, :], -1.0, D[:, :, :], ALU.mult, ALU.max).then_inc(s_abs, 1)
            link(nc.vector.tensor_scalar(ind[:, :, :], D[:, :, :], 0.0, None, ALU.is_gt))
            link(nc.vector.tensor_copy(cum[:, 0, :], ind[:, 0, :]))
            for l in range(1, L):
                link(nc.vector.tensor_tensor(cum[:, l, :], cum[:, l - 1, :], ind[:, l, :], ALU.add))
            dve.wait_ge(s_lp, 1)
            link(nc.vector.tensor_tensor(ca[:, :, :], lp1[:, :, :], cum[:, :, :], ALU.subtract))
            link(nc.vector.tensor_tensor(cb[:, :, :], cum[:, :, :], ca[:, :, :], ALU.subtract))
            link(nc.vector.tensor_tensor(cc[:, :, :], cb[:, :, :], ind[:, :, :], ALU.mult))
            link(nc.vector.tensor_tensor(cd[:, :, :], cc[:, :, :], ca[:, :, :], ALU.add))
            link(nc.vector.reciprocal(cb[:, :, :], cd[:, :, :]))
            dve.wait_ge(s_sg, 1)
            nc.vector.scalar_tensor_tensor(cf[:, :, :], sg[:, :, :], float(DK) ** -0.5, cb[:, :, :], ALU.mult, ALU.mult)
            link(nc.vector.tensor_tensor(same[:, :, :, :], ind[:, :, :].unsqueeze(2).broadcast_to([P, L, L, H]),
                                         ind[:, :, :].unsqueeze(1).broadcast_to([P, L, L, H]), ALU.is_equal))
            link(nc.vector.tensor_tensor(AC[:, :, :, :], same[:, :, :, :], cf[:, :, :].unsqueeze(2).broadcast_to([P, L, L, H]), ALU.mult))

            def attend(l):
                s = l % 2
                m = l + 1
                dve.wait_ge(s_pr, l + 1)
                nc.vector.reduce_sum(S[:, s, 0:m * H], prod[:, s, 0:m * P].rearrange("p (x d) -> p x d", d=DK), X_AXIS).then_inc(s_red, 1)
                dve.wait_ge(s_red, l + 1)
                link(nc.vector.tensor_tensor(S2[:, s, 0:m * H], S[:, s, 0:m * H], AC[:, l, 0:m, :].rearrange("p m h -> p (m h)"), ALU.mult))
                link(nc.vector.tensor_tensor(W[:, s, 0:m * T].rearrange("p (m h d) -> p m h d", m=m, h=H),
                                             S2[:, s, 0:m * H].rearrange("p (m h) -> p m h", m=m).unsqueeze(3).broadcast_to([P, m, H, DV]),
                                             KV[:, 0:m, P:384].rearrange("p m (h d) -> p m h d", h=H), ALU.mult))
                nc.vector.reduce_sum(O[:, l, :], W[:, s, 0:m * T].rearrange("p (m x) -> p x m", m=m), X_AXIS).then_inc(s_O, 1)

            def head_norm(g):
                dve.wait_ge(s_sq, g + 1)
                if g:
                    dve.wait_ge(s_vr, g)
                link(nc.vector.reduce_sum(vs[:, :], sq[:, :, :].rearrange("p l (h d) -> p (l h) d", h=H), X_AXIS))
                nc.vector.tensor_scalar(ve[:, :], vs[:, :], 1.0 / DV, EPS, ALU.mult, ALU.add).then_inc(s_ve, 1)

            def scale(g):
                dve.wait_ge(s_vr, g + 1)
                dve.wait_ge(s_og, g + 1)
                nc.vector.tensor_tensor(on[:, g, :, :].rearrange("p l (h d) -> p (l h) d", h=H), og[:, :, :].rearrange("p l (h d) -> p (l h) d", h=H),
                                        vr[:, :].unsqueeze(2).broadcast_to([P, 4 * H, DV]), ALU.mult).then_inc(s_on, 1)

            def residual(l):
                dve.wait_ge(s_y2, l + 1)
                nc.vector.tensor_tensor(X[:, l, :], PS[2 + l % 2][:, 0:T], X[:, l, :], ALU.add).then_inc(s_x2, 1)

            for l in range(4):
                attend(l)
            attend(4)
            head_norm(0)
            attend(5)
            attend(6)
            scale(0)
            attend(7)
            for l in range(4):
                residual(l)
            head_norm(1)
            scale(1)
            for l in range(4, 8):
                residual(l)

        @block.tensor
        def _(pe):
            def transposes(g):
                pe.wait_ge(s_xn, g + 1)
                if g:
                    pe.wait_ge(s_xt, g)
                for c in range(2):
                    for j in range(2):
                        last = nc.tensor.transpose(PS[c][:, j * P:(j + 1) * P], xn[:, g % 2, j, c * P:(c + 1) * P], ident[:, :])
                last.then_inc(s_t, 1)

            transposes(0)
            for g in range(NG):
                if g + 1 < NG:
                    transposes(g + 1)
                pe.wait_ge(s_xc, g + 1)
                if g == 0:
                    pe.wait_ge(s_wd, 1)
                for j in range(2):
                    l = 2 * g + j
                    if l >= 2:
                        pe.wait_ge(s_qgd, l - 1)
                        pe.wait_ge(s_kv, l - 1)
                    for c in range(2):
                        nc.tensor.matmul(PS[2 + 2 * j][:, 0:400], xc[:, g % 2, c, j, :], wa[:, c, :], start=(c == 0), stop=(c == 1))
                    for c in range(2):
                        last = nc.tensor.matmul(PS[3 + 2 * j][:, 0:384], xc[:, g % 2, c, j, :], wb[:, c, :], start=(c == 0), stop=(c == 1))
                    last.then_inc(s_p, 1)
            pe.wait_ge(s_wo, 16)
            pe.wait_ge(s_qgd, L)
            pe.wait_ge(s_kv, L)
            for l in range(L):
                pe.wait_ge(s_on, l // 4 + 1)
                if l >= 2:
                    pe.wait_ge(s_ots, l - 1)
                for c in range(2):
                    last = nc.tensor.transpose(PS[l % 2][:, c * P:(c + 1) * P], on[:, l // 4, l % 4, c * P:(c + 1) * P], ident[:, :])
                last.then_inc(s_ot, 1)
                pe.wait_ge(s_ots, l + 1)
                if l >= 2:
                    pe.wait_ge(s_x2, l - 1)
                for c in range(2):
                    last = nc.tensor.matmul(PS[2 + l % 2][:, 0:T], oT[:, l % 2, c * P:(c + 1) * P], wo[:, c, :], start=(c == 0), stop=(c == 1))
                last.then_inc(s_y2, 1)


def stage_c(nc, shared, gamma):
    stack = ExitStack()
    with stack:
        def sb(name, shape, dt=F32):
            return stack.enter_context(nc.sbuf_tensor(name, shape, dt))

        sem = shared.sem
        X, C, ident, half = shared.X, shared.C, shared.ident, shared.half
        H, D = 8, 16
        NC = T // P
        ROWS = 6 * D
        GROUPS = ((0, 2), (2, NB))

        gam = sb("c_gamma", [P, 1])
        stats = sb("c_stats", [P, NB, 6])
        mv = sb("c_mv", [P, NB, 2])
        vare = sb("c_vare", [P, NB])
        rstd = sb("c_rstd", [P, NB])
        KS = shared.KS
        VZ = sb("c_VZ", [P, NB, NC, 2, 4, 32])
        OZ = sb("c_OZ", [P, 2, 32])
        xn = sb("c_xn", [P, NB, T])
        qr = sb("c_qr", [P, NB, T])
        qsp = [sb(f"c_qsp{g}", [P, 3, hi - lo, T], BF16) for g, (lo, hi) in enumerate(GROUPS)]
        QS = sb("c_QS", [P, NB, H, T], BF16)
        nm = sb("c_nm", [P, 2, H, NC])
        nmr = sb("c_nmr", [16, P])
        nmT = sb("c_nmT", [16, P])
        nms = sb("c_nms", [16, 2, 3, P], BF16)
        pT = sb("c_pT", [P, 2, NC, H, T])
        pvz = sb("c_pvz_sb", [P, 2, 2 * T])
        rinv = sb("c_rinv", [P, T])
        ret = sb("c_ret", [P, 2, T])

        md = nc.dram_tensor("max_parts", (NB, 16, 3, P), BF16, kind="Internal").ap()
        qd = [nc.dram_tensor(f"q_parts{g}", (D, 3, hi - lo, H, T), BF16, kind="Internal").ap() for g, (lo, hi) in enumerate(GROUPS)]

        PM = [stack.enter_context(nc.psum_tensor(f"c_pm{i}", [P, 512], F32)) for i in range(2)]
        PE2 = [stack.enter_context(nc.psum_tensor(f"c_pe{i}", [P, 1024], F32)) for i in range(2)]
        PVZ = stack.enter_context(nc.psum_tensor("c_pvz", [P, 512], F32))
        PT = stack.enter_context(nc.psum_tensor("c_pt", [P, 512], F32))
        PV, PZ = PVZ[:, 0:T], PVZ[:, T:2 * T]

        s_gam, s_one = sem("c_gamma_in"), sem("c_ones")
        s_mv, s_rstd, s_q = sem("c_mv"), sem("c_rstd"), sem("c_q_split")
        s_qd = [sem(f"c_q_stored{j}") for j in range(2)]
        s_qin = [sem(f"c_q_loaded{j}") for j in range(2)]
        s_vt, s_vz = sem("c_v_transposed"), sem("c_v_sb")
        s_m1, s_mx, s_mt, s_ms = sem("c_scores"), sem("c_max"), sem("c_maxT"), sem("c_max_split")
        s_md, s_mtc, s_min = sem("c_max_stored"), sem("c_maxT_sb"), sem("c_max_loaded")
        s_s2, s_ex, s_pv, s_pvc, s_ret, s_x3 = sem("c_scoresT"), sem("c_exp"), sem("c_pv_done"), sem("c_pvz_copied"), sem("c_ret"), sem("c_x3")
        s_dv, s_pl = sem("c_dve_chain"), sem("c_pool_chain")

        def parts_of_q(eng, g):
            lo, hi = GROUPS[g]
            eng.wait_ge(s_q, g + 1)
            for h in range(H):
                eng.dma_start(qd[g][:, :, :, h, :].rearrange("d j b t -> d (j b) t"), qsp[g][D * h:D * (h + 1), :, :, :].rearrange("p j b t -> p (j b) t")).then_inc(s_qd[g], 16)
            eng.wait_ge(s_qd[g], 16 * H)
            for j, part in enumerate(QPART):
                eng.dma_start(QS[D * j:D * (j + 1), lo:hi, :, :], qd[g][:, part, :, :, :]).then_inc(s_qin[g], 16)

        def sources_left(eng):
            eng.wait_ge(shared.s_kin, 16 * 7)
            eng.wait_ge(shared.s_zeroed, 16 * shared.n_zero_dmas)

        block = stack.enter_context(nc.Block())

        @block.sync
        def _(sp):
            parts_of_q(sp, 0)
            for b in range(NB):
                sp.wait_ge(s_ms, b + 1)
                sp.dma_start(md[b], nms[:, b % 2, :, :]).then_inc(s_md, 16)
                sp.wait_ge(s_md, 16 * (b + 1))
                sp.dma_start(QS[ROWS:ROWS + 3, b, :, :].rearrange("j h (c q) -> j (h c) q", c=NC), md[b].rearrange("r j q -> j r q")).then_inc(s_min, 16)
                sp.wait_ge(s_min, 16 * (b + 1))

        @block.gpsimd
        def _(pool):
            n = [0]

            def link(ins):
                n[0] += 1
                ins.then_inc(s_pl, 1)
                pool.wait_ge(s_pl, n[0])

            sources_left(pool)
            pool.dma_start(gam[:, :], gamma.partition_broadcast(P)).then_inc(s_gam, 16)
            link(pool.memset(OZ[:, :, :], 0.0))
            link(pool.memset(OZ[:, 0, 0:D], 1.0))
            pool.memset(OZ[:, 1, D:2 * D], 1.0).then_inc(s_one, 1)
            pool.wait_ge(s_mv, 1)
            pool.tensor_tensor(rstd[:, :], vare[:, :], half[:, 0:NB], ALU.pow).then_inc(s_rstd, 1)
            pool.memset(VZ[:, :, :, :, :, :], 0.0).then_inc(s_one, 1)
            for b in range(NB):
                pool.wait_ge(s_ret, b + 1)
                pool.tensor_tensor(X[:, b, :], ret[:, b % 2, :], X[:, b, :], ALU.add).then_inc(s_x3, 1)

        @block.scalar
        def _(act):
            parts_of_q(act, 1)

            def take_values(b):
                act.wait_ge(s_pv, b + 1)
                if b >= 2:
                    act.wait_ge(s_ret, b - 1)
                nc.scalar.copy(pvz[:, b % 2, :], PVZ[:, :]).then_inc(s_pvc, 1)

            for b in range(NB):
                for u in range(4):
                    act.wait_ge(s_s2, 4 * b + u + 1)
                    if b >= 2 and u == 0:
                        act.wait_ge(s_pv, b - 1)
                    nc.scalar.activation(pT[:, b % 2, u // 2, 4 * (u % 2):4 * (u % 2) + 4, :], PE2[u % 2][:, :].rearrange("p (h q) -> p h q", h=4),
                                         ACT.Exp, scale=D ** -0.5).then_inc(s_ex, 1)
                if b:
                    take_values(b - 1)
            take_values(NB - 1)

        @block.vector
        def _(dve):
            n = [0]

            def link(ins):
                n[0] += 1
                ins.then_inc(s_dv, 1)
                dve.wait_ge(s_dv, n[0])

            sources_left(dve)
            for b in range(NB):
                last = nc.vector.bn_stats(stats[:, b, :], X[:, b, :])
            link(last)
            for b in range(NB):
                last = nc.vector.bn_aggr(mv[:, b, :], stats[:, b, :])
            link(last)
            nc.vector.tensor_scalar(vare[:, :], mv[:, :, 1], EPS, None, ALU.add).then_inc(s_mv, 1)
            dve.wait_ge(s_rstd, 1)
            for g, (lo, hi) in enumerate(GROUPS):
                for b in range(lo, hi):
                    last = nc.vector.tensor_scalar(xn[:, b, :], X[:, b, :], mv[:, b, 0:1], rstd[:, b:b + 1], ALU.subtract, ALU.mult)
                link(last)
                link(nc.vector.tensor_copy(qsp[g][:, 0, :, :], xn[:, lo:hi, :]))
                link(nc.vector.tensor_tensor(qr[:, lo:hi, :], xn[:, lo:hi, :], qsp[g][:, 0, :, :], ALU.subtract))
                link(nc.vector.tensor_copy(qsp[g][:, 1, :, :], qr[:, lo:hi, :]))
                nc.vector.tensor_tensor(qsp[g][:, 2, :, :], qr[:, lo:hi, :], qsp[g][:, 1, :, :], ALU.subtract).then_inc(s_q, 1)

            def maxima(b, h):
                dve.wait_ge(s_m1, H * b + h + 1)
                if b >= 2 and h == 0:
                    dve.wait_ge(s_mt, b - 1)
                nc.vector.tensor_reduce(nm[:, b % 2, h, :], PM[h % 2][:, :].rearrange("p (c l) -> p c l", c=NC), X_AXIS, ALU.max, negate=True).then_inc(s_mx, 1)

            def split_max(b):
                dve.wait_ge(s_mt, b + 1)
                if b >= 2:
                    dve.wait_ge(s_md, 16 * (b - 1))
                nc.vector.tensor_copy(nmT[:, :], PT[0:16, 0:P]).then_inc(s_mtc, 1)
                dve.wait_ge(s_mtc, b + 1)
                link(nc.vector.tensor_copy(nms[:, b % 2, 0, :], nmT[:, :]))
                link(nc.vector.tensor_tensor(nmr[:, :], nmT[:, :], nms[:, b % 2, 0, :], ALU.subtract))
                link(nc.vector.tensor_copy(nms[:, b % 2, 1, :], nmr[:, :]))
                nc.vector.tensor_tensor(nms[:, b % 2, 2, :], nmr[:, :], nms[:, b % 2, 1, :], ALU.subtract).then_inc(s_ms, 1)
                dve.wait_ge(s_ms, b + 1)

            def finish(b):
                dve.wait_ge(s_pvc, b + 1)
                link(nc.vector.reciprocal(rinv[:, :], pvz[:, b % 2, T:2 * T]))
                if b >= 2:
                    dve.wait_ge(s_x3, b - 1)
                nc.vector.scalar_tensor_tensor(ret[:, b % 2, :], pvz[:, b % 2, 0:T], gam[:, :], rinv[:, :], ALU.mult, ALU.mult).then_inc(s_ret, 1)
                dve.wait_ge(s_ret, b + 1)

            dve.wait_ge(s_one, 2)
            for b in range(NB):
                dve.wait_ge(s_vt, b + 1)
                for a in range(2):
                    last = nc.vector.tensor_copy(VZ[:, b, :, a, :, D * a:D * (a + 1)],
                                                 PM[b % 2][:, 0:T].rearrange("p (c i n) -> p c i n", c=NC, i=4)[:, :, :, D * a:D * (a + 1)])
                last.then_inc(s_vz, 1)
            for h in range(H):
                maxima(0, h)
            split_max(0)
            for h in range(H):
                maxima(1, h)
            dve.wait_ge(s_gam, 16)
            for b in range(NB):
                if b >= 2:
                    finish(b - 2)
                if b + 2 < NB:
                    maxima(b + 2, 0)
                    maxima(b + 2, 1)
                if b + 1 < NB:
                    split_max(b + 1)
                if b + 2 < NB:
                    for h in range(2, H):
                        maxima(b + 2, h)
            finish(NB - 2)
            finish(NB - 1)

        @block.tensor
        def _(pe):
            for b in range(NB):
                if b >= 2:
                    pe.wait_ge(s_vz, b - 1)
                for c in range(NC):
                    last = nc.tensor.transpose(PM[b % 2][:, c * P:(c + 1) * P], C[:, b, c * P:(c + 1) * P], ident[:, :])
                last.then_inc(s_vt, 1)
            pe.wait_ge(s_vz, NB)
            pe.wait_ge(shared.s_kin, 16 * 7)
            pe.wait_ge(s_one, 2)

            def scores(b, h):
                if h == 0 and b in (0, GROUPS[1][0]):
                    pe.wait_ge(s_qin[0 if b == 0 else 1], 16 * 6)
                if H * b + h >= 2:
                    pe.wait_ge(s_mx, H * b + h - 1)
                for c in range(NC):
                    last = nc.tensor.matmul(PM[h % 2][:, c * T:(c + 1) * T], QS[0:ROWS, b, h, c * P:(c + 1) * P], KS[0:ROWS, b, h, :], start=True, stop=True)
                last.then_inc(s_m1, 1)

            def max_rows(b):
                pe.wait_ge(s_mx, H * (b + 1))
                if b:
                    pe.wait_ge(s_mtc, b)
                nc.tensor.transpose(PT[0:16, 0:P], nm[:, b % 2, :, :].rearrange("p h c -> p (h c)"), ident[:, :]).then_inc(s_mt, 1)

            def scores_t(b, u):
                c, h0 = u // 2, 4 * (u % 2)
                if u == 0:
                    pe.wait_ge(s_min, 16 * (b + 1))
                if 4 * b + u >= 2:
                    pe.wait_ge(s_ex, 4 * b + u - 1)
                for k in range(4):
                    last = nc.tensor.matmul(PE2[u % 2][:, k * T:(k + 1) * T], KS[0:ROWS + 3, b, h0 + k, c * P:(c + 1) * P], QS[0:ROWS + 3, b, h0 + k, :], start=True, stop=True)
                last.then_inc(s_s2, 1)

            def values(b, u):
                c, a = u // 2, u % 2
                if u == 0:
                    pe.wait_ge(s_ex, 4 * (b + 1))
                    if b:
                        pe.wait_ge(s_pvc, b)
                for out_, w in ((PV, VZ[:, b, c, a, :, :]), (PZ, None)):
                    for i in range(4):
                        last = nc.tensor.matmul(out_[32 * i:32 * i + 32, :], OZ[:, a, :] if w is None else w[:, i, :], pT[:, b % 2, c, 2 * i + a, :],
                                                start=(u == 0 and w is not None), stop=(u == 3 and w is None))
                if u == 3:
                    last.then_inc(s_pv, 1)

            for h in range(H):
                scores(0, h)
            max_rows(0)
            for h in range(H):
                scores(1, h)
            for b in range(NB + 1):
                for u in range(4):
                    if b < NB:
                        scores_t(b, u)
                    if b + 2 < NB:
                        scores(b + 2, 2 * u)
                        scores(b + 2, 2 * u + 1)
                    if u == 0 and b + 1 < NB:
                        max_rows(b + 1)
                    if b:
                        values(b - 1, u)


def stage_d(nc, shared, w_router, router_bias, w_gate, w_up, w_down, out):
    stack = ExitStack()
    with stack:
        def sb(name, shape, dt=F32):
            return stack.enter_context(nc.sbuf_tensor(name, shape, dt))

        sem = shared.sem
        X, ident, half, XG = shared.X, shared.ident, shared.half, shared.XG
        E, F, K = N_EXPERT, 64, 4
        I32, U32 = mybir.dt.int32, mybir.dt.uint32
        FW = w_gate.shape[1]
        NG = E // 4
        NOG = OVER_TILES // 4
        NSH = (FW - E * F) // P
        NPAIR = NB * K

        WG = sb("d_WG", [P, 2, FW])
        WU = sb("d_WU", [P, 2, FW])
        WD = sb("d_WD", [P, FW // P, T])
        wr = sb("d_wr", [P, 2, E])
        bias = sb("d_bias", [P, E])
        iota = sb("d_iota", [P, E])
        iotai = sb("d_iotai", [P, E], I32)
        base_a = sb("d_base_a", [P, E])
        base_ba = sb("d_base_ba", [P, E])
        steps = sb("d_steps", [P, 7])
        tiles_row = sb("d_tiles_row", [1, OVER_TILES])
        tril = sb("d_tril", [P, P], BF16)
        ones = sb("d_ones", [P, P], BF16)
        zero_row = sb("d_zero_row", [P, E])
        stats = sb("d_stats", [P, NB, 6])
        mv = sb("d_mv", [P, NB, 2])
        vare = sb("d_vare", [P, NB])
        rstd = sb("d_rstd", [P, NB])
        XN = sb("d_XN", [P, NB, T])
        XT = sb("d_XT", [P, 2, NB, P])
        lg = sb("d_lg", [P, NB, E])
        lb = sb("d_lb", [P, NB, E])
        top = sb("d_top", [P, NB, 8])
        topi = sb("d_topi", [P, NB, 8], U32)
        topf = sb("d_topf", [P, NB, 8])
        oh = sb("d_oh", [P, NB, K, E], BF16)
        mask = sb("d_mask", [P, NB, E], BF16)
        nmx = sb("d_nmx", [P, NB])
        cnt = sb("d_cnt", [P, E])
        cmp7 = sb("d_cmp7", [P, 7, E])
        over = sb("d_over", [P, E])
        pref = sb("d_pref", [P, E])
        expf = sb("d_expf", [P, E])
        dba = sb("d_dba", [P, E])
        slot = sb("d_slot", [P, NB, E])
        scr = sb("d_scr", [P, NB, K, E])
        slotk = sb("d_slotk", [P, NPAIR])
        slots = sb("d_slots", [P, NPAIR], U32)
        wk = sb("d_wk", [P, NB, K])
        den = sb("d_den", [P, NB])
        rden = sb("d_rden", [P, NB])
        wt = sb("d_wt", [P, NB, K])
        eid = sb("d_eid", [1, OVER_TILES + 1])
        eidi = sb("d_eidi", [1, OVER_TILES + 1], I32)
        sgs = sb("d_sgs", [P, 2, 512])
        hs = sb("d_hs", [P, NSH, 512])
        xg = sb("d_xg", [P, 3, 4, T])
        xgT = sb("d_xgT", [P, 2, 2, 4, P])
        sg = sb("d_sg", [P, 2, 2 * P])
        h = sb("d_h", [P, 2, 2 * P])
        wdo = sb("d_wdo", [P, 2, T])
        ysb = XT[:, :, :, :].rearrange("p c (t u) n -> p c t (u n)", u=2)
        xgo = hs[:, 0:2, :].rearrange("p a (b t) -> p (a b) t", t=T)
        yso = hs[:, 2:4, :].rearrange("p a (b t) -> p (a b) t", t=T)
        wgo = sgs[:, 0, :].rearrange("p (c t f) -> p c t f", c=2, f=F)
        wuo = sgs[:, 1, :].rearrange("p (c t f) -> p c t f", c=2, f=F)
        YD = shared.YD

        PS = [stack.enter_context(nc.psum_tensor(f"d_ps{i}", [P, 512], F32)) for i in range(8)]
        PGATE, PUP, PY, PX = PS[0:2], PS[2:4], PS[4:6], PS[6:8]

        def sems(*names):
            return [sem("d_" + n) for n in names]

        s_w, s_wd, s_const, s_mv, s_rstd, s_xn = sems("w_in", "wd_in", "consts", "mv", "rstd", "xn")
        s_t, s_xt, s_r, s_mask, s_rank, s_slot = sems("xT_done", "xT_sb", "router", "mask", "rank", "slots")
        s_lgm, s_ex, s_wt, s_eid, s_sc = sems("lg_minus_max", "exp", "weights", "overflow_experts", "scattered")
        s_sgu, s_ssg, s_sh, s_sy, s_shx = sems("sh_gate_up", "sh_silu", "sh_hidden", "sh_down", "sh_added")
        s_xg = sems("xg_in0", "xg_in1", "xg_in2")
        s_xo, s_px, s_xea, s_xed, s_gu = sems("overflow_in", "xg_transposed", "xgT_act", "xgT_dve", "gate_up")
        s_sg, s_h, s_py, s_ya, s_yd = sems("silu", "hidden", "down", "y_act", "y_dve")
        s_yst = sems("y_stored0", "y_stored1")
        s_yso, = sems("y_overflow_stored")
        s_wsh, s_wgu = sems("shared_gu_in", "routed_gu_in")
        s_yg = sems("y_gathered0", "y_gathered1")
        s_x4, s_out, s_dv, s_pl = sems("x4", "out_stored", "dve_chain", "pool_chain")

        ROW0 = E * P
        wg_v = w_gate.rearrange("(c p) n -> p c n", p=P)
        wu_v = w_up.rearrange("(c p) n -> p c n", p=P)

        block = stack.enter_context(nc.Block())

        @block.sync
        def _(sp):
            sp.dma_start(wr[:, :, :], w_router.rearrange("(c p) n -> p c n", p=P)).then_inc(s_w, 16)
            sp.dma_start(bias[:, :], router_bias.partition_broadcast(P)).then_inc(s_w, 16)
            sp.dma_start(WD[:, E * F // P:, :], w_down[E * F:, :].rearrange("(c p) n -> p c n", p=P)).then_inc(s_w, 16)
            for q in range(4):
                n = E * F // P // 4
                sp.dma_start(WD[:, n * q:n * (q + 1), :], w_down[P * n * q:P * n * (q + 1), :].rearrange("(c p) n -> p c n", p=P)).then_inc(s_wd, 16)
            sp.wait_ge(s_sc, 16 * NPAIR)
            for g in range(NG):
                if g >= 3:
                    sp.wait_ge(s_px, g - 2)
                sp.dma_start(xg[:, g % 3, :, :], XG[512 * g:512 * (g + 1), :].rearrange("(t p) d -> p t d", p=P)).then_inc(s_xg[g % 3], 16)
            sp.wait_ge(s_eid, 1)

            def load_overflow(i, results_left=None):
                sp.dma_start(xgo[:, :, :], XG[bass.ds(ROW0 + i * 512, 512), :].rearrange("(t p) d -> p t d", p=P)).then_inc(s_xo, 16)
                for j in range(4):
                    e = sp.value_load(eidi[0:1, bass.ds(i * 4 + j, 1)], min_val=0, max_val=E - 1)
                    sp.dma_start(wgo[:, :, j, :], wg_v[:, :, bass.ds(e * F, F)]).then_inc(s_xo, 16)
                    if j == 3 and results_left is not None:
                        sp.wait_ge(s_yso, results_left)
                    sp.dma_start(wuo[:, :, j, :], wu_v[:, :, bass.ds(e * F, F)]).then_inc(s_xo, 16)
                    sp.dma_start(wdo[64 * (j % 2):64 * (j % 2) + 64, j // 2, :], w_down[bass.ds(e * F, F), :]).then_inc(s_xo, 16)

            load_overflow(0)
            n_over = sp.value_load(eidi[0:1, OVER_TILES:OVER_TILES + 1], min_val=0, max_val=OVER_TILES - 1)
            with sp.Fori(1, NOG) as i:
                with sp.If(i * 4 < n_over):
                    sp.wait_ge(s_py, i + NG)
                    load_overflow(i, i * 16)
            for b in range(NB):
                sp.wait_ge(s_x4, b + 1)
                sp.dma_start(out[b], X[:, b, :]).then_inc(s_out, 16)
            sp.wait_ge(s_out, 16 * NB)

        @block.gpsimd
        def _(pool):
            n = [0]

            def link(ins):
                n[0] += 1
                ins.then_inc(s_pl, 1)
                pool.wait_ge(s_pl, n[0])

            link(pool.iota(iotai[:, :], pattern=[[1, E]], base=0, channel_multiplier=0))
            link(pool.tensor_copy(iota[:, :], iotai[:, :]))
            link(pool.tensor_scalar(base_a[:, :], iota[:, :], float(P), 0.0, ALU.mult, ALU.add))
            link(pool.tensor_scalar(base_ba[:, :], iota[:, :], -float(P), float(P * (E - 1)), ALU.mult, ALU.add))
            link(pool.tensor_copy(tiles_row[:, :], iota[0:1, 0:OVER_TILES]))
            link(pool.tensor_scalar(steps[:, :], iota[:, 1:8], float(P), 0.0, ALU.mult, ALU.add))
            link(pool.memset(zero_row[:, :], 0.0))
            link(pool.memset(ones[:, :], 1.0))
            pool.affine_select(out=tril[:, :], in_=ones[:, :], compare_op=ALU.is_gt, fill=0.0, base=0,
                               pattern=[[1, P]], channel_multiplier=-1).then_inc(s_const, 1)
            pool.wait_ge(s_mv, 1)
            pool.tensor_tensor(rstd[:, :], vare[:, :], half[:, 0:NB], ALU.pow).then_inc(s_rstd, 1)
            pool.wait_ge(shared.s_zeroed, 16 * shared.n_zero_dmas)
            pool.wait_ge(s_xn, NB)
            for i in range(NPAIR):
                if i % (NPAIR // 2) == 0:
                    pool.wait_ge(s_slot, i // (NPAIR // 2) + 1)
                pool.indirect_dma_start(out=XG[:, :], out_offset=bass.IndirectOffsetOnAxis(ap=slots[:, i:i + 1], axis=0),
                                        in_=XN[:, i // K, :], in_offset=None).then_inc(s_sc, 16)
            for g in range(NG):
                pool.wait_ge(s_ya, g + 1)
                pool.wait_ge(s_yd, g + 1)
                pool.dma_start(YD[512 * g:512 * (g + 1), :].rearrange("(t p) d -> p t d", p=P), ysb[:, g % 2, :, :]).then_inc(s_yst[g % 2], 16)
            pool.wait_ge(s_eid, 1)
            n_over = pool.value_load(eidi[0:1, OVER_TILES:OVER_TILES + 1], min_val=0, max_val=OVER_TILES - 1)
            with pool.Fori(0, NOG) as i:
                with pool.If(i * 4 < n_over):
                    pool.wait_ge(s_ya, i + (NG + 1))
                    pool.wait_ge(s_yd, i + (NG + 1))
                    pool.dma_start(YD[bass.ds(ROW0 + i * 512, 512), :].rearrange("(t p) d -> p t d", p=P), yso[:, :, :]).then_inc(s_yso, 16)
                    pool.wait_ge(s_yso, i * 16 + 16)
            pool.wait_ge(s_yst[0], 16 * (NG // 2))
            pool.wait_ge(s_yst[1], 16 * (NG // 2))
            for i in range(NPAIR):
                b, k = i // K, i % K
                if k == 0 and b >= 2:
                    pool.wait_ge(s_x4, b - 1)
                if i == 0:
                    pool.wait_ge(s_px, NG)
                pool.indirect_dma_start(out=xg[:, b % 2, k, :], out_offset=None, in_=YD[:, :],
                                        in_offset=bass.IndirectOffsetOnAxis(ap=slots[:, i:i + 1], axis=0)).then_inc(s_yg[b % 2], 16)

        @block.scalar
        def _(act):
            act.dma_start(WG[:, :, E * F:], wg_v[:, :, E * F:]).then_inc(s_wsh, 16)
            act.dma_start(WU[:, :, E * F:], wu_v[:, :, E * F:]).then_inc(s_wsh, 16)
            for q in range(4):
                cols = slice(E * F // 4 * q, E * F // 4 * (q + 1))
                act.dma_start(WG[:, :, cols], wg_v[:, :, cols]).then_inc(s_wgu, 16)
                act.dma_start(WU[:, :, cols], wu_v[:, :, cols]).then_inc(s_wgu, 16)
            for b in range(NB):
                act.wait_ge(s_t, b + 1)
                nc.scalar.copy(XT[:, :, b, :], (PX[0] if b % 2 == 0 else PY[1])[:, 0:T].rearrange("p (c t) -> p c t", c=2)).then_inc(s_xt, 1)
            act.wait_ge(s_lgm, 1)
            nc.scalar.activation(lb[:, :, :], lb[:, :, :], ACT.Exp).then_inc(s_ex, 1)
            for n in range(2 * NSH):
                act.wait_ge(s_sgu, n + 1)
                if n >= 2:
                    act.wait_ge(s_sh, n - 1)
                nc.scalar.activation(sgs[:, n % 2, :], PGATE[n % 2][:, :], ACT.Silu).then_inc(s_ssg, 1)

            for g in range(NG + 1):
                if g < NG:
                    act.wait_ge(s_px, g + 1)
                    if g >= 2:
                        act.wait_ge(s_gu, g - 1)
                    nc.scalar.copy(xgT[:, g % 2, 0, :, :], PX[0][:, :].rearrange("p (t n) -> p t n", t=4)).then_inc(s_xea, 1)
                if g < NG:
                    act.wait_ge(s_gu, g + 1)
                    if g >= 2:
                        act.wait_ge(s_h, g - 1)
                    nc.scalar.activation(sg[:, g % 2, :], PGATE[g % 2][:, 0:2 * P], ACT.Silu).then_inc(s_sg, 1)
                if g:
                    m = g - 1
                    act.wait_ge(s_py, m + 1)
                    if m >= 2:
                        act.wait_ge(s_yst[m % 2], 16 * (m // 2))
                    nc.scalar.copy(ysb[:, m % 2, 0:4:2, :], PY[0][:, :].rearrange("p (t n) -> p t n", t=2)).then_inc(s_ya, 1)
            act.wait_ge(s_eid, 1)
            n_over = act.value_load(eidi[0:1, OVER_TILES:OVER_TILES + 1], min_val=0, max_val=OVER_TILES - 1)
            with act.Fori(0, NOG) as i:
                with act.If(i * 4 < n_over):
                    act.wait_ge(s_px, i + (NG + 1))
                    nc.scalar.copy(xgT[:, 0, 0, :, :], PX[0][:, :].rearrange("p (t n) -> p t n", t=4)).then_inc(s_xea, 1)
                    act.wait_ge(s_gu, i + (NG + 1))
                    nc.scalar.activation(sg[:, 0, :], PGATE[0][:, 0:2 * P], ACT.Silu).then_inc(s_sg, 1)
                    act.wait_ge(s_py, i + (NG + 1))
                    nc.scalar.copy(yso[:, 0:4:2, :], PY[0][:, :].rearrange("p (t n) -> p t n", t=2)).then_inc(s_ya, 1)

        @block.vector
        def _(dve):
            n = [0]

            def link(ins):
                n[0] += 1
                ins.then_inc(s_dv, 1)
                dve.wait_ge(s_dv, n[0])

            for b in range(NB):
                last = nc.vector.bn_stats(stats[:, b, :], X[:, b, :])
            link(last)
            for b in range(NB):
                last = nc.vector.bn_aggr(mv[:, b, :], stats[:, b, :])
            link(last)
            nc.vector.tensor_scalar(vare[:, :], mv[:, :, 1], EPS, None, ALU.add).then_inc(s_mv, 1)
            dve.wait_ge(s_rstd, 1)
            for b in range(NB):
                nc.vector.tensor_scalar(XN[:, b, :], X[:, b, :], mv[:, b, 0:1], rstd[:, b:b + 1], ALU.subtract, ALU.mult).then_inc(s_xn, 1)
            dve.wait_ge(s_w, 48)
            dve.wait_ge(s_r, 1)
            link(nc.vector.tensor_copy(lg[:, :, :], PX[1][:, :].rearrange("p (b e) -> p b e", b=NB)))
            link(nc.vector.tensor_tensor(lb[:, :, :], lg[:, :, :], bias[:, :].unsqueeze(1).broadcast_to([P, NB, E]), ALU.add))
            for b in range(NB):
                last = nc.vector.max(top[:, b, :], lb[:, b, :])
            link(last)
            for b in range(NB):
                last = nc.vector.max_index(topi[:, b, :], top[:, b, :], lb[:, b, :])
            link(last)
            link(nc.vector.tensor_copy(topf[:, :, :], topi[:, :, :]))
            dve.wait_ge(s_const, 1)
            link(nc.vector.tensor_tensor(oh[:, :, :, :], iota[:, :].unsqueeze(1).unsqueeze(1).broadcast_to([P, NB, K, E]),
                                         topf[:, :, 0:K].unsqueeze(3).broadcast_to([P, NB, K, E]), ALU.is_equal))
            with nc.allow_low_precision(reason="counts of 0 and 1"):
                nc.vector.reduce_sum(mask[:, :, :], oh[:, :, :, :].rearrange("p b k e -> p b e k"), X_AXIS).then_inc(s_mask, 1)
            link(nc.vector.tensor_reduce(nmx[:, :], lg[:, :, :], X_AXIS, ALU.max, negate=True))
            nc.vector.tensor_tensor(lb[:, :, :], lg[:, :, :], nmx[:, :].unsqueeze(2).broadcast_to([P, NB, E]), ALU.add).then_inc(s_lgm, 1)
            dve.wait_ge(s_rank, 1)
            link(nc.vector.tensor_copy(cnt[:, :], PX[0][:, 0:E]))
            link(nc.vector.tensor_tensor(cmp7[:, :, :], cnt[:, :].unsqueeze(1).broadcast_to([P, 7, E]), steps[:, :].unsqueeze(2).broadcast_to([P, 7, E]), ALU.is_gt))
            link(nc.vector.reduce_sum(over[:, :], cmp7[:, :, :].rearrange("p j e -> p e j"), X_AXIS))
            link(nc.vector.tensor_tensor_scan(pref[:, :], over[:, :], zero_row[:, :], 0.0, ALU.add, ALU.add))
            link(nc.vector.tensor_tensor(expf[:, :], pref[:, :], over[:, :], ALU.subtract))
            link(nc.vector.scalar_tensor_tensor(dba[:, :], expf[:, :], float(P), base_ba[:, :], ALU.mult, ALU.add))
            ge = scr[:, 0:2, :, :].rearrange("p a b e -> p (a b) e")
            t1 = scr[:, 2:4, :, :].rearrange("p a b e -> p (a b) e")
            t2 = scr[:, 4:6, :, :].rearrange("p a b e -> p (a b) e")
            rank = PX[1][:, :].rearrange("p (b e) -> p b e", b=NB)
            nc.vector.tensor_tensor(t2, rank, base_a[:, :].unsqueeze(1).broadcast_to([P, NB, E]), ALU.add)
            link(nc.vector.tensor_scalar(ge, rank, float(P), None, ALU.is_ge))
            link(nc.vector.tensor_tensor(t1, ge, dba[:, :].unsqueeze(1).broadcast_to([P, NB, E]), ALU.mult))
            link(nc.vector.tensor_tensor(slot[:, :, :], t1, t2, ALU.add))
            for q in range(2):
                bs = slice(4 * q, 4 * q + 4)
                link(nc.vector.tensor_tensor(scr[:, bs, :, :], oh[:, bs, :, :], slot[:, bs, :].unsqueeze(2).broadcast_to([P, 4, K, E]), ALU.mult))
                link(nc.vector.reduce_sum(slotk[:, 16 * q:16 * q + 16], scr[:, bs, :, :].rearrange("p b k e -> p (b k) e"), X_AXIS))
                nc.vector.tensor_copy(slots[:, 16 * q:16 * q + 16], slotk[:, 16 * q:16 * q + 16]).then_inc(s_slot, 1)
            ecmp = scr[0:1, :, :, :].rearrange("p b k e -> p (b k) e")
            dve.wait_ge(s_slot, 2)
            link(nc.vector.tensor_tensor(ecmp, pref[0:1, :].unsqueeze(1).broadcast_to([1, OVER_TILES, E]), tiles_row[:, :].unsqueeze(2).broadcast_to([1, OVER_TILES, E]), ALU.is_le))
            link(nc.vector.reduce_sum(eid[:, 0:OVER_TILES], ecmp, X_AXIS))
            link(nc.vector.tensor_scalar(eid[:, 0:OVER_TILES], eid[:, 0:OVER_TILES], float(E - 1), None, ALU.min))
            link(nc.vector.tensor_copy(eid[:, OVER_TILES:OVER_TILES + 1], pref[0:1, E - 1:E]))
            nc.vector.tensor_copy(eidi[:, :], eid[:, :]).then_inc(s_eid, 1)

            def shared_hidden(n):
                dve.wait_ge(s_ssg, n + 1)
                if n == NSH:
                    dve.wait_ge(s_sy, 2)
                nc.vector.tensor_tensor(hs[:, n % NSH, :], PUP[n % 2][:, :], sgs[:, n % 2, :], ALU.mult).then_inc(s_sh, 1)

            def shared_add(m):
                dve.wait_ge(s_sy, m + 1)
                nc.vector.tensor_tensor(X[:, 2 * m:2 * m + 2, :], PY[m % 2][:, :].rearrange("p (b t) -> p b t", b=2), X[:, 2 * m:2 * m + 2, :], ALU.add).then_inc(s_shx, 1)

            for n_ in range(NSH):
                shared_hidden(n_)
            dve.wait_ge(s_ex, 1)
            dve.wait_ge(s_eid, 1)
            link(nc.vector.tensor_tensor(scr[:, :, :, :], oh[:, :, :, :], lb[:, :, :].unsqueeze(2).broadcast_to([P, NB, K, E]), ALU.mult))
            link(nc.vector.reduce_sum(wk[:, :, :].rearrange("p b k -> p (b k)"), scr[:, :, :, :].rearrange("p b k e -> p (b k) e"), X_AXIS))
            link(nc.vector.reduce_sum(den[:, :], wk[:, :, :], X_AXIS))
            link(nc.vector.reciprocal(rden[:, :], den[:, :]))
            nc.vector.tensor_tensor(wt[:, :, :], wk[:, :, :], rden[:, :].unsqueeze(2).broadcast_to([P, NB, K]), ALU.mult).then_inc(s_wt, 1)
            shared_add(0)
            shared_add(1)
            for n_ in range(NSH, 2 * NSH):
                shared_hidden(n_)
            shared_add(2)
            shared_add(3)

            for g in range(NG + 1):
                if g < NG:
                    dve.wait_ge(s_px, g + 1)
                    if g >= 2:
                        dve.wait_ge(s_gu, g - 1)
                    nc.vector.tensor_copy(xgT[:, g % 2, 1, :, :], PX[1][:, :].rearrange("p (t n) -> p t n", t=4)).then_inc(s_xed, 1)
                if g < NG:
                    dve.wait_ge(s_sg, g + 1)
                    if g >= 2:
                        dve.wait_ge(s_py, g - 1)
                    nc.vector.tensor_tensor(h[:, g % 2, :], PUP[g % 2][:, 0:2 * P], sg[:, g % 2, :], ALU.mult).then_inc(s_h, 1)
                if g:
                    m = g - 1
                    dve.wait_ge(s_py, m + 1)
                    if m >= 2:
                        dve.wait_ge(s_yst[m % 2], 16 * (m // 2))
                    nc.vector.tensor_copy(ysb[:, m % 2, 1:4:2, :], PY[1][:, :].rearrange("p (t n) -> p t n", t=2)).then_inc(s_yd, 1)
            n_over = dve.value_load(eidi[0:1, OVER_TILES:OVER_TILES + 1], min_val=0, max_val=OVER_TILES - 1)
            with dve.Fori(0, NOG) as i:
                with dve.If(i * 4 < n_over):
                    dve.wait_ge(s_px, i + (NG + 1))
                    nc.vector.tensor_copy(xgT[:, 0, 1, :, :], PX[1][:, :].rearrange("p (t n) -> p t n", t=4)).then_inc(s_xed, 1)
                    dve.wait_ge(s_sg, i + (NG + 1))
                    nc.vector.tensor_tensor(h[:, 0, :], PUP[0][:, 0:2 * P], sg[:, 0, :], ALU.mult).then_inc(s_h, 1)
                    dve.wait_ge(s_py, i + (NG + 1))
                    nc.vector.tensor_copy(yso[:, 1:4:2, :], PY[1][:, :].rearrange("p (t n) -> p t n", t=2)).then_inc(s_yd, 1)
            for b in range(NB):
                dve.wait_ge(s_yg[b % 2], 16 * K * (b // 2 + 1))
                for k in range(K):
                    ins = nc.vector.scalar_tensor_tensor(X[:, b, :], xg[:, b % 2, k, :], wt[:, b, k:k + 1], X[:, b, :], ALU.mult, ALU.add)
                    if k < K - 1:
                        link(ins)
                ins.then_inc(s_x4, 1)

        @block.tensor
        def _(pe):
            for b in range(NB):
                pe.wait_ge(s_xn, b + 1)
                if b >= 2:
                    pe.wait_ge(s_xt, b - 1)
                bank = PX[0] if b % 2 == 0 else PY[1]
                for c in range(2):
                    last = nc.tensor.transpose(bank[:, c * P:(c + 1) * P], XN[:, b, c * P:(c + 1) * P], ident[:, :])
                last.then_inc(s_t, 1)
                if b == 0:
                    pe.wait_ge(s_w, 48)
                if b:
                    pe.wait_ge(s_xt, b)
                    for c in range(2):
                        nc.tensor.matmul(PX[1][:, E * (b - 1):E * b], XT[:, c, b - 1, :], wr[:, c, :], start=(c == 0), stop=(c == 1))
            pe.wait_ge(s_xt, NB)
            for c in range(2):
                last = nc.tensor.matmul(PX[1][:, E * (NB - 1):E * NB], XT[:, c, NB - 1, :], wr[:, c, :], start=(c == 0), stop=(c == 1))
            last.then_inc(s_r, 1)

            def shared_gate_up(n):
                tg, fc = n // NSH, n % NSH
                if n >= 2:
                    pe.wait_ge(s_sh, n - 1)
                for bank, w in ((PGATE, WG), (PUP, WU)):
                    for c in range(2):
                        last = nc.tensor.matmul(bank[n % 2][:, :], w[:, c, E * F + P * fc:E * F + P * (fc + 1)],
                                                XT[:, c, 4 * tg:4 * tg + 4, :], start=(c == 0), stop=(c == 1))
                last.then_inc(s_sgu, 1)

            def shared_down(m):
                pe.wait_ge(s_sh, NSH * (m // 2 + 1))
                if m >= 2:
                    pe.wait_ge(s_shx, m - 1)
                for j in range(2):
                    b = 2 * m + j
                    for fc in range(NSH):
                        last = nc.tensor.matmul(PY[m % 2][:, j * T:(j + 1) * T], hs[:, fc, (b % 4) * P:(b % 4 + 1) * P], WD[:, E * F // P + fc, :],
                                                start=(fc == 0), stop=(fc == NSH - 1))
                last.then_inc(s_sy, 1)

            pe.wait_ge(s_wsh, 32)
            shared_gate_up(0)
            shared_gate_up(1)
            pe.wait_ge(s_mask, 1)
            nc.tensor.matmul(PX[1][:, :], tril[:, :], mask[:, :, :], start=True, stop=False)
            for b in range(NB - 1):
                nc.tensor.matmul(PX[1][:, E * (b + 1):], ones[:, :], mask[:, b, :].unsqueeze(1).broadcast_to([P, NB - 1 - b, E]), start=False, stop=(b == NB - 2))
            for b in range(NB):
                last = nc.tensor.matmul(PX[0][:, 0:E], ones[:, :], mask[:, b, :], start=(b == 0), stop=(b == NB - 1))
            last.then_inc(s_rank, 1)
            for n in range(2, NSH):
                shared_gate_up(n)
            shared_down(0)
            shared_down(1)
            for n in range(NSH, 2 * NSH):
                shared_gate_up(n)
            shared_down(2)
            shared_down(3)

            def transposes(src):
                for c in range(2):
                    for t in range(4):
                        last = nc.tensor.transpose(PX[c][:, t * P:(t + 1) * P], src[:, t, c * P:(c + 1) * P], ident[:, :])
                last.then_inc(s_px, 1)

            def gate_up(slot, wg, wu):
                for bank, w in ((PGATE[slot], wg), (PUP[slot], wu)):
                    for j in range(2):
                        for c in range(2):
                            for s in range(2):
                                last = nc.tensor.matmul(bank[64 * s:64 * s + 64, j * P:(j + 1) * P], w(c, 2 * j + s), xgT[:, slot, c, 2 * j + s, :],
                                                        start=(c == 0), stop=(c == 1))
                last.then_inc(s_gu, 1)

            def down(slot, wd):
                for j in range(2):
                    for s in range(2):
                        last = nc.tensor.matmul(PY[s][:, j * T:(j + 1) * T], h[64 * s:64 * s + 64, slot, j * P:(j + 1) * P], wd(j, s), start=True, stop=True)
                last.then_inc(s_py, 1)

            def first_half(g):
                pe.wait_ge(s_xg[g % 3], 16 * (g // 3 + 1))
                if g:
                    pe.wait_ge(s_xea, g)
                    pe.wait_ge(s_xed, g)
                transposes(xg[:, g % 3, :, :])

            first_half(0)
            pe.wait_ge(s_wgu, 16 * 8)
            pe.wait_ge(s_shx, 4)
            pe.wait_ge(s_sh, 2 * NSH)
            for g in range(NG):
                pe.wait_ge(s_xea, g + 1)
                pe.wait_ge(s_xed, g + 1)
                if g >= 2:
                    pe.wait_ge(s_h, g - 1)
                gate_up(g % 2, lambda c, t: WG[:, c, F * (4 * g + t):F * (4 * g + t + 1)], lambda c, t: WU[:, c, F * (4 * g + t):F * (4 * g + t + 1)])
                if g + 1 < NG:
                    first_half(g + 1)
                pe.wait_ge(s_h, g + 1)
                if g == 0:
                    pe.wait_ge(s_wd, 64)
                else:
                    pe.wait_ge(s_ya, g)
                    pe.wait_ge(s_yd, g)
                down(g % 2, lambda j, s: WD[64 * s:64 * s + 64, 2 * g + j, :])
            pe.wait_ge(s_eid, 1)
            n_over = pe.value_load(eidi[0:1, OVER_TILES:OVER_TILES + 1], min_val=0, max_val=OVER_TILES - 1)
            with pe.Fori(0, NOG) as i:
                with pe.If(i * 4 < n_over):
                    pe.wait_ge(s_xo, i * (13 * 16) + 13 * 16)
                    pe.wait_ge(s_xea, i + NG)
                    pe.wait_ge(s_xed, i + NG)
                    transposes(xgo)
                    pe.wait_ge(s_xea, i + (NG + 1))
                    pe.wait_ge(s_xed, i + (NG + 1))
                    pe.wait_ge(s_h, i + NG)
                    gate_up(0, lambda c, t: wgo[:, c, t, :], lambda c, t: wuo[:, c, t, :])
                    pe.wait_ge(s_h, i + (NG + 1))
                    pe.wait_ge(s_ya, i + NG)
                    pe.wait_ge(s_yd, i + NG)
                    down(0, lambda j, s: wdo[64 * s:64 * s + 64, j, :])


def build(nc, x, ctx_in, theta_wT, phi_wT, g_wT, out_wT2, col_consts, gamma2, beta2,
          conv_cols, w_qg, w_kv, rw, rot, w_out, gamma,
          w_router, router_bias, w_gate, w_up, w_down, out):
    stack = ExitStack()
    with stack:
        shared = Shared()
        shared.sem = lambda name: stack.enter_context(nc.semaphore(name))
        shared.X = stack.enter_context(nc.sbuf_tensor("X", [P, NB, T], F32))
        shared.C = stack.enter_context(nc.sbuf_tensor("C", [P, NB, T], F32))
        shared.ident = stack.enter_context(nc.sbuf_tensor("ident", [P, P], F32))
        shared.half = stack.enter_context(nc.sbuf_tensor("half", [P, 64], F32))
        shared.YD = nc.dram_tensor("expert_rows_out", (N_TILES * P, T), F32, kind="Internal").ap()
        shared.XG = nc.dram_tensor("expert_rows_in", (N_TILES * P, T), F32, kind="Internal").ap()
        shared.kd = nc.dram_tensor("k_parts", (16, 3, NB, 8, T), BF16, kind="Internal").ap()
        shared.s_zeroed = shared.sem("expert_rows_zeroed")
        shared.s_kd, shared.s_kin = shared.sem("k_stored"), shared.sem("k_loaded")
        with nc.sbuf_tensor("KS", [P, NB, 8, T], BF16) as shared.KS:
            with nc.sbuf_tensor("ksp", [P, 3, NB, T], BF16) as shared.ksp:
                stage_a(nc, shared, x, ctx_in, theta_wT, phi_wT, g_wT, out_wT2, col_consts, gamma2, beta2)
                stage_b(nc, shared, conv_cols, w_qg, w_kv, rw, rot, w_out)
            stage_c(nc, shared, gamma)
        stage_d(nc, shared, w_router, router_bias, w_gate, w_up, w_down, out)


def kernel(**inputs):
    import concourse.bacc as _bacc
    from concourse import mybir as _mybir
    from concourse.bass_utils import run_bass_kernel_spmd as _run

    a = {k: np.asarray(v) for k, v in inputs.items()}
    two = lambda m: np.ascontiguousarray(np.concatenate([m, m], axis=0))
    def own_half(w):
        z = np.zeros_like(w)
        return np.stack([np.concatenate([w, z]), np.concatenate([z, w])], axis=1)

    host = {
        "x": a["x"], "ctx_in": a["ctx_2048"],
        "theta_wT": a["L0_xattn_theta_w"].T, "phi_wT": a["L0_xattn_phi_w"].T, "g_wT": a["L0_xattn_g_w"].T,
        "out_wT2": own_half(a["L0_xattn_out_w"].T),
        "col_consts": np.stack([two(a["L0_xattn_theta_b"]), two(a["L0_xattn_phi_b"]), two(a["L0_xattn_g_b"]), a["L0_xattn_out_b"]], axis=1),
        "gamma2": two(a["L0_xattn_ln_gamma"]), "beta2": two(a["L0_xattn_ln_beta"]),
    }
    def side_by_side(routed, common):
        return np.concatenate([w.transpose(1, 0, 2).reshape(T, -1) for w in (routed, common)], axis=1)

    inv_freq = (1.0 / np.float32(10000.0) ** (np.arange(0, 8, 2, dtype=np.float32) / np.float32(8))).astype(np.float32)
    ang = np.arange(NB, dtype=np.float32)[:, None] * inv_freq[None, :]
    host |= {
        "conv_cols": a["L0_ffn_conv_w"].reshape(2, P, 2).transpose(1, 0, 2),
        "w_qg": np.concatenate([a["L0_ffn_Wq"], a["L0_ffn_Wg"]], axis=1),
        "w_kv": np.concatenate([a["L0_ffn_Wk"], a["L0_ffn_Wv"]], axis=1),
        "rw": a["L0_ffn_router_w"],
        "rot": np.stack([np.cos(ang), np.sin(ang), -np.sin(ang)]).astype(np.float32),
        "w_out": a["L0_ffn_Wout"],
        "c_gamma": a["L1_xattn_gamma"].reshape(1),
        "w_router": a["L1_ffn_router_w"], "router_bias": a["L1_ffn_router_bias"],
        "w_gate": side_by_side(a["L1_ffn_wg"], a["L1_ffn_swg"]), "w_up": side_by_side(a["L1_ffn_wu"], a["L1_ffn_swu"]),
        "w_down": np.concatenate([a["L1_ffn_wd"].reshape(-1, T), a["L1_ffn_swd"].reshape(-1, T)], axis=0),
    }
    nc = _bacc.Bacc("TRN2", target_bir_lowering=False, num_devices=1)
    arrays, args = {}, []
    for name, v in host.items():
        v = np.ascontiguousarray(v)
        arrays[name + "_dram"] = v
        args.append(nc.dram_tensor(name + "_dram", v.shape, _mybir.dt.from_np(v.dtype), kind="ExternalInput").ap())
    args.append(nc.dram_tensor("out_dram", (NB, P, T), F32, kind="ExternalOutput").ap())
    build(nc, *args)
    r = _run(nc, [arrays], core_ids=[0])
    return r.results[0]["out_dram"]
```

```python
import numpy as np
import concourse.bass as bass
from concourse import mybir
from contextlib import ExitStack

F32 = mybir.dt.float32
BF16 = mybir.dt.bfloat16
ALU = mybir.AluOpType
ACT = mybir.ActivationFunctionType
X_AXIS = mybir.AxisListType.X

P = 128
NB = 8
T = 256
EPS = 1e-5
QPART = (0, 1, 2, 0, 1, 0)
KPART = (0, 0, 0, 1, 1, 2)
N_EXPERT = 64
OVER_TILES = 32
N_TILES = N_EXPERT + OVER_TILES


class Shared:
    pass


def stage_a(nc, shared, x, ctx_in, theta_wT, phi_wT, g_wT, out_wT2, col_consts, gamma2, beta2):
    stack = ExitStack()
    with stack:
        def sb(name, shape, dt=F32):
            return stack.enter_context(nc.sbuf_tensor(name, shape, dt))

        sem = shared.sem

        NP = NB // 2
        X, C, ident, half = shared.X, shared.C, shared.ident, shared.half
        thw = sb("thw", [P, 64])
        phw = sb("phw", [P, 64])
        gw = sb("gw", [P, 64])
        outw = sb("outw", [P, 2, P])
        cols = sb("cols", [P, 4])
        gamma = sb("gamma", [P, T])
        beta = sb("beta", [P, T])
        blk64 = sb("blk64", [P, P])

        stats = shared.stats
        mv = sb("mv", [P, NB, 2])
        vare = sb("vare", [P, NB])
        rstd = sb("rstd", [P, NB])
        xn = sb("xn", [P, 2, 2, T])
        thph = sb("thph", [P, 2, 2 * T])
        gx = sb("gx", [P, 2, 2 * 2 * 64])
        nmax = sb("nmax", [P, 2, 4])
        psums = sb("psums", [P, 2, 4])
        prec = sb("prec", [P, 2, 4])
        pr = sb("pr", [P, 2, 4, T])
        pn = sb("pn", [P, 4, T])
        pT = sb("pT", [P, 4, T])
        tx = sb("tx", [P, T])
        tstat = sb("tstat", [P, 6])
        tmv = sb("tmv", [P, 2])
        te = sb("te", [P, 2])
        tm = sb("tm", [P, 4])
        trs = sb("trs", [P, 1])
        h1 = sb("h1", [P, T])
        h2 = sb("h2", [P, T])
        h3 = sb("h3", [P, T])
        hr = sb("hr", [P, T])
        xa = sb("xa", [P, 2, T])
        ksp, kr = shared.ksp, sb("kr", [P, 2, T])

        PS = [stack.enter_context(nc.psum_tensor(f"ps{i}", [P, 512], F32)) for i in range(8)]

        sx, sc_, sw = sem("x_in"), sem("ctx_in"), sem("w_in")
        s_id = sem("ident_ready")
        s_mv = sem("mv_ready")
        s_rstd = sem("rstd_ready")
        s_xn = sem("xn_ready")
        s_tp = sem("thetaphi_done")
        s_g = sem("g_done")
        s_tps = sem("thetaphi_sb")
        s_gs = sem("g_sb")
        s_sc = sem("scores_done")
        s_nm = sem("nmax_ready")
        s_ex = sem("exp_done")
        s_pn = sem("pn_ready")
        s_pt = sem("pT_done")
        s_pta = sem("pT_sb_act")
        s_ptd = sem("pT_sb_dve")
        s_tx = sem("tx_done")
        s_txs = sem("tx_sb")
        s_te = sem("te_ready")
        s_st = sem("stat_done")
        s_tv = sem("tvar_ready")
        s_tr = sem("trstd_ready")
        s_h1 = sem("h1_ready")
        s_h2 = sem("h2_ready")
        s_h3 = sem("h3_ready")
        s_h = sem("h_ready")
        s_o = sem("o_done")
        s_xa = sem("xa_ready")
        s_x1 = sem("x1_ready")
        s_dv = sem("dve_chain")
        s_ks, s_kr = sem("ctx_split"), sem("ctx_rest")

        thb, phb, gb, outb = (cols[:, j:j + 1] for j in range(4))

        block = stack.enter_context(nc.Block())

        @block.sync
        def _(sp):
            sp.dma_start(X[:, 0:2, :], x[0:2].rearrange("b p t -> p b t")).then_inc(sx, 16)
            sp.dma_start(X[:, 2:NB, :], x[2:NB].rearrange("b p t -> p b t")).then_inc(sx, 16)
            sp.wait_ge(s_ks, 3 * NP)
            for h in range(8):
                sp.dma_start(shared.kd[:, :, :, h, :].rearrange("d j b t -> d (j b) t"), ksp[16 * h:16 * h + 16, :, :, :].rearrange("p j b t -> p (j b) t")).then_inc(shared.s_kd, 16)

        @block.gpsimd
        def _(pool):
            pool.memset(ident[:, :], 0.0).then_inc(s_id, 1)
            pool.memset(blk64[:, :], 0.0).then_inc(s_id, 1)
            pool.memset(half[:, :], -0.5).then_inc(s_id, 1)
            pool.wait_ge(s_id, 3)
            pool.affine_select(out=ident[:, :], in_=ident[:, :], compare_op=ALU.not_equal, fill=1.0, base=0,
                               pattern=[[-1, P]], channel_multiplier=1).then_inc(s_id, 1)
            pool.wait_ge(s_id, 4)
            pool.memset(blk64[0:64, 0:64], 1.0 / 64).then_inc(s_id, 1)
            pool.wait_ge(s_id, 5)
            pool.memset(blk64[64:128, 64:128], 1.0 / 64).then_inc(s_id, 1)
            pool.wait_ge(s_id, 6)
            pool.wait_ge(s_mv, 1)
            pool.tensor_tensor(rstd[:, :], vare[:, :], half[:, 0:NB], ALU.pow).then_inc(s_rstd, 1)

            def split(i):
                bs = slice(2 * i, 2 * i + 2)
                pool.wait_ge(sc_, 16)
                pool.tensor_copy(ksp[:, 0, bs, :], C[:, bs, :]).then_inc(s_ks, 1)
                pool.wait_ge(s_ks, 3 * i + 1)
                pool.tensor_tensor(kr[:, :, :], C[:, bs, :], ksp[:, 0, bs, :], ALU.subtract).then_inc(s_kr, 1)
                pool.wait_ge(s_kr, i + 1)
                pool.tensor_copy(ksp[:, 1, bs, :], kr[:, :, :]).then_inc(s_ks, 1)
                pool.wait_ge(s_ks, 3 * i + 2)
                pool.tensor_tensor(ksp[:, 2, bs, :], kr[:, :, :], ksp[:, 1, bs, :], ALU.subtract).then_inc(s_ks, 1)
                pool.wait_ge(s_ks, 3 * i + 3)

            for i in range(NP - 1):
                split(i)
            for i in range(NP):
                pool.wait_ge(s_tv, i + 1)
                pool.tensor_tensor(trs[:, :], tm[:, 3:4], half[:, 0:1], ALU.pow).then_inc(s_tr, 1)
                pool.wait_ge(s_h1, i + 1)
                pool.tensor_tensor(h2[:, :], h1[:, :], gamma[:, :], ALU.mult).then_inc(s_h2, 1)
                pool.wait_ge(s_h2, i + 1)
                pool.tensor_tensor(h3[:, :], h2[:, :], beta[:, :], ALU.add).then_inc(s_h3, 1)
                if i == 0:
                    split(NP - 1)
                pool.wait_ge(s_xa, i + 1)
                pool.tensor_tensor(X[:, 2 * i:2 * i + 2, :], xa[:, :, :], C[:, 2 * i:2 * i + 2, :], ALU.add).then_inc(s_x1, 1)

        @block.scalar
        def _(act):
            act.dma_start(cols[:, :], col_consts).then_inc(sw, 16)
            act.dma_start(thw[:, :], theta_wT).then_inc(sw, 16)
            act.dma_start(phw[:, :], phi_wT).then_inc(sw, 16)
            act.dma_start(gw[:, :], g_wT).then_inc(sw, 16)
            act.dma_start(C[:, :, :], ctx_in.rearrange("b p t -> p b t")).then_inc(sc_, 16)
            act.dma_start(outw[:, :, :], out_wT2).then_inc(sw, 16)
            act.dma_start(gamma[:, :], gamma2).then_inc(sw, 16)
            act.dma_start(beta[:, :], beta2).then_inc(sw, 16)
            act.wait_ge(sw, 7 * 16)

            def theta_phi(i):
                act.wait_ge(s_tp, i + 1)
                nc.scalar.activation(thph[:, i % 2, 0:T], PS[0][:, 0:T], ACT.Identity, bias=thb)
                nc.scalar.activation(thph[:, i % 2, T:2 * T], PS[0][:, T:2 * T], ACT.Identity, bias=phb).then_inc(s_tps, 1)

            def exps(i):
                s = i % 2
                act.wait_ge(s_nm, i + 1)
                for k in range(4):
                    last = nc.scalar.activation(pr[:, s, k, :], PS[2 + k // 2][:, (k % 2) * T:(k % 2 + 1) * T], ACT.Exp,
                                                bias=nmax[:, s, k:k + 1], accum_out=psums[:, s, k:k + 1])
                last.then_inc(s_ex, 1)

            def attended(i):
                act.wait_ge(s_pt, i + 1)
                nc.scalar.copy(pT[:, 0:2, :], PS[4][:, :]).then_inc(s_pta, 1)
                act.wait_ge(s_tx, i + 1)
                if i:
                    act.wait_ge(s_h1, i)
                nc.scalar.activation(tx[:, :], PS[6][:, 0:T], ACT.Identity, bias=gb).then_inc(s_txs, 1)

            def relu(i):
                act.wait_ge(s_h3, i + 1)
                if i:
                    act.wait_ge(s_o, i)
                nc.scalar.activation(hr[:, :], h3[:, :], ACT.Relu).then_inc(s_h, 1)

            for i in range(NP + 2):
                if i < NP:
                    theta_phi(i)
                if i >= 2:
                    relu(i - 2)
                if i < NP:
                    exps(i)
                if 1 <= i <= NP:
                    attended(i - 1)

        @block.vector
        def _(dve):
            n = [0]

            def link(ins):
                n[0] += 1
                ins.then_inc(s_dv, 1)
                dve.wait_ge(s_dv, n[0])

            dve.wait_ge(sx, 32)
            for b in range(NB):
                last = nc.vector.bn_stats(stats[:, b, :], X[:, b, :])
            link(last)
            for b in range(NB):
                last = nc.vector.bn_aggr(mv[:, b, :], stats[:, b, :])
            link(last)
            nc.vector.tensor_scalar(vare[:, :], mv[:, :, 1], EPS, None, ALU.add).then_inc(s_mv, 1)
            dve.wait_ge(s_rstd, 1)

            def xnorm(i):
                s = i % 2
                if i >= 2:
                    dve.wait_ge(s_g, i - 1)
                for j in range(2):
                    b = 2 * i + j
                    last = nc.vector.tensor_scalar(xn[:, s, j, :], X[:, b, :], mv[:, b, 0:1], rstd[:, b:b + 1], ALU.subtract, ALU.mult)
                last.then_inc(s_xn, 1)

            def take_g(i):
                dve.wait_ge(s_g, i + 1)
                nc.vector.tensor_copy(gx[:, i % 2, :], PS[1][:, 0:256]).then_inc(s_gs, 1)

            def maxima(i):
                dve.wait_ge(s_sc, i + 1)
                for k in range(2):
                    last = nc.vector.tensor_reduce(nmax[:, i % 2, 2 * k:2 * k + 2], PS[2 + k][:, :].rearrange("p (c s) -> p c s", c=2),
                                                   X_AXIS, ALU.max, negate=True)
                last.then_inc(s_nm, 1)

            def norm(i):
                s = i % 2
                dve.wait_ge(s_ex, i + 1)
                link(nc.vector.reciprocal(prec[:, s, :], psums[:, s, :]))
                if i:
                    dve.wait_ge(s_pt, i)
                for k in range(4):
                    last = nc.vector.tensor_scalar(pn[:, k, :], pr[:, s, k, :], prec[:, s, k:k + 1], None, ALU.mult)
                last.then_inc(s_pn, 1)

            def take_pT(i):
                dve.wait_ge(s_pt, i + 1)
                nc.vector.tensor_copy(pT[:, 2:4, :], PS[5][:, :].rearrange("p (c s) -> p c s", c=2)).then_inc(s_ptd, 1)

            def moments(i):
                dve.wait_ge(s_txs, i + 1)
                link(nc.vector.bn_stats(tstat[:, :], tx[:, :]))
                link(nc.vector.bn_aggr(tmv[:, :], tstat[:, :]))
                nc.vector.tensor_copy(te[:, 0:1], tmv[:, 0:1])
                link(nc.vector.tensor_tensor(tm[:, 0:1], tmv[:, 0:1], tmv[:, 0:1], ALU.mult))
                nc.vector.tensor_tensor(te[:, 1:2], tm[:, 0:1], tmv[:, 1:2], ALU.add).then_inc(s_te, 1)

            def layer_norm(i):
                dve.wait_ge(s_st, i + 1)
                link(nc.vector.tensor_copy(tm[:, 1:3], PS[6][:, T:T + 2]))
                link(nc.vector.tensor_tensor(tm[:, 0:1], tm[:, 1:2], tm[:, 1:2], ALU.mult))
                link(nc.vector.tensor_tensor(tm[:, 0:1], tm[:, 2:3], tm[:, 0:1], ALU.subtract))
                nc.vector.tensor_scalar(tm[:, 3:4], tm[:, 0:1], EPS, None, ALU.add).then_inc(s_tv, 1)
                dve.wait_ge(s_tr, i + 1)
                if i:
                    dve.wait_ge(s_h2, i)
                nc.vector.tensor_scalar(h1[:, :], tx[:, :], tm[:, 1:2], trs[:, :], ALU.subtract, ALU.mult).then_inc(s_h1, 1)

            def add_x(i):
                dve.wait_ge(s_o, i + 1)
                if i:
                    dve.wait_ge(s_x1, i)
                nc.vector.scalar_tensor_tensor(xa[:, :, :], PS[7][:, :].rearrange("p (b t) -> p b t", b=2), outb,
                                               X[:, 2 * i:2 * i + 2, :], ALU.add, ALU.add).then_inc(s_xa, 1)

            def new_stats(i):
                dve.wait_ge(s_x1, i + 1)
                for b in (2 * i, 2 * i + 1):
                    nc.vector.bn_stats(stats[:, b, :], X[:, b, :])

            xnorm(0)
            for i in range(NP + 2):
                if i + 1 < NP:
                    xnorm(i + 1)
                if i < NP:
                    take_g(i)
                if i >= 2:
                    layer_norm(i - 2)
                if i < NP:
                    maxima(i)
                if 1 <= i <= NP:
                    take_pT(i - 1)
                if i < NP:
                    norm(i)
                if i == NP:
                    moments(i - 1)
                if i >= 2:
                    add_x(i - 2)
                if 1 <= i < NP:
                    moments(i - 1)
                if i >= 3:
                    new_stats(i - 3)
            new_stats(NP - 1)

        @block.tensor
        def _(pe):
            pe.wait_ge(sw, 7 * 16)
            pe.wait_ge(sc_, 16)
            pe.wait_ge(s_id, 6)

            def projections(i):
                s = i % 2
                if i:
                    pe.wait_ge(s_tps, i)
                for j in range(2):
                    nc.tensor.matmul(PS[0][64 * j:64 * j + 64, 0:T], thw[:, :], C[:, 2 * i + j, :], start=True, stop=True)
                pe.wait_ge(s_xn, i + 1)
                for j in range(2):
                    last = nc.tensor.matmul(PS[0][64 * j:64 * j + 64, T:2 * T], phw[:, :], xn[:, s, j, :], start=True, stop=True)
                last.then_inc(s_tp, 1)
                if i:
                    pe.wait_ge(s_gs, i)
                for j in range(2):
                    for c in range(2):
                        k = 2 * j + c
                        last = nc.tensor.matmul(PS[1][:, 64 * k:64 * k + 64], xn[:, s, j, c * P:(c + 1) * P], gw[:, :], start=True, stop=True)
                last.then_inc(s_g, 1)

            def scores(i):
                s = i % 2
                pe.wait_ge(s_tps, i + 1)
                if i:
                    pe.wait_ge(s_ex, i)
                for j in range(2):
                    for c in range(2):
                        last = nc.tensor.matmul(PS[2 + j][:, c * T:(c + 1) * T], thph[64 * j:64 * j + 64, s, c * P:(c + 1) * P],
                                                thph[64 * j:64 * j + 64, s, T:2 * T], start=True, stop=True)
                last.then_inc(s_sc, 1)

            def attend(i):
                s = i % 2
                pe.wait_ge(s_pn, i + 1)
                if i:
                    pe.wait_ge(s_pta, i)
                    pe.wait_ge(s_ptd, i)
                for j in range(2):
                    for c in range(2):
                        for ct in range(2):
                            last = nc.tensor.transpose(PS[4 + j][:, c * T + ct * P:c * T + (ct + 1) * P], pn[:, 2 * j + ct, c * P:(c + 1) * P], ident[:, :])
                last.then_inc(s_pt, 1)
                pe.wait_ge(s_gs, i + 1)
                pe.wait_ge(s_pta, i + 1)
                pe.wait_ge(s_ptd, i + 1)
                if i:
                    pe.wait_ge(s_tv, i)
                for c in range(2):
                    for j in range(2):
                        last = nc.tensor.matmul(PS[6][64 * j:64 * j + 64, 0:T], gx[:, s, 64 * (2 * j + c):64 * (2 * j + c) + 64],
                                                pT[:, 2 * j + c, :], start=(c == 0), stop=(c == 1))
                last.then_inc(s_tx, 1)

            def mean_over_rows(i):
                pe.wait_ge(s_te, i + 1)
                nc.tensor.matmul(PS[6][:, T:T + 2], blk64[:, :], te[:, :], start=True, stop=True).then_inc(s_st, 1)

            def project_out(i):
                pe.wait_ge(s_h, i + 1)
                if i:
                    pe.wait_ge(s_xa, i)
                for j in range(2):
                    last = nc.tensor.matmul(PS[7][:, j * T:(j + 1) * T], outw[:, j, :], hr[:, :], start=True, stop=True)
                last.then_inc(s_o, 1)

            for i in range(NP + 2):
                if i < NP:
                    projections(i)
                if i >= 2:
                    mean_over_rows(i - 2)
                if i < NP:
                    scores(i)
                if 1 <= i <= NP:
                    attend(i - 1)
                if i >= 2:
                    project_out(i - 2)


def stage_b(nc, shared, conv_cols, w_qg, w_kv, rw, rot, w_out):
    stack = ExitStack()
    with stack:
        def sb(name, shape, dt=F32):
            return stack.enter_context(nc.sbuf_tensor(name, shape, dt))

        sem = shared.sem
        X, ident, half = shared.X, shared.ident, shared.half
        L, H, DK, DV = NB, 16, 8, 16
        NG = L // 2

        zeros = sb("b_zeros", [P, T])
        one3 = sb("b_one3", [3, 8 * T], BF16)
        s_z, s_one3 = sem("b_zeros_ready"), sem("b_ones_ready")
        shared.n_zero_dmas = 8
        cw = sb("b_cw", [P, 2, 2])
        wa = sb("b_wa", [P, 2, 400])
        wb = sb("b_wb", [P, 2, 384])
        wo = sb("b_wo", [P, 2, T])
        rws = sb("b_rw", [P, H, DV, 2])
        rwd = sb("b_rwd", [P, H, DV])
        wtmp = sb("b_wtmp", [P, 2, T])
        wmean = sb("b_wmean", [P, 2, H])
        trig = sb("b_trig", [P, 3, L, 4])
        lp1 = sb("b_lp1", [P, L, H])

        stats = shared.stats
        mv = sb("b_mv", [P, L, 2])
        vare = sb("b_vare", [P, L])
        rstd = sb("b_rstd", [P, L])
        xn = sb("b_xn", [P, 2, 2, T])
        XT = sb("b_XT", [P, 2, L + 1, P])
        tmp = sb("b_tmp", [P, 2, 2, P])
        y = sb("b_y", [P, 2, 2, P])
        xc = sb("b_xc", [P, 2, 2, 2, P])
        Q = sb("b_Q", [P, L, P])
        G = sb("b_G", [P, L, T])
        D = sb("b_D", [P, L, H])
        KV = sb("b_KV", [P, L, 384])
        r1 = sb("b_r1", [P, 4, P])
        r2 = sb("b_r2", [P, 4, P])
        r1k = sb("b_r1k", [P, 4, P])
        r2k = sb("b_r2k", [P, 4, P])
        QR = sb("b_QR", [P, L, P])
        KR = sb("b_KR", [P, L, P])
        ind = sb("b_ind", [P, L, H])
        cum = sb("b_cum", [P, L, H])
        ca = sb("b_ca", [P, L, H])
        cb = sb("b_cb", [P, L, H])
        cc = sb("b_cc", [P, L, H])
        cd = sb("b_cd", [P, L, H])
        absd = sb("b_absd", [P, L, H])
        sg = sb("b_sg", [P, L, H])
        cf = sb("b_cf", [P, L, H])
        same = sb("b_same", [P, L, L, H])
        AC = sb("b_AC", [P, L, L, H])
        prod = sb("b_prod", [P, 2, L * P])
        S = sb("b_S", [P, 2, L * H])
        S2 = sb("b_S2", [P, 2, L * H])
        W = sb("b_W", [P, 2, L * T])
        O = sb("b_O", [P, L, T])
        sq = sb("b_sq", [P, 4, T])
        vs = sb("b_vs", [P, 4 * H])
        ve = sb("b_ve", [P, 4 * H])
        std = sb("b_std", [P, 4 * H])
        vr = sb("b_vr", [P, 4 * H])
        og = sb("b_og", [P, 4, T])
        on = sb("b_on", [P, 2, 4, T])
        oT = xn[:, :, :, :].rearrange("p a j t -> p a (j t)")

        PS = [stack.enter_context(nc.psum_tensor(f"b_ps{i}", [P, 512], F32)) for i in range(8)]
        s_w, s_cw, s_rw, s_wo, s_tg = sem("b_w_in"), sem("b_cw_in"), sem("b_rw_in"), sem("b_wo_in"), sem("b_trig_in")
        s_lp = sem("b_consts")
        s_wd = sem("b_weights_ready")
        s_mv, s_rstd = sem("b_mv"), sem("b_rstd")
        s_xn, s_t, s_xt, s_y, s_xc, s_p = sem("b_xn"), sem("b_transposed"), sem("b_xT_sb"), sem("b_conv"), sem("b_xc"), sem("b_proj")
        s_qgd, s_kv = sem("b_qgd_sb"), sem("b_kv_sb")
        s_qr, s_kr = sem("b_q_rot"), sem("b_k_rot")
        s_abs, s_sg = sem("b_abs"), sem("b_sig")
        s_pr, s_s2, s_W, s_O = sem("b_prod"), sem("b_scores"), sem("b_W"), sem("b_O")
        s_kva = sem("b_kv_sb_act")
        s_red, s_std = sem("b_prod_used"), sem("b_std")
        s_sq, s_ve, s_vr, s_og, s_on, s_ot, s_ots, s_y2, s_x2 = (sem("b_" + n) for n in
            ("sq", "ve", "vr", "og", "on", "oT", "oT_sb", "wout", "x2"))
        s_dv, s_pl = sem("b_dve_chain"), sem("b_pool_chain")

        block = stack.enter_context(nc.Block())

        @block.sync
        def _(sp):
            sp.dma_start(cw[:, :, :], conv_cols).then_inc(s_cw, 16)
            sp.dma_start(wa[:, :, 0:384], w_qg.rearrange("(c p) n -> p c n", p=P)).then_inc(s_w, 16)
            sp.dma_start(wb[:, :, :], w_kv.rearrange("(c p) n -> p c n", p=P)).then_inc(s_w, 16)
            sp.dma_start(rws[:, :, :, :], rw.partition_broadcast(P)).then_inc(s_rw, 16)
            sp.dma_start(trig[:, :, :, :], rot.partition_broadcast(P)).then_inc(s_tg, 16)
            sp.dma_start(wo[:, :, :], w_out.rearrange("(c p) n -> p c n", p=P)).then_inc(s_wo, 16)
            sp.wait_ge(shared.s_kd, 16 * 8)
            for j, part in enumerate(KPART):
                sp.dma_start(shared.KS[16 * j:16 * (j + 1), :, :, :], shared.kd[:, part, :, :, :]).then_inc(shared.s_kin, 16)
            sp.wait_ge(s_one3, 1)
            sp.dma_start(shared.KS[96:99, :, :, :].rearrange("j b h t -> j b (h t)"), one3[:, :].unsqueeze(1).broadcast_to([3, NB, 8 * T])).then_inc(shared.s_kin, 16)
            sp.wait_ge(s_z, 1)
            per = N_TILES // 6
            for j, rows in [(j, shared.XG) for j in range(6)] + [(4, shared.YD), (5, shared.YD)]:
                sp.dma_start(rows[P * per * j:P * per * (j + 1), :].rearrange("(p t) d -> p t d", p=P), zeros[:, :].unsqueeze(1).broadcast_to([P, per, T])).then_inc(shared.s_zeroed, 16)

        @block.gpsimd
        def _(pool):
            n = [0]

            def link(ins):
                n[0] += 1
                ins.then_inc(s_pl, 1)
                pool.wait_ge(s_pl, n[0])

            pool.wait_ge(s_mv, 1)
            pool.tensor_tensor(rstd[:, :], vare[:, :], half[:, 0:L], ALU.pow).then_inc(s_rstd, 1)
            pool.memset(one3[:, :], 1.0).then_inc(s_one3, 1)
            pool.wait_ge(s_one3, 1)
            pool.memset(zeros[:, :], 0.0).then_inc(s_z, 1)
            pool.wait_ge(s_z, 1)
            pool.memset(XT[:, :, 0, :], 0.0).then_inc(s_lp, 1)
            pool.wait_ge(s_lp, 1)
            for l in range(L):
                pool.memset(lp1[:, l, :], float(l + 1)).then_inc(s_lp, 1)

            pool.wait_ge(s_tg, 16)

            def rot_k(g):
                pool.wait_ge(s_kv if g == 0 else s_kva, 4)
                ls = slice(4 * g, 4 * g + 4)
                k = KV[:, ls, 0:P]
                cos = trig[:, 0, ls, :].unsqueeze(2).broadcast_to([P, 4, 2 * H, 4])
                sin = trig[:, 1, ls, :].unsqueeze(2).broadcast_to([P, 4, H, 4])
                nsin = trig[:, 2, ls, :].unsqueeze(2).broadcast_to([P, 4, H, 4])
                k5 = k.rearrange("p l (h e f) -> p l h e f", e=2, f=4)
                t5 = r2k[:, :, :].rearrange("p l (h e f) -> p l h e f", e=2, f=4)
                pool.tensor_tensor(r1k[:, :, :].rearrange("p l (h f) -> p l h f", f=4), k.rearrange("p l (h f) -> p l h f", f=4), cos, ALU.mult)
                pool.tensor_tensor(t5[:, :, :, 0, :], k5[:, :, :, 1, :], nsin, ALU.mult)
                link(pool.tensor_tensor(t5[:, :, :, 1, :], k5[:, :, :, 0, :], sin, ALU.mult))
                pool.tensor_tensor(KR[:, ls, :], r1k[:, :, :], r2k[:, :, :], ALU.add).then_inc(s_kr, 1)
                pool.wait_ge(s_kr, g + 1)

            def prod_qk(l):
                pool.wait_ge(s_qr, l // 4 + 1)
                if l >= 2:
                    pool.wait_ge(s_red, l - 1)
                pool.tensor_tensor(prod[:, l % 2, 0:(l + 1) * P].rearrange("p (m x) -> p m x", m=l + 1),
                                   QR[:, l, :].unsqueeze(1).broadcast_to([P, l + 1, P]), KR[:, 0:l + 1, :], ALU.mult).then_inc(s_pr, 1)

            def gate(g):
                pool.wait_ge(s_O, 4 * (g + 1))
                if g:
                    pool.wait_ge(s_on, g)
                pool.tensor_tensor(og[:, :, :], O[:, 4 * g:4 * g + 4, :], G[:, 4 * g:4 * g + 4, :], ALU.mult).then_inc(s_og, 1)

            rot_k(0)
            for l in range(4):
                prod_qk(l)
            rot_k(1)
            for l in range(4, 8):
                prod_qk(l)
                if l == 4:
                    gate(0)
            gate(1)

        @block.scalar
        def _(act):
            def weight_of_choice(g):
                ls = slice(4 * g, 4 * g + 4)
                act.wait_ge(s_abs, g + 1)
                nc.scalar.activation(sg[:, ls, :], absd[:, ls, :], ACT.Sigmoid).then_inc(s_sg, 1)

            for g in range(NG + 1):
                if g < NG:
                    act.wait_ge(s_t, g + 1)
                    for c in range(2):
                        last = nc.scalar.copy(XT[:, c, 1 + 2 * g:3 + 2 * g, :], PS[c][:, 0:256].rearrange("p (l b) -> p l b", l=2))
                    last.then_inc(s_xt, 1)
                    act.wait_ge(s_y, g + 1)
                    if g >= 2:
                        act.wait_ge(s_p, 2 * (g - 1))
                    nc.scalar.activation(xc[:, g % 2, :, :, :], y[:, :, :, :], ACT.Silu).then_inc(s_xc, 1)
                if g > 0:
                    for l in (2 * g - 2, 2 * g - 1):
                        act.wait_ge(s_p, l + 1)
                        bank = PS[2 + 2 * (l % 2)]
                        nc.scalar.activation(Q[:, l, :], bank[:, 0:P], ACT.Silu)
                        nc.scalar.activation(G[:, l, :], bank[:, P:P + T], ACT.Silu)
                        nc.scalar.copy(D[:, l, :], bank[:, 384:400]).then_inc(s_qgd, 1)
                        if l >= 4:
                            nc.scalar.copy(KV[:, l, :], PS[3 + 2 * (l % 2)][:, 0:384]).then_inc(s_kva, 1)
                        if l == 5:
                            weight_of_choice(0)
            weight_of_choice(1)
            for g in range(2):
                act.wait_ge(s_O, 4 * (g + 1))
                if g:
                    act.wait_ge(s_ve, g)
                nc.scalar.activation(sq[:, :, :], O[:, 4 * g:4 * g + 4, :], ACT.Square).then_inc(s_sq, 1)
                act.wait_ge(s_ve, g + 1)
                if g:
                    act.wait_ge(s_vr, g)
                nc.scalar.activation(std[:, :], ve[:, :], ACT.Sqrt).then_inc(s_std, 1)
                for j in range(4):
                    l = 4 * g + j
                    act.wait_ge(s_ot, l + 1)
                    if l >= 2:
                        act.wait_ge(s_y2, l - 1)
                    nc.scalar.copy(oT[:, l % 2, 0:T], PS[l % 2][:, 0:T]).then_inc(s_ots, 1)

        @block.vector
        def _(dve):
            n = [0]

            def link(ins):
                n[0] += 1
                ins.then_inc(s_dv, 1)
                dve.wait_ge(s_dv, n[0])

            for b in range(L):
                last = nc.vector.bn_aggr(mv[:, b, :], stats[:, b, :])
            link(last)
            nc.vector.tensor_scalar(vare[:, :], mv[:, :, 1], EPS, None, ALU.add).then_inc(s_mv, 1)
            dve.wait_ge(s_rstd, 1)

            def norm(g):
                if g >= 2:
                    dve.wait_ge(s_t, g - 1)
                for j in range(2):
                    l = 2 * g + j
                    last = nc.vector.tensor_scalar(xn[:, g % 2, j, :], X[:, l, :], mv[:, l, 0:1], rstd[:, l:l + 1], ALU.subtract, ALU.mult)
                last.then_inc(s_xn, 1)

            norm(0)
            norm(1)
            dve.wait_ge(s_rw, 16)
            link(nc.vector.tensor_tensor(rwd[:, :, :], rws[:, :, :, 1], rws[:, :, :, 0], ALU.subtract))
            dve.wait_ge(s_w, 32)
            wv = wb[:, :, P:384]
            link(nc.vector.tensor_tensor(wtmp[:, :, :], wv, rwd[:, :, :].rearrange("p h d -> p (h d)").unsqueeze(1).broadcast_to([P, 2, T]), ALU.mult))
            for c in range(2):
                nc.vector.reduce_sum(wa[:, c, 384:400], wtmp[:, c, :].rearrange("p (h d) -> p h d", h=H), X_AXIS)
                last = nc.vector.reduce_sum(wmean[:, c, :], wb[:, c, P:384].rearrange("p (h d) -> p h d", h=H), X_AXIS)
            link(last)
            for c in range(2):
                v = wb[:, c, P:384].rearrange("p (h d) -> p h d", h=H)
                last = nc.vector.scalar_tensor_tensor(v, wmean[:, c, :].unsqueeze(2).broadcast_to([P, H, DV]), -1.0 / DV, v, ALU.mult, ALU.add)
            last.then_inc(s_wd, 1)
            dve.wait_ge(s_cw, 16)
            dve.wait_ge(s_lp, 1)

            def conv(g):
                dve.wait_ge(s_xt, g + 1)
                if g:
                    dve.wait_ge(s_xc, g)
                for c in range(2):
                    last = nc.vector.tensor_scalar(tmp[:, c, :, :], XT[:, c, 1 + 2 * g:3 + 2 * g, :], cw[:, c, 1:2], None, ALU.mult)
                link(last)
                for c in range(2):
                    last = nc.vector.scalar_tensor_tensor(y[:, c, :, :], XT[:, c, 2 * g:2 * g + 2, :], cw[:, c, 0:1], tmp[:, c, :, :], ALU.mult, ALU.add)
                last.then_inc(s_y, 1)

            def take_kv(l):
                dve.wait_ge(s_p, l + 1)
                nc.vector.tensor_copy(KV[:, l, :], PS[3 + 2 * (l % 2)][:, 0:384]).then_inc(s_kv, 1)

            for g in range(NG + 1):
                if g < NG:
                    conv(g)
                    if g + 2 < NG:
                        norm(g + 2)
                if g in (1, 2):
                    take_kv(2 * g - 2)
                    take_kv(2 * g - 1)

            def absolute(g):
                ls = slice(4 * g, 4 * g + 4)
                dve.wait_ge(s_qgd, 4 * (g + 1))
                nc.vector.scalar_tensor_tensor(absd[:, ls, :], D[:, ls, :], -1.0, D[:, ls, :], ALU.mult, ALU.max).then_inc(s_abs, 1)

            def rotate_q(g):
                ls = slice(4 * g, 4 * g + 4)
                q = Q[:, ls, :]
                cos = trig[:, 0, ls, :].unsqueeze(2).broadcast_to([P, 4, 2 * H, 4])
                sin = trig[:, 1, ls, :].unsqueeze(2).broadcast_to([P, 4, H, 4])
                nsin = trig[:, 2, ls, :].unsqueeze(2).broadcast_to([P, 4, H, 4])
                q5 = q.rearrange("p l (h e f) -> p l h e f", e=2, f=4)
                t5 = r2[:, :, :].rearrange("p l (h e f) -> p l h e f", e=2, f=4)
                nc.vector.tensor_tensor(r1[:, :, :].rearrange("p l (h f) -> p l h f", f=4), q.rearrange("p l (h f) -> p l h f", f=4), cos, ALU.mult)
                nc.vector.tensor_tensor(t5[:, :, :, 0, :], q5[:, :, :, 1, :], nsin, ALU.mult)
                link(nc.vector.tensor_tensor(t5[:, :, :, 1, :], q5[:, :, :, 0, :], sin, ALU.mult))
                nc.vector.tensor_tensor(QR[:, ls, :], r1[:, :, :], r2[:, :, :], ALU.add).then_inc(s_qr, 1)
                dve.wait_ge(s_qr, g + 1)

            def choices(g):
                lo, hi = 4 * g, 4 * g + 4
                ls = slice(lo, hi)
                link(nc.vector.tensor_scalar(ind[:, ls, :], D[:, ls, :], 0.0, None, ALU.is_gt))
                for l in range(lo, hi):
                    if l == 0:
                        link(nc.vector.tensor_copy(cum[:, 0, :], ind[:, 0, :]))
                    else:
                        link(nc.vector.tensor_tensor(cum[:, l, :], cum[:, l - 1, :], ind[:, l, :], ALU.add))
                dve.wait_ge(s_lp, 1 + L)
                link(nc.vector.tensor_tensor(ca[:, ls, :], lp1[:, ls, :], cum[:, ls, :], ALU.subtract))
                link(nc.vector.tensor_tensor(cb[:, ls, :], cum[:, ls, :], ca[:, ls, :], ALU.subtract))
                link(nc.vector.tensor_tensor(cc[:, ls, :], cb[:, ls, :], ind[:, ls, :], ALU.mult))
                link(nc.vector.tensor_tensor(cd[:, ls, :], cc[:, ls, :], ca[:, ls, :], ALU.add))
                link(nc.vector.reciprocal(cb[:, ls, :], cd[:, ls, :]))
                dve.wait_ge(s_sg, g + 1)
                nc.vector.scalar_tensor_tensor(cf[:, ls, :], sg[:, ls, :], float(DK) ** -0.5, cb[:, ls, :], ALU.mult, ALU.mult)
                link(nc.vector.tensor_tensor(same[:, ls, 0:hi, :], ind[:, ls, :].unsqueeze(2).broadcast_to([P, 4, hi, H]),
                                             ind[:, 0:hi, :].unsqueeze(1).broadcast_to([P, 4, hi, H]), ALU.is_equal))
                link(nc.vector.tensor_tensor(AC[:, ls, 0:hi, :], same[:, ls, 0:hi, :], cf[:, ls, :].unsqueeze(2).broadcast_to([P, 4, hi, H]), ALU.mult))

            def attend(l):
                s = l % 2
                m = l + 1
                dve.wait_ge(s_pr, l + 1)
                nc.vector.reduce_sum(S[:, s, 0:m * H], prod[:, s, 0:m * P].rearrange("p (x d) -> p x d", d=DK), X_AXIS).then_inc(s_red, 1)
                dve.wait_ge(s_red, l + 1)
                link(nc.vector.tensor_tensor(S2[:, s, 0:m * H], S[:, s, 0:m * H], AC[:, l, 0:m, :].rearrange("p m h -> p (m h)"), ALU.mult))
                link(nc.vector.tensor_tensor(W[:, s, 0:m * T].rearrange("p (m h d) -> p m h d", m=m, h=H),
                                             S2[:, s, 0:m * H].rearrange("p (m h) -> p m h", m=m).unsqueeze(3).broadcast_to([P, m, H, DV]),
                                             KV[:, 0:m, P:384].rearrange("p m (h d) -> p m h d", h=H), ALU.mult))
                nc.vector.reduce_sum(O[:, l, :], W[:, s, 0:m * T].rearrange("p (m x) -> p x m", m=m), X_AXIS).then_inc(s_O, 1)

            def head_norm(g):
                dve.wait_ge(s_sq, g + 1)
                if g:
                    dve.wait_ge(s_vr, g)
                link(nc.vector.reduce_sum(vs[:, :], sq[:, :, :].rearrange("p l (h d) -> p (l h) d", h=H), X_AXIS))
                nc.vector.tensor_scalar(ve[:, :], vs[:, :], 1.0 / DV, EPS, ALU.mult, ALU.add).then_inc(s_ve, 1)

            def scale(g):
                dve.wait_ge(s_std, g + 1)
                nc.vector.reciprocal(vr[:, :], std[:, :]).then_inc(s_vr, 1)
                dve.wait_ge(s_vr, g + 1)
                dve.wait_ge(s_og, g + 1)
                nc.vector.tensor_tensor(on[:, g, :, :].rearrange("p l (h d) -> p (l h) d", h=H), og[:, :, :].rearrange("p l (h d) -> p (l h) d", h=H),
                                        vr[:, :].unsqueeze(2).broadcast_to([P, 4 * H, DV]), ALU.mult).then_inc(s_on, 1)

            def residual(l):
                dve.wait_ge(s_y2, l + 1)
                nc.vector.tensor_tensor(X[:, l, :], PS[2 + l % 2][:, 0:T], X[:, l, :], ALU.add).then_inc(s_x2, 1)
                dve.wait_ge(s_x2, l + 1)
                nc.vector.bn_stats(stats[:, l, :], X[:, l, :])

            dve.wait_ge(s_tg, 16)
            absolute(0)
            rotate_q(0)
            choices(0)
            for l in range(4):
                attend(l)
            absolute(1)
            rotate_q(1)
            choices(1)
            attend(4)
            head_norm(0)
            attend(5)
            scale(0)
            attend(6)
            residual(0)
            residual(1)
            attend(7)
            residual(2)
            head_norm(1)
            residual(3)
            scale(1)
            for l in range(4, 8):
                residual(l)

        @block.tensor
        def _(pe):
            def transposes(g):
                pe.wait_ge(s_xn, g + 1)
                if g:
                    pe.wait_ge(s_xt, g)
                for c in range(2):
                    for j in range(2):
                        last = nc.tensor.transpose(PS[c][:, j * P:(j + 1) * P], xn[:, g % 2, j, c * P:(c + 1) * P], ident[:, :])
                last.then_inc(s_t, 1)

            transposes(0)
            for g in range(NG):
                if g + 1 < NG:
                    transposes(g + 1)
                pe.wait_ge(s_xc, g + 1)
                if g == 0:
                    pe.wait_ge(s_wd, 1)
                for j in range(2):
                    l = 2 * g + j
                    if l >= 2:
                        pe.wait_ge(s_qgd, l - 1)
                        pe.wait_ge(s_kv if l < 6 else s_kva, l - 1 if l < 6 else l - 5)
                    for c in range(2):
                        nc.tensor.matmul(PS[2 + 2 * j][:, 0:400], xc[:, g % 2, c, j, :], wa[:, c, :], start=(c == 0), stop=(c == 1))
                    for c in range(2):
                        last = nc.tensor.matmul(PS[3 + 2 * j][:, 0:384], xc[:, g % 2, c, j, :], wb[:, c, :], start=(c == 0), stop=(c == 1))
                    last.then_inc(s_p, 1)
            pe.wait_ge(s_wo, 16)
            pe.wait_ge(s_qgd, L)
            pe.wait_ge(s_kva, L - 4)

            def transpose_gated(l):
                pe.wait_ge(s_on, l // 4 + 1)
                if l >= 2:
                    pe.wait_ge(s_ots, l - 1)
                for c in range(2):
                    last = nc.tensor.transpose(PS[l % 2][:, c * P:(c + 1) * P], on[:, l // 4, l % 4, c * P:(c + 1) * P], ident[:, :])
                last.then_inc(s_ot, 1)

            for l in range(L):
                if l % 4 == 0:
                    transpose_gated(l)
                if l % 4 < 3:
                    transpose_gated(l + 1)
                pe.wait_ge(s_ots, l + 1)
                if l >= 2:
                    pe.wait_ge(s_x2, l - 1)
                for c in range(2):
                    last = nc.tensor.matmul(PS[2 + l % 2][:, 0:T], oT[:, l % 2, c * P:(c + 1) * P], wo[:, c, :], start=(c == 0), stop=(c == 1))
                last.then_inc(s_y2, 1)


def stage_c(nc, shared, gamma):
    stack = ExitStack()
    with stack:
        def sb(name, shape, dt=F32):
            return stack.enter_context(nc.sbuf_tensor(name, shape, dt))

        sem = shared.sem
        X, C, ident, half = shared.X, shared.C, shared.ident, shared.half
        H, D = 8, 16
        NC = T // P
        ROWS = 6 * D
        GROUPS = ((0, 2), (2, NB))

        gam = sb("c_gamma", [P, 1])
        stats = shared.stats
        mv = sb("c_mv", [P, NB, 2])
        vare = sb("c_vare", [P, NB])
        rstd = sb("c_rstd", [P, NB])
        KS = shared.KS
        VZ = sb("c_VZ", [P, NB, NC, 2, 4, 32])
        OZ = sb("c_OZ", [P, 2, 32])
        xn = sb("c_xn", [P, NB, T])
        qr = sb("c_qr", [P, NB, T])
        qsp = [sb(f"c_qsp{g}", [P, 3, hi - lo, T], BF16) for g, (lo, hi) in enumerate(GROUPS)]
        QS = sb("c_QS", [P, NB, H, T], BF16)
        nm = sb("c_nm", [P, 2, H, NC])
        nmr = sb("c_nmr", [16, P])
        nmT = sb("c_nmT", [16, P])
        nms = sb("c_nms", [16, 2, 3, P], BF16)
        pT = sb("c_pT", [P, 2, NC, H, T])
        pvz = sb("c_pvz_sb", [P, 2, 2 * T])
        rinv = sb("c_rinv", [P, T])
        ret = sb("c_ret", [P, 2, T])

        md = nc.dram_tensor("max_parts", (NB, 16, 3, P), BF16, kind="Internal").ap()
        qd = [nc.dram_tensor(f"q_parts{g}", (D, 3, hi - lo, H, T), BF16, kind="Internal").ap() for g, (lo, hi) in enumerate(GROUPS)]

        PM = [stack.enter_context(nc.psum_tensor(f"c_pm{i}", [P, 512], F32)) for i in range(2)]
        PE2 = [stack.enter_context(nc.psum_tensor(f"c_pe{i}", [P, 1024], F32)) for i in range(2)]
        PVZ = stack.enter_context(nc.psum_tensor("c_pvz", [P, 512], F32))
        PT = stack.enter_context(nc.psum_tensor("c_pt", [P, 512], F32))
        PV, PZ = PVZ[:, 0:T], PVZ[:, T:2 * T]

        s_gam, s_one = sem("c_gamma_in"), sem("c_ones")
        s_mv, s_rstd, s_q = sem("c_mv"), sem("c_rstd"), sem("c_q_split")
        s_qd = [sem(f"c_q_stored{j}") for j in range(2)]
        s_qin = [sem(f"c_q_loaded{j}") for j in range(2)]
        s_vt, s_vz = sem("c_v_transposed"), sem("c_v_sb")
        s_m1, s_mx, s_mt, s_ms = sem("c_scores"), sem("c_max"), sem("c_maxT"), sem("c_max_split")
        s_md, s_mtc, s_min = sem("c_max_stored"), sem("c_maxT_sb"), sem("c_max_loaded")
        s_s2, s_ex, s_pv, s_pvc, s_ret, s_x3 = sem("c_scoresT"), sem("c_exp"), sem("c_pv_done"), sem("c_pvz_copied"), sem("c_ret"), sem("c_x3")
        s_dv, s_pl = sem("c_dve_chain"), sem("c_pool_chain")
        s_ri = sem("c_rinv")

        def parts_of_q(eng, g):
            lo, hi = GROUPS[g]
            eng.wait_ge(s_q, g + 1)
            for h in range(H):
                eng.dma_start(qd[g][:, :, :, h, :].rearrange("d j b t -> d (j b) t"), qsp[g][D * h:D * (h + 1), :, :, :].rearrange("p j b t -> p (j b) t")).then_inc(s_qd[g], 16)
            eng.wait_ge(s_qd[g], 16 * H)
            for j, part in enumerate(QPART):
                eng.dma_start(QS[D * j:D * (j + 1), lo:hi, :, :], qd[g][:, part, :, :, :]).then_inc(s_qin[g], 16)

        def sources_left(eng):
            eng.wait_ge(shared.s_kin, 16 * 7)
            eng.wait_ge(shared.s_zeroed, 16 * shared.n_zero_dmas)

        block = stack.enter_context(nc.Block())

        @block.sync
        def _(sp):
            parts_of_q(sp, 0)
            for b in range(NB):
                sp.wait_ge(s_ms, b + 1)
                sp.dma_start(md[b], nms[:, b % 2, :, :]).then_inc(s_md, 16)
                sp.wait_ge(s_md, 16 * (b + 1))
                sp.dma_start(QS[ROWS:ROWS + 3, b, :, :].rearrange("j h (c q) -> j (h c) q", c=NC), md[b].rearrange("r j q -> j r q")).then_inc(s_min, 16)
                sp.wait_ge(s_min, 16 * (b + 1))

        @block.gpsimd
        def _(pool):
            n = [0]

            def link(ins):
                n[0] += 1
                ins.then_inc(s_pl, 1)
                pool.wait_ge(s_pl, n[0])

            sources_left(pool)
            pool.wait_ge(s_mv, 1)
            pool.tensor_tensor(rstd[:, :], vare[:, :], half[:, 0:NB], ALU.pow).then_inc(s_rstd, 1)
            pool.dma_start(gam[:, :], gamma.partition_broadcast(P)).then_inc(s_gam, 16)
            link(pool.memset(OZ[:, :, :], 0.0))
            link(pool.memset(OZ[:, 0, 0:D], 1.0))
            pool.memset(OZ[:, 1, D:2 * D], 1.0).then_inc(s_one, 1)
            pool.memset(VZ[:, :, :, :, :, :], 0.0).then_inc(s_one, 1)
            for b in range(NB):
                pool.wait_ge(s_ret, b + 1)
                pool.tensor_tensor(X[:, b, :], ret[:, b % 2, :], X[:, b, :], ALU.add).then_inc(s_x3, 1)

        @block.scalar
        def _(act):
            parts_of_q(act, 1)

            def take_values(b):
                act.wait_ge(s_pv, b + 1)
                if b >= 2:
                    act.wait_ge(s_ret, b - 1)
                nc.scalar.copy(pvz[:, b % 2, :], PVZ[:, :]).then_inc(s_pvc, 1)

            for b in range(NB):
                for u in range(4):
                    act.wait_ge(s_s2, 4 * b + u + 1)
                    if b >= 2 and u == 0:
                        act.wait_ge(s_pv, b - 1)
                    nc.scalar.activation(pT[:, b % 2, u // 2, 4 * (u % 2):4 * (u % 2) + 4, :], PE2[u % 2][:, :].rearrange("p (h q) -> p h q", h=4),
                                         ACT.Exp, scale=D ** -0.5).then_inc(s_ex, 1)
                if b:
                    take_values(b - 1)
            take_values(NB - 1)

        @block.vector
        def _(dve):
            n = [0]

            def link(ins):
                n[0] += 1
                ins.then_inc(s_dv, 1)
                dve.wait_ge(s_dv, n[0])

            sources_left(dve)
            for b in range(NB):
                last = nc.vector.bn_aggr(mv[:, b, :], stats[:, b, :])
            link(last)
            nc.vector.tensor_scalar(vare[:, :], mv[:, :, 1], EPS, None, ALU.add).then_inc(s_mv, 1)
            dve.wait_ge(s_rstd, 1)
            for g, (lo, hi) in enumerate(GROUPS):
                for b in range(lo, hi):
                    last = nc.vector.tensor_scalar(xn[:, b, :], X[:, b, :], mv[:, b, 0:1], rstd[:, b:b + 1], ALU.subtract, ALU.mult)
                link(last)
                link(nc.vector.tensor_copy(qsp[g][:, 0, :, :], xn[:, lo:hi, :]))
                link(nc.vector.tensor_tensor(qr[:, lo:hi, :], xn[:, lo:hi, :], qsp[g][:, 0, :, :], ALU.subtract))
                link(nc.vector.tensor_copy(qsp[g][:, 1, :, :], qr[:, lo:hi, :]))
                nc.vector.tensor_tensor(qsp[g][:, 2, :, :], qr[:, lo:hi, :], qsp[g][:, 1, :, :], ALU.subtract).then_inc(s_q, 1)

            def maxima(b, h):
                dve.wait_ge(s_m1, H * b + h + 1)
                if b >= 2 and h == 0:
                    dve.wait_ge(s_mt, b - 1)
                nc.vector.tensor_reduce(nm[:, b % 2, h, :], PM[h % 2][:, :].rearrange("p (c l) -> p c l", c=NC), X_AXIS, ALU.max, negate=True).then_inc(s_mx, 1)

            def split_max(b):
                dve.wait_ge(s_mt, b + 1)
                if b >= 2:
                    dve.wait_ge(s_md, 16 * (b - 1))
                nc.vector.tensor_copy(nmT[:, :], PT[0:16, 0:P]).then_inc(s_mtc, 1)
                dve.wait_ge(s_mtc, b + 1)
                link(nc.vector.tensor_copy(nms[:, b % 2, 0, :], nmT[:, :]))
                link(nc.vector.tensor_tensor(nmr[:, :], nmT[:, :], nms[:, b % 2, 0, :], ALU.subtract))
                link(nc.vector.tensor_copy(nms[:, b % 2, 1, :], nmr[:, :]))
                nc.vector.tensor_tensor(nms[:, b % 2, 2, :], nmr[:, :], nms[:, b % 2, 1, :], ALU.subtract).then_inc(s_ms, 1)
                dve.wait_ge(s_ms, b + 1)

            def inverse(b, half_):
                dve.wait_ge(s_pvc, b + 1)
                if b and half_ == 0:
                    dve.wait_ge(s_ret, b)
                qs = slice(P * half_, P * (half_ + 1))
                nc.vector.reciprocal(rinv[:, qs], pvz[:, b % 2, T + P * half_:T + P * (half_ + 1)]).then_inc(s_ri, 1)

            def new_stats(b):
                dve.wait_ge(s_x3, b + 1)
                nc.vector.bn_stats(stats[:, b, :], X[:, b, :])

            def finish(b):
                dve.wait_ge(s_ri, 2 * (b + 1))
                if b >= 2:
                    dve.wait_ge(s_x3, b - 1)
                nc.vector.scalar_tensor_tensor(ret[:, b % 2, :], pvz[:, b % 2, 0:T], gam[:, :], rinv[:, :], ALU.mult, ALU.mult).then_inc(s_ret, 1)
                dve.wait_ge(s_ret, b + 1)

            dve.wait_ge(s_one, 2)
            for b in range(NB):
                dve.wait_ge(s_vt, b + 1)
                for a in range(2):
                    last = nc.vector.tensor_copy(VZ[:, b, :, a, :, D * a:D * (a + 1)],
                                                 PM[b % 2][:, 0:T].rearrange("p (c i n) -> p c i n", c=NC, i=4)[:, :, :, D * a:D * (a + 1)])
                last.then_inc(s_vz, 1)
            for h in range(H):
                maxima(0, h)
            split_max(0)
            for h in range(H):
                maxima(1, h)
            dve.wait_ge(s_gam, 16)
            for b in range(NB):
                if b + 2 < NB:
                    maxima(b + 2, 0)
                    maxima(b + 2, 1)
                if b + 1 < NB:
                    split_max(b + 1)
                for h in range(2, H):
                    if b + 2 < NB:
                        maxima(b + 2, h)
                    if b >= 2:
                        if h in (2, 4):
                            inverse(b - 2, (h - 2) // 2)
                        if h == 6:
                            finish(b - 2)
                    if h == 7 and b >= 3:
                        new_stats(b - 3)
            for b in (NB - 2, NB - 1):
                inverse(b, 0)
                inverse(b, 1)
                finish(b)
                new_stats(b - 1)
            new_stats(NB - 1)

        @block.tensor
        def _(pe):
            for b in range(NB):
                if b >= 2:
                    pe.wait_ge(s_vz, b - 1)
                for c in range(NC):
                    last = nc.tensor.transpose(PM[b % 2][:, c * P:(c + 1) * P], C[:, b, c * P:(c + 1) * P], ident[:, :])
                last.then_inc(s_vt, 1)
            pe.wait_ge(s_vz, NB)
            pe.wait_ge(shared.s_kin, 16 * 7)
            pe.wait_ge(s_one, 2)

            def scores(b, h):
                if h == 0 and b in (0, GROUPS[1][0]):
                    pe.wait_ge(s_qin[0 if b == 0 else 1], 16 * 6)
                if H * b + h >= 2:
                    pe.wait_ge(s_mx, H * b + h - 1)
                for c in range(NC):
                    last = nc.tensor.matmul(PM[h % 2][:, c * T:(c + 1) * T], QS[0:ROWS, b, h, c * P:(c + 1) * P], KS[0:ROWS, b, h, :], start=True, stop=True)
                last.then_inc(s_m1, 1)

            def max_rows(b):
                pe.wait_ge(s_mx, H * (b + 1))
                if b:
                    pe.wait_ge(s_mtc, b)
                nc.tensor.transpose(PT[0:16, 0:P], nm[:, b % 2, :, :].rearrange("p h c -> p (h c)"), ident[:, :]).then_inc(s_mt, 1)

            def scores_t(b, u):
                c, h0 = u // 2, 4 * (u % 2)
                if u == 0:
                    pe.wait_ge(s_min, 16 * (b + 1))
                if 4 * b + u >= 2:
                    pe.wait_ge(s_ex, 4 * b + u - 1)
                for k in range(4):
                    last = nc.tensor.matmul(PE2[u % 2][:, k * T:(k + 1) * T], KS[0:ROWS + 3, b, h0 + k, c * P:(c + 1) * P], QS[0:ROWS + 3, b, h0 + k, :], start=True, stop=True)
                last.then_inc(s_s2, 1)

            def values(b, u):
                c, a = u // 2, u % 2
                if u == 0:
                    pe.wait_ge(s_ex, 4 * (b + 1))
                    if b:
                        pe.wait_ge(s_pvc, b)
                for out_, w in ((PV, VZ[:, b, c, a, :, :]), (PZ, None)):
                    for i in range(4):
                        last = nc.tensor.matmul(out_[32 * i:32 * i + 32, :], OZ[:, a, :] if w is None else w[:, i, :], pT[:, b % 2, c, 2 * i + a, :],
                                                start=(u == 0 and w is not None), stop=(u == 3 and w is None))
                if u == 3:
                    last.then_inc(s_pv, 1)

            for h in range(H):
                scores(0, h)
            max_rows(0)
            for h in range(H):
                scores(1, h)
            for b in range(NB + 1):
                for u in range(4):
                    if b < NB:
                        scores_t(b, u)
                    if b + 2 < NB:
                        scores(b + 2, 2 * u)
                        scores(b + 2, 2 * u + 1)
                    if u == 0 and b + 1 < NB:
                        max_rows(b + 1)
                    if b:
                        values(b - 1, u)


def stage_d(nc, shared, w_router, router_bias, w_gate, w_up, w_down, out):
    stack = ExitStack()
    with stack:
        def sb(name, shape, dt=F32):
            return stack.enter_context(nc.sbuf_tensor(name, shape, dt))

        sem = shared.sem
        X, ident, half, XG = shared.X, shared.ident, shared.half, shared.XG
        E, F, K = N_EXPERT, 64, 4
        I32, U32 = mybir.dt.int32, mybir.dt.uint32
        FW = w_gate.shape[1]
        NG = E // 4
        NOG = OVER_TILES // 4
        AHEAD = 2
        NS = NG + AHEAD
        NSH = (FW - E * F) // P
        NPAIR = NB * K

        WG = sb("d_WG", [P, 2, FW])
        WU = sb("d_WU", [P, 2, FW])
        WD = sb("d_WD", [P, FW // P, T])
        wr = sb("d_wr", [P, 2, E])
        bias = sb("d_bias", [P, E])
        iota = sb("d_iota", [P, E])
        iotai = sb("d_iotai", [P, E], I32)
        base_a = sb("d_base_a", [P, E])
        base_ba = sb("d_base_ba", [P, E])
        steps = sb("d_steps", [P, 7])
        tiles_row = sb("d_tiles_row", [1, OVER_TILES])
        tril = sb("d_tril", [P, P], BF16)
        ones = sb("d_ones", [P, P], BF16)
        zero_row = sb("d_zero_row", [P, E])
        stats = shared.stats
        mv = sb("d_mv", [P, NB, 2])
        vare = sb("d_vare", [P, NB])
        rstd = sb("d_rstd", [P, NB])
        XN = sb("d_XN", [P, NB, T])
        XT = sb("d_XT", [P, 2, NB, P])
        lg = sb("d_lg", [P, NB, E])
        lb = sb("d_lb", [P, NB, E])
        top = sb("d_top", [P, NB, 8])
        topi = sb("d_topi", [P, NB, 8], U32)
        topf = sb("d_topf", [P, NB, 8])
        oh = sb("d_oh", [P, NB, K, E], BF16)
        mask = sb("d_mask", [P, NB, E], BF16)
        nmx = sb("d_nmx", [P, NB])
        cnt = sb("d_cnt", [P, E])
        cmp7 = sb("d_cmp7", [P, 7, E])
        over = sb("d_over", [P, E])
        pref = sb("d_pref", [P, E])
        expf = sb("d_expf", [P, E])
        dba = sb("d_dba", [P, E])
        slot = sb("d_slot", [P, NB, E])
        scr = shared.C[:, :, :].rearrange("p b (k e) -> p b k e", k=K)
        slotk = sb("d_slotk", [P, NPAIR])
        slots = sb("d_slots", [P, NPAIR], U32)
        wk = sb("d_wk", [P, NB, K])
        den = sb("d_den", [P, NB])
        rden = sb("d_rden", [P, NB])
        wt = sb("d_wt", [P, NB, K])
        eid = sb("d_eid", [1, OVER_TILES + 1])
        eidi = sb("d_eidi", [1, OVER_TILES + 1], I32)
        sgs = sb("d_sgs", [P, 2, 512])
        hs = sb("d_hs", [P, NSH, 512])
        xg = sb("d_xg", [P, 3, 4, T])
        xgT = sb("d_xgT", [P, 2, 2, 4, P])
        sg = sb("d_sg", [P, 2, 2 * P])
        h = sb("d_h", [P, 2, 2 * P])
        wgo = sb("d_wgo", [P, AHEAD, 2, 4, F])
        wuo = sb("d_wuo", [P, AHEAD, 2, 4, F])
        wdo = sb("d_wdo", [P, AHEAD, 2, T])
        ysb = XT[:, :, :, :].rearrange("p c (t u) n -> p c t (u n)", u=2)
        xgo = hs[:, 0:2, :].rearrange("p a (b t) -> p (a b) t", t=T)
        yso = hs[:, 2:4, :].rearrange("p a (b t) -> p (a b) t", t=T)
        YD = shared.YD

        PS = [stack.enter_context(nc.psum_tensor(f"d_ps{i}", [P, 512], F32)) for i in range(8)]
        PGATE, PUP, PY, PX = PS[0:2], PS[2:4], PS[4:6], PS[6:8]

        def sems(*names):
            return [sem("d_" + n) for n in names]

        s_w, s_wd, s_const, s_mv, s_rstd, s_xn = sems("w_in", "wd_in", "consts", "mv", "rstd", "xn")
        s_t, s_xt, s_r, s_mask, s_rank, s_slot = sems("xT_done", "xT_sb", "router", "mask", "rank", "slots")
        s_lgm, s_ex, s_wt, s_eid, s_sc = sems("lg_minus_max", "exp", "weights", "overflow_experts", "scattered")
        s_sgu, s_ssg, s_sh, s_sy, s_shx = sems("sh_gate_up", "sh_silu", "sh_hidden", "sh_down", "sh_added")
        s_xg = sems("xg_in0", "xg_in1", "xg_in2")
        s_xo, s_px, s_xea, s_xed, s_gu = sems("overflow_in", "xg_transposed", "xgT_act", "xgT_dve", "gate_up")
        s_sg, s_h, s_py, s_ya, s_yd = sems("silu", "hidden", "down", "y_act", "y_dve")
        s_yst = sems("y_stored0", "y_stored1")
        s_wo, = sems("overflow_weights_in")
        s_yso, = sems("y_overflow_stored")
        s_wsh, s_wgu = sems("shared_gu_in", "routed_gu_in")
        s_yg = sems("y_gathered0", "y_gathered1")
        s_x4, s_out, s_dv, s_pl = sems("x4", "out_stored", "dve_chain", "pool_chain")

        ROW0 = E * P
        wg_v = w_gate.rearrange("(c p) n -> p c n", p=P)
        wu_v = w_up.rearrange("(c p) n -> p c n", p=P)

        block = stack.enter_context(nc.Block())

        @block.sync
        def _(sp):
            sp.dma_start(wr[:, :, :], w_router.rearrange("(c p) n -> p c n", p=P)).then_inc(s_w, 16)
            sp.dma_start(bias[:, :], router_bias.partition_broadcast(P)).then_inc(s_w, 16)
            sp.dma_start(WD[:, E * F // P:, :], w_down[E * F:, :].rearrange("(c p) n -> p c n", p=P)).then_inc(s_w, 16)
            for q in range(4):
                n = E * F // P // 4
                sp.dma_start(WD[:, n * q:n * (q + 1), :], w_down[P * n * q:P * n * (q + 1), :].rearrange("(c p) n -> p c n", p=P)).then_inc(s_wd, 16)
            def load_weights(i, part, signal, results_left=None):
                for j in range(4):
                    e = sp.value_load(eidi[0:1, (bass.ds(i * 4 + j, 1) if results_left is not None else slice(i * 4 + j, i * 4 + j + 1))], min_val=0, max_val=E - 1)
                    sp.dma_start(wgo[:, part, :, j, :], wg_v[:, :, bass.ds(e * F, F)]).then_inc(signal, 16)
                    if j == 3 and results_left is not None:
                        sp.wait_ge(s_yso, results_left)
                    sp.dma_start(wuo[:, part, :, j, :], wu_v[:, :, bass.ds(e * F, F)]).then_inc(signal, 16)
                    sp.dma_start(wdo[64 * (j % 2):64 * (j % 2) + 64, part, j // 2, :], w_down[bass.ds(e * F, F), :]).then_inc(signal, 16)

            sp.wait_ge(s_eid, 1)
            for i in range(AHEAD):
                load_weights(i, i, s_wo)
            sp.wait_ge(s_sc, 16 * NPAIR)
            for g in range(NS):
                if g >= 3:
                    sp.wait_ge(s_px, g - 2)
                sp.dma_start(xg[:, g % 3, :, :], XG[512 * g:512 * (g + 1), :].rearrange("(t p) d -> p t d", p=P)).then_inc(s_xg[g % 3], 16)
            n_over = sp.value_load(eidi[0:1, OVER_TILES:OVER_TILES + 1], min_val=0, max_val=OVER_TILES - 1)
            with sp.Fori(AHEAD, NOG) as i:
                with sp.If(i * 4 < n_over):
                    sp.wait_ge(s_py, i + NG)
                    sp.dma_start(xgo[:, :, :], XG[bass.ds(ROW0 + i * 512, 512), :].rearrange("(t p) d -> p t d", p=P)).then_inc(s_xo, 16)
                    load_weights(i, 0, s_xo, i * 16)
            for b in range(NB):
                sp.wait_ge(s_x4, b + 1)
                sp.dma_start(out[b], X[:, b, :]).then_inc(s_out, 16)
            sp.wait_ge(s_out, 16 * NB)

        @block.gpsimd
        def _(pool):
            n = [0]

            def link(ins):
                n[0] += 1
                ins.then_inc(s_pl, 1)
                pool.wait_ge(s_pl, n[0])

            pool.wait_ge(s_mv, 1)
            pool.tensor_tensor(rstd[:, :], vare[:, :], half[:, 0:NB], ALU.pow).then_inc(s_rstd, 1)
            link(pool.iota(iotai[:, :], pattern=[[1, E]], base=0, channel_multiplier=0))
            link(pool.tensor_copy(iota[:, :], iotai[:, :]))
            link(pool.tensor_scalar(base_a[:, :], iota[:, :], float(P), 0.0, ALU.mult, ALU.add))
            link(pool.tensor_scalar(base_ba[:, :], iota[:, :], -float(P), float(P * (E - 1)), ALU.mult, ALU.add))
            link(pool.tensor_copy(tiles_row[:, :], iota[0:1, 0:OVER_TILES]))
            link(pool.tensor_scalar(steps[:, :], iota[:, 1:8], float(P), 0.0, ALU.mult, ALU.add))
            link(pool.memset(zero_row[:, :], 0.0))
            link(pool.memset(ones[:, :], 1.0))
            pool.affine_select(out=tril[:, :], in_=ones[:, :], compare_op=ALU.is_gt, fill=0.0, base=0,
                               pattern=[[1, P]], channel_multiplier=-1).then_inc(s_const, 1)
            pool.wait_ge(shared.s_zeroed, 16 * shared.n_zero_dmas)
            pool.wait_ge(s_xn, NB)
            for i in range(NPAIR):
                if i % (NPAIR // 2) == 0:
                    pool.wait_ge(s_slot, i // (NPAIR // 2) + 1)
                pool.indirect_dma_start(out=XG[:, :], out_offset=bass.IndirectOffsetOnAxis(ap=slots[:, i:i + 1], axis=0),
                                        in_=XN[:, i // K, :], in_offset=None).then_inc(s_sc, 16)
            for g in range(NS):
                pool.wait_ge(s_ya, g + 1)
                pool.wait_ge(s_yd, g + 1)
                pool.dma_start(YD[512 * g:512 * (g + 1), :].rearrange("(t p) d -> p t d", p=P), ysb[:, g % 2, :, :]).then_inc(s_yst[g % 2] if g < NG else s_yso, 16)
            pool.wait_ge(s_eid, 1)
            n_over = pool.value_load(eidi[0:1, OVER_TILES:OVER_TILES + 1], min_val=0, max_val=OVER_TILES - 1)
            with pool.Fori(AHEAD, NOG) as i:
                with pool.If(i * 4 < n_over):
                    pool.wait_ge(s_ya, i + (NG + 1))
                    pool.wait_ge(s_yd, i + (NG + 1))
                    pool.dma_start(YD[bass.ds(ROW0 + i * 512, 512), :].rearrange("(t p) d -> p t d", p=P), yso[:, :, :]).then_inc(s_yso, 16)
                    pool.wait_ge(s_yso, i * 16 + 16)
            pool.wait_ge(s_yst[0], 16 * (NG // 2))
            pool.wait_ge(s_yst[1], 16 * (NG // 2))
            pool.wait_ge(s_yso, 16 * AHEAD)
            for i in range(NPAIR):
                b, k = i // K, i % K
                if k == 0 and b >= 2:
                    pool.wait_ge(s_x4, b - 1)
                if i == 0:
                    pool.wait_ge(s_px, NS)
                pool.indirect_dma_start(out=xg[:, b % 2, k, :], out_offset=None, in_=YD[:, :],
                                        in_offset=bass.IndirectOffsetOnAxis(ap=slots[:, i:i + 1], axis=0)).then_inc(s_yg[b % 2], 16)

        @block.scalar
        def _(act):
            act.dma_start(WG[:, :, E * F:], wg_v[:, :, E * F:]).then_inc(s_wsh, 16)
            act.dma_start(WU[:, :, E * F:], wu_v[:, :, E * F:]).then_inc(s_wsh, 16)
            for q in range(4):
                cols = slice(E * F // 4 * q, E * F // 4 * (q + 1))
                act.dma_start(WG[:, :, cols], wg_v[:, :, cols]).then_inc(s_wgu, 16)
                act.dma_start(WU[:, :, cols], wu_v[:, :, cols]).then_inc(s_wgu, 16)
            for b in range(NB):
                act.wait_ge(s_t, b + 1)
                nc.scalar.copy(XT[:, :, b, :], (PX[0] if b % 2 == 0 else PY[1])[:, 0:T].rearrange("p (c t) -> p c t", c=2)).then_inc(s_xt, 1)
            act.wait_ge(s_lgm, 1)
            nc.scalar.activation(lb[:, :, :], lb[:, :, :], ACT.Exp).then_inc(s_ex, 1)
            for n in range(2 * NSH):
                act.wait_ge(s_sgu, n + 1)
                if n >= 2:
                    act.wait_ge(s_sh, n - 1)
                nc.scalar.activation(sgs[:, n % 2, :], PGATE[n % 2][:, :], ACT.Silu).then_inc(s_ssg, 1)

            for g in range(NS + 1):
                if g < NS:
                    act.wait_ge(s_px, g + 1)
                    if g >= 2:
                        act.wait_ge(s_gu, g - 1)
                    nc.scalar.copy(xgT[:, g % 2, 0, :, :], PX[0][:, :].rearrange("p (t n) -> p t n", t=4)).then_inc(s_xea, 1)
                if g:
                    m = g - 1
                    act.wait_ge(s_py, m + 1)
                    if m >= 2:
                        act.wait_ge(s_yst[m % 2], 16 * (m // 2))
                    nc.scalar.copy(ysb[:, m % 2, 0:4:2, :], PY[0][:, :].rearrange("p (t n) -> p t n", t=2)).then_inc(s_ya, 1)
                if g < NS:
                    act.wait_ge(s_gu, g + 1)
                    if g >= 2:
                        act.wait_ge(s_h, g - 1)
                    nc.scalar.activation(sg[:, g % 2, :], PGATE[g % 2][:, 0:2 * P], ACT.Silu).then_inc(s_sg, 1)
            act.wait_ge(s_eid, 1)
            n_over = act.value_load(eidi[0:1, OVER_TILES:OVER_TILES + 1], min_val=0, max_val=OVER_TILES - 1)
            with act.Fori(AHEAD, NOG) as i:
                with act.If(i * 4 < n_over):
                    act.wait_ge(s_px, i + (NG + 1))
                    nc.scalar.copy(xgT[:, 0, 0, :, :], PX[0][:, :].rearrange("p (t n) -> p t n", t=4)).then_inc(s_xea, 1)
                    act.wait_ge(s_gu, i + (NG + 1))
                    nc.scalar.activation(sg[:, 0, :], PGATE[0][:, 0:2 * P], ACT.Silu).then_inc(s_sg, 1)
                    act.wait_ge(s_py, i + (NG + 1))
                    nc.scalar.copy(yso[:, 0:4:2, :], PY[0][:, :].rearrange("p (t n) -> p t n", t=2)).then_inc(s_ya, 1)

        @block.vector
        def _(dve):
            n = [0]

            def link(ins):
                n[0] += 1
                ins.then_inc(s_dv, 1)
                dve.wait_ge(s_dv, n[0])

            for b in range(NB):
                last = nc.vector.bn_aggr(mv[:, b, :], stats[:, b, :])
            link(last)
            nc.vector.tensor_scalar(vare[:, :], mv[:, :, 1], EPS, None, ALU.add).then_inc(s_mv, 1)
            dve.wait_ge(s_rstd, 1)
            for b in range(NB):
                nc.vector.tensor_scalar(XN[:, b, :], X[:, b, :], mv[:, b, 0:1], rstd[:, b:b + 1], ALU.subtract, ALU.mult).then_inc(s_xn, 1)
            def shared_hidden(n):
                dve.wait_ge(s_ssg, n + 1)
                if n == NSH:
                    dve.wait_ge(s_sy, 2)
                nc.vector.tensor_tensor(hs[:, n % NSH, :], PUP[n % 2][:, :], sgs[:, n % 2, :], ALU.mult).then_inc(s_sh, 1)

            def shared_add(m):
                dve.wait_ge(s_sy, m + 1)
                nc.vector.tensor_tensor(X[:, 2 * m:2 * m + 2, :], PY[m % 2][:, :].rearrange("p (b t) -> p b t", b=2), X[:, 2 * m:2 * m + 2, :], ALU.add).then_inc(s_shx, 1)

            dve.wait_ge(s_w, 48)
            dve.wait_ge(s_r, 1)
            link(nc.vector.tensor_copy(lg[:, :, :], PX[1][:, :].rearrange("p (b e) -> p b e", b=NB)))
            link(nc.vector.tensor_tensor(lb[:, :, :], lg[:, :, :], bias[:, :].unsqueeze(1).broadcast_to([P, NB, E]), ALU.add))
            for b in range(NB):
                last = nc.vector.max(top[:, b, :], lb[:, b, :])
            link(last)
            for b in range(NB):
                last = nc.vector.max_index(topi[:, b, :], top[:, b, :], lb[:, b, :])
            link(last)
            link(nc.vector.tensor_copy(topf[:, :, :], topi[:, :, :]))
            dve.wait_ge(s_const, 1)
            link(nc.vector.tensor_tensor(oh[:, :, :, :], iota[:, :].unsqueeze(1).unsqueeze(1).broadcast_to([P, NB, K, E]),
                                         topf[:, :, 0:K].unsqueeze(3).broadcast_to([P, NB, K, E]), ALU.is_equal))
            with nc.allow_low_precision(reason="counts of 0 and 1"):
                nc.vector.reduce_sum(mask[:, :, :], oh[:, :, :, :].rearrange("p b k e -> p b e k"), X_AXIS).then_inc(s_mask, 1)
            link(nc.vector.tensor_reduce(nmx[:, :], lg[:, :, :], X_AXIS, ALU.max, negate=True))
            nc.vector.tensor_tensor(lb[:, :, :], lg[:, :, :], nmx[:, :].unsqueeze(2).broadcast_to([P, NB, E]), ALU.add).then_inc(s_lgm, 1)
            dve.wait_ge(s_rank, 1)
            link(nc.vector.tensor_copy(cnt[:, :], PX[0][:, 0:E]))
            link(nc.vector.tensor_tensor(cmp7[:, :, :], cnt[:, :].unsqueeze(1).broadcast_to([P, 7, E]), steps[:, :].unsqueeze(2).broadcast_to([P, 7, E]), ALU.is_gt))
            link(nc.vector.reduce_sum(over[:, :], cmp7[:, :, :].rearrange("p j e -> p e j"), X_AXIS))
            link(nc.vector.tensor_tensor_scan(pref[:, :], over[:, :], zero_row[:, :], 0.0, ALU.add, ALU.add))
            link(nc.vector.tensor_tensor(expf[:, :], pref[:, :], over[:, :], ALU.subtract))
            link(nc.vector.scalar_tensor_tensor(dba[:, :], expf[:, :], float(P), base_ba[:, :], ALU.mult, ALU.add))
            ge = scr[:, 0:2, :, :].rearrange("p a b e -> p (a b) e")
            t1 = scr[:, 2:4, :, :].rearrange("p a b e -> p (a b) e")
            t2 = scr[:, 4:6, :, :].rearrange("p a b e -> p (a b) e")
            rank = PX[1][:, :].rearrange("p (b e) -> p b e", b=NB)
            nc.vector.tensor_tensor(t2, rank, base_a[:, :].unsqueeze(1).broadcast_to([P, NB, E]), ALU.add)
            link(nc.vector.tensor_scalar(ge, rank, float(P), None, ALU.is_ge))
            link(nc.vector.tensor_tensor(t1, ge, dba[:, :].unsqueeze(1).broadcast_to([P, NB, E]), ALU.mult))
            link(nc.vector.tensor_tensor(slot[:, :, :], t1, t2, ALU.add))
            shared_hidden(0)
            shared_hidden(1)
            for q in range(2):
                bs = slice(4 * q, 4 * q + 4)
                link(nc.vector.tensor_tensor(scr[:, bs, :, :], oh[:, bs, :, :], slot[:, bs, :].unsqueeze(2).broadcast_to([P, 4, K, E]), ALU.mult))
                link(nc.vector.reduce_sum(slotk[:, 16 * q:16 * q + 16], scr[:, bs, :, :].rearrange("p b k e -> p (b k) e"), X_AXIS))
                nc.vector.tensor_copy(slots[:, 16 * q:16 * q + 16], slotk[:, 16 * q:16 * q + 16]).then_inc(s_slot, 1)
            shared_hidden(2)
            ecmp = scr[0:1, :, :, :].rearrange("p b k e -> p (b k) e")
            dve.wait_ge(s_slot, 2)
            link(nc.vector.tensor_tensor(ecmp, pref[0:1, :].unsqueeze(1).broadcast_to([1, OVER_TILES, E]), tiles_row[:, :].unsqueeze(2).broadcast_to([1, OVER_TILES, E]), ALU.is_le))
            link(nc.vector.reduce_sum(eid[:, 0:OVER_TILES], ecmp, X_AXIS))
            link(nc.vector.tensor_scalar(eid[:, 0:OVER_TILES], eid[:, 0:OVER_TILES], float(E - 1), None, ALU.min))
            link(nc.vector.tensor_copy(eid[:, OVER_TILES:OVER_TILES + 1], pref[0:1, E - 1:E]))
            nc.vector.tensor_copy(eidi[:, :], eid[:, :]).then_inc(s_eid, 1)

            shared_hidden(3)
            dve.wait_ge(s_ex, 1)
            dve.wait_ge(s_eid, 1)
            link(nc.vector.tensor_tensor(scr[:, :, :, :], oh[:, :, :, :], lb[:, :, :].unsqueeze(2).broadcast_to([P, NB, K, E]), ALU.mult))
            link(nc.vector.reduce_sum(wk[:, :, :].rearrange("p b k -> p (b k)"), scr[:, :, :, :].rearrange("p b k e -> p (b k) e"), X_AXIS))
            link(nc.vector.reduce_sum(den[:, :], wk[:, :, :], X_AXIS))
            link(nc.vector.reciprocal(rden[:, :], den[:, :]))
            nc.vector.tensor_tensor(wt[:, :, :], wk[:, :, :], rden[:, :].unsqueeze(2).broadcast_to([P, NB, K]), ALU.mult).then_inc(s_wt, 1)
            shared_add(0)
            shared_add(1)
            for n_ in range(NSH, 2 * NSH):
                shared_hidden(n_)
            shared_add(2)
            shared_add(3)

            for g in range(NS + 1):
                if g < NS:
                    dve.wait_ge(s_px, g + 1)
                    if g >= 2:
                        dve.wait_ge(s_gu, g - 1)
                    nc.vector.tensor_copy(xgT[:, g % 2, 1, :, :], PX[1][:, :].rearrange("p (t n) -> p t n", t=4)).then_inc(s_xed, 1)
                if g:
                    m = g - 1
                    dve.wait_ge(s_py, m + 1)
                    if m >= 2:
                        dve.wait_ge(s_yst[m % 2], 16 * (m // 2))
                    nc.vector.tensor_copy(ysb[:, m % 2, 1:4:2, :], PY[1][:, :].rearrange("p (t n) -> p t n", t=2)).then_inc(s_yd, 1)
                if g < NS:
                    dve.wait_ge(s_sg, g + 1)
                    if g >= 2:
                        dve.wait_ge(s_py, g - 1)
                    nc.vector.tensor_tensor(h[:, g % 2, :], PUP[g % 2][:, 0:2 * P], sg[:, g % 2, :], ALU.mult).then_inc(s_h, 1)
            n_over = dve.value_load(eidi[0:1, OVER_TILES:OVER_TILES + 1], min_val=0, max_val=OVER_TILES - 1)
            with dve.Fori(AHEAD, NOG) as i:
                with dve.If(i * 4 < n_over):
                    dve.wait_ge(s_px, i + (NG + 1))
                    nc.vector.tensor_copy(xgT[:, 0, 1, :, :], PX[1][:, :].rearrange("p (t n) -> p t n", t=4)).then_inc(s_xed, 1)
                    dve.wait_ge(s_sg, i + (NG + 1))
                    nc.vector.tensor_tensor(h[:, 0, :], PUP[0][:, 0:2 * P], sg[:, 0, :], ALU.mult).then_inc(s_h, 1)
                    dve.wait_ge(s_py, i + (NG + 1))
                    nc.vector.tensor_copy(yso[:, 1:4:2, :], PY[1][:, :].rearrange("p (t n) -> p t n", t=2)).then_inc(s_yd, 1)
            for b in range(NB):
                dve.wait_ge(s_yg[b % 2], 16 * K * (b // 2 + 1))
                for k in range(K):
                    ins = nc.vector.scalar_tensor_tensor(X[:, b, :], xg[:, b % 2, k, :], wt[:, b, k:k + 1], X[:, b, :], ALU.mult, ALU.add)
                    if k < K - 1:
                        link(ins)
                ins.then_inc(s_x4, 1)

        @block.tensor
        def _(pe):
            for b in range(NB):
                pe.wait_ge(s_xn, b + 1)
                if b >= 2:
                    pe.wait_ge(s_xt, b - 1)
                bank = PX[0] if b % 2 == 0 else PY[1]
                for c in range(2):
                    last = nc.tensor.transpose(bank[:, c * P:(c + 1) * P], XN[:, b, c * P:(c + 1) * P], ident[:, :])
                last.then_inc(s_t, 1)
                if b == 0:
                    pe.wait_ge(s_w, 48)
                if b:
                    pe.wait_ge(s_xt, b)
                    for c in range(2):
                        nc.tensor.matmul(PX[1][:, E * (b - 1):E * b], XT[:, c, b - 1, :], wr[:, c, :], start=(c == 0), stop=(c == 1))
            pe.wait_ge(s_xt, NB)
            for c in range(2):
                last = nc.tensor.matmul(PX[1][:, E * (NB - 1):E * NB], XT[:, c, NB - 1, :], wr[:, c, :], start=(c == 0), stop=(c == 1))
            last.then_inc(s_r, 1)

            def shared_gate_up(n):
                tg, fc = n // NSH, n % NSH
                if n >= 2:
                    pe.wait_ge(s_sh, n - 1)
                for bank, w in ((PGATE, WG), (PUP, WU)):
                    for c in range(2):
                        last = nc.tensor.matmul(bank[n % 2][:, :], w[:, c, E * F + P * fc:E * F + P * (fc + 1)],
                                                XT[:, c, 4 * tg:4 * tg + 4, :], start=(c == 0), stop=(c == 1))
                last.then_inc(s_sgu, 1)

            def shared_down(m):
                pe.wait_ge(s_sh, NSH * (m // 2 + 1))
                if m >= 2:
                    pe.wait_ge(s_shx, m - 1)
                for j in range(2):
                    b = 2 * m + j
                    for fc in range(NSH):
                        last = nc.tensor.matmul(PY[m % 2][:, j * T:(j + 1) * T], hs[:, fc, (b % 4) * P:(b % 4 + 1) * P], WD[:, E * F // P + fc, :],
                                                start=(fc == 0), stop=(fc == NSH - 1))
                last.then_inc(s_sy, 1)

            pe.wait_ge(s_wsh, 32)
            shared_gate_up(0)
            shared_gate_up(1)
            pe.wait_ge(s_mask, 1)
            nc.tensor.matmul(PX[1][:, :], tril[:, :], mask[:, :, :], start=True, stop=False)
            for b in range(NB - 1):
                nc.tensor.matmul(PX[1][:, E * (b + 1):], ones[:, :], mask[:, b, :].unsqueeze(1).broadcast_to([P, NB - 1 - b, E]), start=False, stop=(b == NB - 2))
            for b in range(NB):
                last = nc.tensor.matmul(PX[0][:, 0:E], ones[:, :], mask[:, b, :], start=(b == 0), stop=(b == NB - 1))
            last.then_inc(s_rank, 1)
            for n in range(2, NSH):
                shared_gate_up(n)
            shared_down(0)
            shared_down(1)
            for n in range(NSH, 2 * NSH):
                shared_gate_up(n)
            shared_down(2)
            shared_down(3)

            def transposes(src):
                for c in range(2):
                    for t in range(4):
                        last = nc.tensor.transpose(PX[c][:, t * P:(t + 1) * P], src[:, t, c * P:(c + 1) * P], ident[:, :])
                last.then_inc(s_px, 1)

            def gate_up(slot, wg, wu):
                for bank, w in ((PGATE[slot], wg), (PUP[slot], wu)):
                    for j in range(2):
                        for c in range(2):
                            for s in range(2):
                                last = nc.tensor.matmul(bank[64 * s:64 * s + 64, j * P:(j + 1) * P], w(c, 2 * j + s), xgT[:, slot, c, 2 * j + s, :],
                                                        start=(c == 0), stop=(c == 1))
                last.then_inc(s_gu, 1)

            def down(slot, wd):
                for j in range(2):
                    for s in range(2):
                        last = nc.tensor.matmul(PY[s][:, j * T:(j + 1) * T], h[64 * s:64 * s + 64, slot, j * P:(j + 1) * P], wd(j, s), start=True, stop=True)
                last.then_inc(s_py, 1)

            def first_half(g):
                pe.wait_ge(s_xg[g % 3], 16 * (g // 3 + 1))
                if g:
                    pe.wait_ge(s_xea, g)
                    pe.wait_ge(s_xed, g)
                transposes(xg[:, g % 3, :, :])

            first_half(0)
            pe.wait_ge(s_wgu, 16 * 8)
            pe.wait_ge(s_shx, 4)
            pe.wait_ge(s_sh, 2 * NSH)
            for g in range(NS):
                if g == NG:
                    pe.wait_ge(s_wo, 16 * 12 * AHEAD)
                pe.wait_ge(s_xea, g + 1)
                pe.wait_ge(s_xed, g + 1)
                if g >= 2:
                    pe.wait_ge(s_h, g - 1)
                if g < NG:
                    gate_up(g % 2, lambda c, t: WG[:, c, F * (4 * g + t):F * (4 * g + t + 1)], lambda c, t: WU[:, c, F * (4 * g + t):F * (4 * g + t + 1)])
                else:
                    gate_up(g % 2, lambda c, t: wgo[:, g - NG, c, t, :], lambda c, t: wuo[:, g - NG, c, t, :])
                if g + 1 < NS:
                    first_half(g + 1)
                pe.wait_ge(s_h, g + 1)
                if g == 0:
                    pe.wait_ge(s_wd, 64)
                else:
                    pe.wait_ge(s_ya, g)
                    pe.wait_ge(s_yd, g)
                down(g % 2, lambda j, s: WD[64 * s:64 * s + 64, 2 * g + j, :] if g < NG else wdo[64 * s:64 * s + 64, g - NG, j, :])
            pe.wait_ge(s_eid, 1)
            n_over = pe.value_load(eidi[0:1, OVER_TILES:OVER_TILES + 1], min_val=0, max_val=OVER_TILES - 1)
            with pe.Fori(AHEAD, NOG) as i:
                with pe.If(i * 4 < n_over):
                    pe.wait_ge(s_xo, i * (13 * 16) - (AHEAD - 1) * 13 * 16)
                    pe.wait_ge(s_xea, i + NG)
                    pe.wait_ge(s_xed, i + NG)
                    transposes(xgo)
                    pe.wait_ge(s_xea, i + (NG + 1))
                    pe.wait_ge(s_xed, i + (NG + 1))
                    pe.wait_ge(s_h, i + NG)
                    gate_up(0, lambda c, t: wgo[:, 0, c, t, :], lambda c, t: wuo[:, 0, c, t, :])
                    pe.wait_ge(s_h, i + (NG + 1))
                    pe.wait_ge(s_ya, i + NG)
                    pe.wait_ge(s_yd, i + NG)
                    down(0, lambda j, s: wdo[64 * s:64 * s + 64, 0, j, :])


def build(nc, x, ctx_in, theta_wT, phi_wT, g_wT, out_wT2, col_consts, gamma2, beta2,
          conv_cols, w_qg, w_kv, rw, rot, w_out, gamma,
          w_router, router_bias, w_gate, w_up, w_down, out):
    stack = ExitStack()
    with stack:
        shared = Shared()
        shared.sem = lambda name: stack.enter_context(nc.semaphore(name))
        shared.X = stack.enter_context(nc.sbuf_tensor("X", [P, NB, T], F32))
        shared.C = stack.enter_context(nc.sbuf_tensor("C", [P, NB, T], F32))
        shared.ident = stack.enter_context(nc.sbuf_tensor("ident", [P, P], F32))
        shared.stats = stack.enter_context(nc.sbuf_tensor("stats", [P, NB, 6], F32))
        shared.half = stack.enter_context(nc.sbuf_tensor("half", [P, 64], F32))
        shared.YD = nc.dram_tensor("expert_rows_out", (N_TILES * P, T), F32, kind="Internal").ap()
        shared.XG = nc.dram_tensor("expert_rows_in", (N_TILES * P, T), F32, kind="Internal").ap()
        shared.kd = nc.dram_tensor("k_parts", (16, 3, NB, 8, T), BF16, kind="Internal").ap()
        shared.s_zeroed = shared.sem("expert_rows_zeroed")
        shared.s_kd, shared.s_kin = shared.sem("k_stored"), shared.sem("k_loaded")
        with nc.sbuf_tensor("KS", [P, NB, 8, T], BF16) as shared.KS:
            with nc.sbuf_tensor("ksp", [P, 3, NB, T], BF16) as shared.ksp:
                stage_a(nc, shared, x, ctx_in, theta_wT, phi_wT, g_wT, out_wT2, col_consts, gamma2, beta2)
                stage_b(nc, shared, conv_cols, w_qg, w_kv, rw, rot, w_out)
            stage_c(nc, shared, gamma)
        stage_d(nc, shared, w_router, router_bias, w_gate, w_up, w_down, out)


def kernel(**inputs):
    import concourse.bacc as _bacc
    from concourse import mybir as _mybir
    from concourse.bass_utils import run_bass_kernel_spmd as _run

    a = {k: np.asarray(v) for k, v in inputs.items()}
    two = lambda m: np.ascontiguousarray(np.concatenate([m, m], axis=0))
    def own_half(w):
        z = np.zeros_like(w)
        return np.stack([np.concatenate([w, z]), np.concatenate([z, w])], axis=1)

    host = {
        "x": a["x"], "ctx_in": a["ctx_2048"],
        "theta_wT": a["L0_xattn_theta_w"].T, "phi_wT": a["L0_xattn_phi_w"].T, "g_wT": a["L0_xattn_g_w"].T,
        "out_wT2": own_half(a["L0_xattn_out_w"].T),
        "col_consts": np.stack([two(a["L0_xattn_theta_b"]), two(a["L0_xattn_phi_b"]), two(a["L0_xattn_g_b"]), a["L0_xattn_out_b"]], axis=1),
        "gamma2": two(a["L0_xattn_ln_gamma"]), "beta2": two(a["L0_xattn_ln_beta"]),
    }
    def side_by_side(routed, common):
        return np.concatenate([w.transpose(1, 0, 2).reshape(T, -1) for w in (routed, common)], axis=1)

    inv_freq = (1.0 / np.float32(10000.0) ** (np.arange(0, 8, 2, dtype=np.float32) / np.float32(8))).astype(np.float32)
    ang = np.arange(NB, dtype=np.float32)[:, None] * inv_freq[None, :]
    host |= {
        "conv_cols": a["L0_ffn_conv_w"].reshape(2, P, 2).transpose(1, 0, 2),
        "w_qg": np.concatenate([a["L0_ffn_Wq"], a["L0_ffn_Wg"]], axis=1),
        "w_kv": np.concatenate([a["L0_ffn_Wk"], a["L0_ffn_Wv"]], axis=1),
        "rw": a["L0_ffn_router_w"],
        "rot": np.stack([np.cos(ang), np.sin(ang), -np.sin(ang)]).astype(np.float32),
        "w_out": a["L0_ffn_Wout"],
        "c_gamma": a["L1_xattn_gamma"].reshape(1),
        "w_router": a["L1_ffn_router_w"], "router_bias": a["L1_ffn_router_bias"],
        "w_gate": side_by_side(a["L1_ffn_wg"], a["L1_ffn_swg"]), "w_up": side_by_side(a["L1_ffn_wu"], a["L1_ffn_swu"]),
        "w_down": np.concatenate([a["L1_ffn_wd"].reshape(-1, T), a["L1_ffn_swd"].reshape(-1, T)], axis=0),
    }
    nc = _bacc.Bacc("TRN2", target_bir_lowering=False, num_devices=1)
    arrays, args = {}, []
    for name, v in host.items():
        v = np.ascontiguousarray(v)
        arrays[name + "_dram"] = v
        args.append(nc.dram_tensor(name + "_dram", v.shape, _mybir.dt.from_np(v.dtype), kind="ExternalInput").ap())
    args.append(nc.dram_tensor("out_dram", (NB, P, T), F32, kind="ExternalOutput").ap())
    build(nc, *args)
    r = _run(nc, [arrays], core_ids=[0])
    return r.results[0]["out_dram"]
```
